# Optimizing a Trainium2 kernel written in Bass

```python
import numpy as np
import jax
import jax.numpy as jnp

def _softmax(x, axis=-1):
    return jax.nn.softmax(x, axis=axis)

def _gelu(x):
    return jax.nn.gelu(x, approximate=True)

def _silu(x):
    return jax.nn.silu(x)

def _sigmoid(x):
    return jax.nn.sigmoid(x)

def _layernorm(x, axis=-1, eps=1e-05):
    m = jnp.mean(x, axis=axis, keepdims=True)
    v = jnp.var(x, axis=axis, keepdims=True)
    return (x - m) / jnp.sqrt(v + eps)

def _scatter_add(tgt, idx, src, axis=0):
    return tgt.at[idx].add(src)

def _segment_sum(src, seg, n):
    return jax.ops.segment_sum(src, seg, n)
kernel_name = 'mk_prb_d2_jaxref_r8_ce4f10'

def setup_inputs(seed: int=0):
    np.random.seed(seed)
    _w = jnp.asarray

    def _L0_attn_setup():
        import jax, jax.numpy as jnp
        import numpy as np
        B, S, HID = (4, 128, 128)
        H = 8
        HD = HID // H
        NQ = 8
        RATIO = 0.5
        FF = 4 * HID
        EPS_COS = 1e-08
        LN_EPS = 1e-05

        def _layernorm(x, g, b):
            m = jnp.mean(x, axis=-1, keepdims=True)
            v = jnp.var(x, axis=-1, keepdims=True)
            return (x - m) * jax.lax.rsqrt(v + LN_EPS) * g + b
        key = jax.random.key(seed)
        ks = jax.random.split(key, 24)
        sc = 0.02
        inp = {'x': jax.random.normal(ks[0], (B, S, HID), jnp.float32), 'Wq': jax.random.normal(ks[1], (H, HID, HD)) * sc, 'bq': jnp.zeros((H, HD)), 'Wk': jax.random.normal(ks[2], (H, HID, HD)) * sc, 'bk': jnp.zeros((H, HD)), 'Wv': jax.random.normal(ks[3], (H, HID, HD)) * sc, 'bv': jnp.zeros((H, HD)), 'Wc2q': jax.random.normal(ks[4], (H, HD, NQ)) * sc, 'bc2q': jnp.zeros((H, NQ)), 'Wo': jax.random.normal(ks[5], (HID, HID)) * sc, 'bo': jnp.zeros((HID,)), 'g1': jnp.ones((HID,)), 'beta1': jnp.zeros((HID,)), 'g2': jnp.ones((HID,)), 'beta2': jnp.zeros((HID,)), 'W1': jax.random.normal(ks[6], (HID, FF)) * sc, 'b1': jnp.zeros((FF,)), 'Wm': jax.random.normal(ks[7], (FF, NQ)) * sc, 'bm': jnp.zeros((NQ,)), 'Wqo': jax.random.normal(ks[8], (NQ, FF)) * sc, 'bqo': jnp.zeros((FF,)), 'W2': jax.random.normal(ks[9], (FF, HID)) * sc, 'b2': jnp.zeros((HID,))}
        return inp
    _L0_attn_in = _L0_attn_setup()

    def _L0_ffn_setup():
        import jax, jax.numpy as jnp
        import numpy as np
        E = 16
        H = 128
        F = 256
        TOP_K = 1
        B, S = (2, 128)
        key = jax.random.key(seed)
        ks = jax.random.split(key, 7)
        s = 0.02
        return {'hidden_states': jax.random.normal(ks[0], (B, S, H), jnp.float32), 'w_router': jax.random.normal(ks[1], (E, H), jnp.float32) * s, 'gate_up_proj': jax.random.normal(ks[2], (E, H, 2 * F), jnp.float32) * s, 'down_proj': jax.random.normal(ks[3], (E, F, H), jnp.float32) * s, 'w_gate': jax.random.normal(ks[4], (F, H), jnp.float32) * s, 'w_up': jax.random.normal(ks[5], (F, H), jnp.float32) * s, 'w_down': jax.random.normal(ks[6], (H, F), jnp.float32) * s}
    _L0_ffn_in = _L0_ffn_setup()

    def _L1_attn_setup():
        import jax, jax.numpy as jnp
        import numpy as np
        import math
        B, T, C, H = (4, 256, 128, 16)
        EPS = 1e-10

        def layernorm(x):
            mean = jnp.mean(x, axis=-1, keepdims=True)
            xmu = x - mean
            var = jnp.mean(xmu * xmu, axis=-1, keepdims=True)
            return xmu / jnp.sqrt(var + EPS)

        def new_gelu(x):
            c = math.sqrt(2.0 / math.pi)
            return 0.5 * x * (1.0 + jnp.tanh(c * (x + 0.044715 * x * x * x)))

        def attention(x, w_attn, b_attn, w_proj, b_proj):
            b, t, cdim = x.shape
            d = cdim // H
            ca = x @ w_attn.T + b_attn
            q, k, v = jnp.split(ca, 3, axis=2)
            q = q.reshape(b, t, H, d)
            k = k.reshape(b, t, H, d)
            v = v.reshape(b, t, H, d)
            att = jnp.einsum('bthd,bshd->bhts', q, k) * (1.0 / math.sqrt(d))
            mask = jnp.tril(jnp.ones((t, t), dtype=bool))
            att = jnp.where(mask, att, -jnp.inf)
            att = jax.nn.softmax(att, axis=-1)
            y = jnp.einsum('bhts,bshd->bthd', att, v).reshape(b, t, cdim)
            return y @ w_proj.T + b_proj
        key = jax.random.key(seed)
        ks = jax.random.split(key, 9)
        s = 0.02
        return {'x': jax.random.normal(ks[0], (B, T, C), jnp.float32), 'w_attn': jax.random.normal(ks[1], (3 * C, C), jnp.float32) * s, 'b_attn': jax.random.normal(ks[2], (3 * C,), jnp.float32) * s, 'w_proj': jax.random.normal(ks[3], (C, C), jnp.float32) * s, 'b_proj': jax.random.normal(ks[4], (C,), jnp.float32) * s, 'w_fc': jax.random.normal(ks[5], (4 * C, C), jnp.float32) * s, 'b_fc': jax.random.normal(ks[6], (4 * C,), jnp.float32) * s, 'w_mlp_proj': jax.random.normal(ks[7], (C, 4 * C), jnp.float32) * s, 'b_mlp_proj': jax.random.normal(ks[8], (C,), jnp.float32) * s}
    _L1_attn_in = _L1_attn_setup()

    def _L1_ffn_setup():
        import jax, jax.numpy as jnp
        import numpy as np
        D_MODEL = 128
        D_FF = 512
        NUM_EXPERTS = 8
        TOP_K = 2
        B, S = (4, 512)
        key = jax.random.key(seed)
        ks = jax.random.split(key, 7)
        s_dm = 1.0 / np.sqrt(D_MODEL)
        s_ff = 1.0 / np.sqrt(D_FF)
        return {'x': jax.random.normal(ks[0], (B, S, D_MODEL), jnp.float32), 'router_w': jax.random.normal(ks[1], (D_MODEL, NUM_EXPERTS), jnp.float32) * s_dm, 'router_b': jnp.zeros((NUM_EXPERTS,), jnp.float32), 'w1': jax.random.normal(ks[2], (NUM_EXPERTS, D_MODEL, D_FF), jnp.float32) * s_dm, 'b1': jnp.zeros((NUM_EXPERTS, D_FF), jnp.float32), 'w2': jax.random.normal(ks[3], (NUM_EXPERTS, D_FF, D_MODEL), jnp.float32) * s_ff, 'b2': jnp.zeros((NUM_EXPERTS, D_MODEL), jnp.float32)}
    _L1_ffn_in = _L1_ffn_setup()
    _d = {'L0_attn_x': _L0_attn_in['x'], 'L0_attn_Wq': _L0_attn_in['Wq'], 'L0_attn_bq': _L0_attn_in['bq'], 'L0_attn_Wk': _L0_attn_in['Wk'], 'L0_attn_bk': _L0_attn_in['bk'], 'L0_attn_Wv': _L0_attn_in['Wv'], 'L0_attn_bv': _L0_attn_in['bv'], 'L0_attn_Wc2q': _L0_attn_in['Wc2q'], 'L0_attn_bc2q': _L0_attn_in['bc2q'], 'L0_attn_Wo': _L0_attn_in['Wo'], 'L0_attn_bo': _L0_attn_in['bo'], 'L0_attn_g1': _L0_attn_in['g1'], 'L0_attn_beta1': _L0_attn_in['beta1'], 'L0_attn_g2': _L0_attn_in['g2'], 'L0_attn_beta2': _L0_attn_in['beta2'], 'L0_attn_W1': _L0_attn_in['W1'], 'L0_attn_b1': _L0_attn_in['b1'], 'L0_attn_Wm': _L0_attn_in['Wm'], 'L0_attn_bm': _L0_attn_in['bm'], 'L0_attn_Wqo': _L0_attn_in['Wqo'], 'L0_attn_bqo': _L0_attn_in['bqo'], 'L0_attn_W2': _L0_attn_in['W2'], 'L0_attn_b2': _L0_attn_in['b2'], 'L0_ffn_w_router': _L0_ffn_in['w_router'], 'L0_ffn_gate_up_proj': _L0_ffn_in['gate_up_proj'], 'L0_ffn_down_proj': _L0_ffn_in['down_proj'], 'L0_ffn_w_gate': _L0_ffn_in['w_gate'], 'L0_ffn_w_up': _L0_ffn_in['w_up'], 'L0_ffn_w_down': _L0_ffn_in['w_down'], 'L1_attn_w_attn': _L1_attn_in['w_attn'], 'L1_attn_b_attn': _L1_attn_in['b_attn'], 'L1_attn_w_proj': _L1_attn_in['w_proj'], 'L1_attn_b_proj': _L1_attn_in['b_proj'], 'L1_attn_w_fc': _L1_attn_in['w_fc'], 'L1_attn_b_fc': _L1_attn_in['b_fc'], 'L1_attn_w_mlp_proj': _L1_attn_in['w_mlp_proj'], 'L1_attn_b_mlp_proj': _L1_attn_in['b_mlp_proj'], 'L1_ffn_router_w': _L1_ffn_in['router_w'], 'L1_ffn_router_b': _L1_ffn_in['router_b'], 'L1_ffn_w1': _L1_ffn_in['w1'], 'L1_ffn_b1': _L1_ffn_in['b1'], 'L1_ffn_w2': _L1_ffn_in['w2'], 'L1_ffn_b2': _L1_ffn_in['b2']}
    _x0 = _d['L0_attn_x']
    _d['L0_attn_x'] = jax.random.normal(jax.random.fold_in(jax.random.key(seed), 1), (2, 1024, 128), dtype=_x0.dtype)
    del _x0
    return _d

def reference(L0_attn_x, L0_attn_Wq, L0_attn_bq, L0_attn_Wk, L0_attn_bk, L0_attn_Wv, L0_attn_bv, L0_attn_Wc2q, L0_attn_bc2q, L0_attn_Wo, L0_attn_bo, L0_attn_g1, L0_attn_beta1, L0_attn_g2, L0_attn_beta2, L0_attn_W1, L0_attn_b1, L0_attn_Wm, L0_attn_bm, L0_attn_Wqo, L0_attn_bqo, L0_attn_W2, L0_attn_b2, L0_ffn_w_router, L0_ffn_gate_up_proj, L0_ffn_down_proj, L0_ffn_w_gate, L0_ffn_w_up, L0_ffn_w_down, L1_attn_w_attn, L1_attn_b_attn, L1_attn_w_proj, L1_attn_b_proj, L1_attn_w_fc, L1_attn_b_fc, L1_attn_w_mlp_proj, L1_attn_b_mlp_proj, L1_ffn_router_w, L1_ffn_router_b, L1_ffn_w1, L1_ffn_b1, L1_ffn_w2, L1_ffn_b2):

    def _L0_attn_ref(x, Wq, bq, Wk, bk, Wv, bv, Wc2q, bc2q, Wo, bo, g1, beta1, g2, beta2, W1, b1, Wm, bm, Wqo, bqo, W2, b2):
        import jax, jax.numpy as jnp
        import numpy as np
        B, S, HID = (4, 128, 128)
        H = 8
        HD = HID // H
        NQ = 8
        RATIO = 0.5
        FF = 4 * HID
        EPS_COS = 1e-08
        LN_EPS = 1e-05

        def _layernorm(x, g, b):
            m = jnp.mean(x, axis=-1, keepdims=True)
            v = jnp.var(x, axis=-1, keepdims=True)
            return (x - m) * jax.lax.rsqrt(v + LN_EPS) * g + b
        Q = jnp.einsum('bsh,nhd->bnsd', x, Wq) + bq[None, :, None, :]
        K = jnp.einsum('bsh,nhd->bnsd', x, Wk) + bk[None, :, None, :]
        V = jnp.einsum('bsh,nhd->bnsd', x, Wv) + bv[None, :, None, :]
        qq = jnp.einsum('bnsd,ndq->bnsq', Q, Wc2q) + bc2q[None, :, None, :]
        kq = jnp.einsum('bnsd,ndq->bnsq', K, Wc2q) + bc2q[None, :, None, :]
        qn = jnp.linalg.norm(qq, axis=-1)
        kn = jnp.linalg.norm(kq, axis=-1)
        dots = jnp.einsum('bnsq,bntq->bnst', qq, kq)
        fid = dots / jnp.maximum(qn[..., :, None] * kn[..., None, :], EPS_COS)
        qw = fid * (1.0 + 0.1 * jnp.sin(fid * jnp.pi))
        cw = jnp.einsum('bnsd,bntd->bnst', Q, K) / np.sqrt(HD).astype(np.float32)
        aw = RATIO * qw + (1.0 - RATIO) * cw
        probs = jax.nn.softmax(aw, axis=-1)
        heads = jnp.einsum('bnst,bntd->bnsd', probs, V)
        attn = heads.transpose(0, 2, 1, 3).reshape(x.shape[0], x.shape[1], HID)
        attn = attn @ Wo + bo
        x1 = _layernorm(x + attn, g1, beta1)
        h = x1 @ W1 + b1
        qm = h @ Wm + bm
        qe = jnp.tanh(qm) * jnp.cos(qm * (jnp.pi / 4))
        ha = qe @ Wqo + bqo
        ff = ha @ W2 + b2
        out = _layernorm(x1 + ff, g2, beta2)
        return out

    def _L0_ffn_ref(hidden_states, w_router, gate_up_proj, down_proj, w_gate, w_up, w_down):
        import jax, jax.numpy as jnp
        import numpy as np
        E = 16
        H = 128
        F = 256
        TOP_K = 1
        B, S = (2, 128)
        b, s, h = hidden_states.shape
        x = hidden_states.reshape(-1, h)
        logits = x @ w_router.T
        _, top_idx = jax.lax.top_k(logits, TOP_K)
        mask = jax.nn.one_hot(top_idx, E, dtype=logits.dtype).sum(axis=1)
        scores = jax.nn.sigmoid(logits) * mask
        masked_inputs = scores.T[:, :, None] * x[None, :, :]
        gate_up = jnp.einsum('eth,ehf->etf', masked_inputs, gate_up_proj)
        gate, up = jnp.split(gate_up, 2, axis=-1)
        expert_out = jnp.einsum('etf,efh->eth', up * jax.nn.silu(gate), down_proj)
        shared = jax.nn.silu(x @ w_gate.T) * (x @ w_up.T) @ w_down.T
        out = shared + expert_out.sum(axis=0)
        return out.reshape(b, s, h)

    def _L1_attn_ref(x, w_attn, b_attn, w_proj, b_proj, w_fc, b_fc, w_mlp_proj, b_mlp_proj):
        import jax, jax.numpy as jnp
        import numpy as np
        import math
        B, T, C, H = (4, 256, 128, 16)
        EPS = 1e-10

        def layernorm(x):
            mean = jnp.mean(x, axis=-1, keepdims=True)
            xmu = x - mean
            var = jnp.mean(xmu * xmu, axis=-1, keepdims=True)
            return xmu / jnp.sqrt(var + EPS)

        def new_gelu(x):
            c = math.sqrt(2.0 / math.pi)
            return 0.5 * x * (1.0 + jnp.tanh(c * (x + 0.044715 * x * x * x)))

        def attention(x, w_attn, b_attn, w_proj, b_proj):
            b, t, cdim = x.shape
            d = cdim // H
            ca = x @ w_attn.T + b_attn
            q, k, v = jnp.split(ca, 3, axis=2)
            q = q.reshape(b, t, H, d)
            k = k.reshape(b, t, H, d)
            v = v.reshape(b, t, H, d)
            att = jnp.einsum('bthd,bshd->bhts', q, k) * (1.0 / math.sqrt(d))
            mask = jnp.tril(jnp.ones((t, t), dtype=bool))
            att = jnp.where(mask, att, -jnp.inf)
            att = jax.nn.softmax(att, axis=-1)
            y = jnp.einsum('bhts,bshd->bthd', att, v).reshape(b, t, cdim)
            return y @ w_proj.T + b_proj
        x = x + attention(layernorm(x), w_attn, b_attn, w_proj, b_proj)
        h = new_gelu(layernorm(x) @ w_fc.T + b_fc)
        x = x + (h @ w_mlp_proj.T + b_mlp_proj)
        return x

    def _L1_ffn_ref(x, router_w, router_b, w1, b1, w2, b2):
        import jax, jax.numpy as jnp
        import numpy as np
        D_MODEL = 128
        D_FF = 512
        NUM_EXPERTS = 8
        TOP_K = 2
        B, S = (4, 512)
        Bx, Sx, D = x.shape
        xf = x.reshape(-1, D)
        logits = xf @ router_w + router_b
        top_w, sel = jax.lax.top_k(logits, TOP_K)
        gates = jax.nn.softmax(top_w, axis=-1)

        def body(i, acc):
            h = jax.nn.gelu(xf @ w1[i] + b1[i], approximate=False)
            out_i = h @ w2[i] + b2[i]
            gate_i = jnp.sum(gates * (sel == i), axis=-1, keepdims=True)
            return acc + out_i * gate_i
        out = jax.lax.fori_loop(0, NUM_EXPERTS, body, jnp.zeros_like(xf))
        return out.reshape(Bx, Sx, D)
    x = L0_attn_x
    xn = _layernorm(x, axis=-1)
    x = x + _L0_attn_ref(xn, L0_attn_Wq, L0_attn_bq, L0_attn_Wk, L0_attn_bk, L0_attn_Wv, L0_attn_bv, L0_attn_Wc2q, L0_attn_bc2q, L0_attn_Wo, L0_attn_bo, L0_attn_g1, L0_attn_beta1, L0_attn_g2, L0_attn_beta2, L0_attn_W1, L0_attn_b1, L0_attn_Wm, L0_attn_bm, L0_attn_Wqo, L0_attn_bqo, L0_attn_W2, L0_attn_b2) + _L0_ffn_ref(xn, L0_ffn_w_router, L0_ffn_gate_up_proj, L0_ffn_down_proj, L0_ffn_w_gate, L0_ffn_w_up, L0_ffn_w_down)
    xn = _layernorm(x, axis=-1)
    x = x + _L1_attn_ref(xn, L1_attn_w_attn, L1_attn_b_attn, L1_attn_w_proj, L1_attn_b_proj, L1_attn_w_fc, L1_attn_b_fc, L1_attn_w_mlp_proj, L1_attn_b_mlp_proj) + _L1_ffn_ref(xn, L1_ffn_router_w, L1_ffn_router_b, L1_ffn_w1, L1_ffn_b1, L1_ffn_w2, L1_ffn_b2)
    return x

_drawn_inputs = setup_inputs


def setup_inputs(seed=0):
    import zlib

    import numpy as np

    out = dict(_drawn_inputs(seed))
    spreads = {'L0_attn_bq': (0.0, 2.0),
     'L0_attn_bk': (0.0, 2.0),
     'L0_attn_bv': (0.0, 0.478),
     'L0_attn_bc2q': (0.0, 2.0),
     'L0_attn_bo': (0.0, 0.392),
     'L0_attn_g1': (1.0, 0.2),
     'L0_attn_beta1': (0.0, 0.386),
     'L0_attn_g2': (1.0, 0.2),
     'L0_attn_beta2': (0.0, 0.413),
     'L0_attn_b1': (0.0, 2.0),
     'L0_attn_bm': (0.0, 2.0),
     'L0_attn_bqo': (0.0, 0.8),
     'L0_attn_b2': (0.0, 0.435),
     'L1_ffn_router_b': (0.0, 0.427),
     'L1_ffn_b1': (0.0, 1.243),
     'L1_ffn_b2': (0.0, 0.846)}
    factors = {'L0_attn_Wq': 8.0,
     'L0_attn_Wk': 8.0,
     'L0_attn_Wv': 8.0,
     'L0_attn_Wc2q': 200.0,
     'L0_attn_Wo': 3.183,
     'L0_attn_W1': 23.833,
     'L0_attn_Wm': 23.433,
     'L0_attn_Wqo': 22.992,
     'L0_ffn_w_router': 8.0,
     'L0_ffn_gate_up_proj': 8.0,
     'L0_ffn_down_proj': 8.0,
     'L0_ffn_w_gate': 8.0,
     'L0_ffn_w_up': 7.779,
     'L0_ffn_w_down': 6.48,
     'L1_attn_w_attn': 8.0,
     'L1_attn_b_attn': 8.0,
     'L1_attn_w_proj': 8.0,
     'L1_attn_b_proj': 21.369,
     'L1_attn_w_fc': 3.233,
     'L1_attn_b_fc': 24.019,
     'L1_attn_w_mlp_proj': 3.184,
     'L1_attn_b_mlp_proj': 21.879}
    for name, (base, spread) in spreads.items():
        noise = np.random.default_rng([zlib.crc32(name.encode()), seed]).standard_normal(out[name].shape)
        drawn = base * np.exp(spread * noise) if base else spread * noise
        out[name] = jnp.asarray(drawn.astype(out[name].dtype))
    for name, factor in factors.items():
        out[name] = (out[name] * factor).astype(out[name].dtype)
    return out
```

```python
from contextlib import ExitStack
import math

import numpy as np
import concourse.bass as bass
from concourse import mybir

ALU = mybir.AluOpType
ACT = mybir.ActivationFunctionType
AX = mybir.AxisListType
F32 = mybir.dt.float32
BF16 = mybir.dt.bfloat16
U32 = mybir.dt.uint32
I32 = mybir.dt.int32

P = 128
B, S, C = 2, 1024, 128
NT = B * S // P
KT = S // P
NEG = -1e30
ROUND = 12582912.0
PARTS = 3
Q_ROWS = (0, 0, 1, 1, 0, 2)
K_ROWS = (0, 1, 0, 1, 2, 0)
NR = len(Q_ROWS)

H0, D0, NQ = 8, 16, 8
R0 = NR * D0
RF = NR * NQ
UNITS0 = B * H0
PAIRS0 = UNITS0 // 2
QSCALE0 = 10.0 / math.sqrt(D0)
EPS_COS = 1e-8
PI_IN = math.pi * (1 - 8e-7)
E0, F0 = 16, 256
NB0 = NT + E0
XB, SHB = NB0 // PAIRS0, NT // PAIRS0
NBP = XB + SHB
H1, D1 = 16, 8
R1 = NR * D1
UNITS1 = B * H1
E1, F1, TOP1 = 8, 512, 2
NB1 = TOP1 * NT + E1


def build(nc, a, out, upto=9):
    with ExitStack() as ctx:
        def sb(name, shape, dt=F32):
            return ctx.enter_context(nc.sbuf_tensor(name, shape, dt))

        def dram(name, shape, dt=F32):
            return nc.dram_tensor(name, shape, dt, kind="Internal").ap()

        q0d = dram("q0d", (B * H0 * D0, NR, S), BF16)
        k0d = dram("k0d", (B * H0 * D0, NR, S), BF16)
        fq0d = dram("fq0d", (B * H0 * NQ, NR, S), BF16)
        fk0d = dram("fk0d", (B * H0 * NQ, NR, S), BF16)
        n0d = dram("n0d", (2 * UNITS0, S))
        m0d = dram("m0d", (UNITS0, PARTS * KT, P), BF16)
        xs0 = dram("xs0", (NB0 * P, C))
        q1d = dram("q1d", (UNITS1 * D1, NR, S), BF16)
        k1d = dram("k1d", (UNITS1 * D1, NR, S), BF16)
        m1d = dram("m1d", (UNITS1, PARTS * KT, P), BF16)
        xs1 = dram("xs1", (NB1 * P, C))
        ys1 = dram("ys1", (NB1 * P, C))
        x1d = dram("x1d", (P, NT * C))
        ys0 = dram("ys0", ((NB0 + NT) * P, C))

        xn = sb("xn", [P, NT, C])
        xT = sb("xT", [P, NT * P])
        W = sb("W", [P, 12288])
        gu_w = W[:, 0:E0 * 2 * F0]
        dn_w = W[:, E0 * 2 * F0:E0 * 2 * F0 + E0 * 2 * C]
        Z = sb("Z", [P, 16384])
        OT = sb("OT", [P, UNITS0, 256])
        snb = sb("snb", [P, 2, S])
        QM = sb("QM", [P, 2, S], BF16)
        KM = sb("KM", [P, 2, S], BF16)
        QS = sb("QS", [P, 2, S], BF16)
        KS = sb("KS", [P, 2, S], BF16)
        FQ = sb("FQ", [P, 2, S], BF16)
        FK = sb("FK", [P, 2, S], BF16)
        Vc = sb("Vc", [P, UNITS0 * KT * D0])
        VU = sb("VU", [P, 2, KT, 32])
        ident = sb("ident", [P, P])
        identb = sb("identb", [P, P], BF16)
        onesb = sb("onesb", [P, P], BF16)
        lowb = sb("lowb", [P, P], BF16)
        ones_row = sb("ones_row", [1, P])
        iota_e = sb("iota_e", [P, E0])
        iota_b = sb("iota_b", [P, NB1])
        ones_e = sb("ones_e", [P, E0])
        minus_half = sb("minus_half", [P, 64])
        below = sb("below", [P, P], BF16)
        above = sb("above", [P, P], BF16)
        sign = sb("sign", [P, 2, KT * D0])
        half_pi = sb("half_pi", [P, 1])
        scan_keep = sb("scan_keep", [P, E0, NT])
        wqkv = sb("wqkv", [P, 3, P])
        bqk = sb("bqk", [P, 2])
        bd = sb("bd", [P, H0 * NQ])
        guT = sb("guT", [P, 2 * F0])
        dnT = sb("dnT", [P, 2, C])
        rout = sb("rout", [P, E0])
        mv = sb("mv", [P, NT, 2])
        st = sb("st", [P, NT, 6])
        ve = sb("ve", [P, NT])
        rstd = sb("rstd", [P, NT])
        M = sb("M", [P, 2, KT])
        msp = sb("msp", [P, 2, 4, KT])
        mpart = sb("mpart", [P, 2, PARTS, KT], BF16)
        mrow = sb("mrow", [PARTS * KT, 2, P], BF16)
        inv = sb("inv", [P, 4, KT * H0])
        ss = sb("ss", [P, 4, KT * H0])
        flag_i = sb("flag_i", [1, 1], I32)
        eb_i = sb("eb_i", [1, 64], I32)
        pos_i = sb("pos_i", [P, TOP1, NT], U32)
        score = sb("score", [P, TOP1, NT])
        xb = sb("xb", [P, 2, C])
        xbT = sb("xbT", [P, 2, P])
        sg = sb("sg", [P, F0])
        hb = sb("hb", [P, 2, F0])
        hT = sb("hT", [P, 2, F0])
        yb = sb("yb", [P, 2, C])

        PS = ctx.enter_context(nc.psum_tensor("PS", [P, 8, 512], F32))

        def bank(i, n=1):
            return PS[:, i:i + n, :].rearrange("p b c -> p (b c)")

        qf = [Z[:, r * S:(r + 1) * S] for r in range(4)]
        res = [Z[:, (4 + r) * S:(5 + r) * S] for r in range(4)]
        part = [Z[:, 8192 + 1536 * r:8192 + 1536 * (r + 1)].bitcast(BF16).rearrange("p (j s) -> p j s", j=3)
                for r in range(4)]
        qq = [Z[:, 14336 + 512 * r:14336 + 512 * (r + 1)] for r in range(4)]
        QSf = QS[:, :, :].rearrange("p a s -> p (a s)").bitcast(F32)
        nT, nrm, small = QSf[0:64, 0:512], QSf[:, 512:768], QSf[:, 768:770]
        OTf = OT[:, :, :].rearrange("p u s -> p (u s)")
        x_in = OTf[:, 0:2048].rearrange("p (t c) -> p t c", c=C)
        sq = OTf[:, 2048:2560]
        R = OTf[:, 2560:4096]
        lg = R[:, 0:256]
        mx8 = R[:, 256:384].rearrange("p (t k) -> p t k", k=8)
        ix8 = R[:, 384:512].bitcast(U32).rearrange("p (t k) -> p t k", k=8)
        ixf = R[:, 512:544].rearrange("p (t k) -> p t k", k=2)
        oh = R[:, 544:800]
        oh_b = R[:, 800:928].bitcast(BF16)
        tot = R[:, 928:1184]
        cum = R[:, 1184:1440]
        nbk, incl = R[:, 1440:1456], R[:, 1456:1472]
        basex, posf = R[:, 1472:1488], R[:, 1488:1520]
        zeros = snb[:, 1, :]
        wst = snb[:, :, :].rearrange("p a s -> p (a s)")

        attn = Z[:, 0:2048].rearrange("p (t c) -> p t c", c=C)
        attnT = Z[:, 2048:4096]
        x1p = Z[:, 4096:6144].rearrange("p (t c) -> p t c", c=C)
        x1 = Z[:, 6144:8192].rearrange("p (t c) -> p t c", c=C)
        bdq = Z[:, 8192:10240].rearrange("p (t c) -> p t c", c=C)
        xr = Z[:, 10240:12288].rearrange("p (t c) -> p t c", c=C)
        yg = Z[:, 12288:14336].rearrange("p (t c) -> p t c", c=C)
        ysh = Z[:, 14336:16384].rearrange("p (t c) -> p t c", c=C)
        NROW = 64
        QMf = QM[:, :, :].rearrange("p a s -> p (a s)").bitcast(F32)
        KMf = KM[:, :, :].rearrange("p a s -> p (a s)").bitcast(F32)
        FQf = FQ[:, :, :].rearrange("p a s -> p (a s)").bitcast(F32)
        FKf = FK[:, :, :].rearrange("p a s -> p (a s)").bitcast(F32)
        w1r, w2r = QMf[:, 0:512], QMf[:, 512:1024].rearrange("p (t c) -> p t c", c=C)
        w1T, qoT = KMf[:, 0:512], KMf[:, 512:1024]
        wo, bo_b = FQf[:, 0:128], FQf[:, 128:256]
        g1_b, be1_b, g2_b, be2_b, b2_b, bff = [FQf[:, 256 + 128 * i:384 + 128 * i] for i in range(6)]
        wm = FKf[:, 0:32].rearrange("p (t q) -> p t q", q=NQ)
        w1m, bm_b, bmm = FKf[:, 32:40], FKf[:, 40:48], FKf[:, 48:56]
        brow = KS[:, :, :].rearrange("p a s -> p (a s)").bitcast(F32)[0:1, :]
        bv_b, bc2q_b = FQf[:, 256:384], FQf[:, 384:448]
        bqk_row = FQf[0:1, 0:2 * P]
        wqo8 = FKf[0:8, 512:1024]
        rep8 = FKf[0:8, 64:192]
        qm, qt, qc, qe = [FKf[:, 192 + 128 * i:320 + 128 * i] for i in range(2)] + [FKf[:, 448:512], None]
        qm = snb[:, 0, 0:128]
        qt = snb[:, 0, 128:256]
        qc = snb[:, 0, 256:384]
        qe = snb[:, 0, 384:512]
        qeT = snb[:, 0, 512:640]
        repcol = snb[:, 1, :]
        rec = snb[:, 0, 640:672]

        w1_all = W[:, 0:E1 * F1]
        w2_all = W[:, E1 * F1:2 * E1 * F1]
        W1 = W[:, 2 * E1 * F1:12288]
        raw_attn, raw_proj, raw_fc, raw_mlp = W1[:, 0:384], W1[:, 384:512], W1[:, 512:1024], W1[:, 1024:1536]
        wprojT, wfcT, wmlpT = W1[:, 1536:1664], W1[:, 1664:2176], W1[:, 2176:2688]
        bv1_b, bproj_b, bmlp_b, rb1_b, rw1 = W1[:, 2688:2816], W1[:, 2816:2944], W1[:, 2944:3072], W1[:, 3072:3080], W1[:, 3080:3088]
        bcols = W1[:, 3088:3094]
        brow1 = W1[0:1, 3200:3968]
        b1_row, b2_row = OTf[0:1, :], FQf[0:1, :]
        lx = snb[:, :, :].rearrange("p a (t c) -> p (a t) c", c=C)
        lxT = OTf[:, 0:2048]
        slots = [(QS, KS, 0), (QS, KS, 1), (QM, KM, 0), (QM, KM, 1)]
        M2 = msp[:, :, 3, 0:4]
        OT1 = Z[:, 8192:16384].rearrange("p (u s) -> p u s", s=256)
        hb1 = snb[:, 0, :].rearrange("p (i f) -> p i f", i=2)
        hT1 = snb[:, 1, :].rearrange("p (i f) -> p i f", i=2)
        HT = Z[:, 8192:16384].rearrange("p (f s) -> p f s", f=4)
        lx2 = x1p
        yg1 = Z[:, 8192:12288].rearrange("p (k t c) -> p k t c", k=2, c=C)
        x1r = Z[:, 12288:14336].rearrange("p (t c) -> p t c", c=C)
        MB = (0, 1, 7)

        names = """const x_loaded wqkv_loaded w_raw0 w_small0 gu_loaded dn_loaded zeroed
            ln_stats ln_rstd ln_done tr_ready tr_done wt_ready wt_done
            v_ready v_done lg_ready lg_done proj_ready qf_ready p1_ready res_ready p2_ready p3_ready qk_stored
            qq_ready ss_ready inv_ready qh_ready hat_ready hatT_ready f_stored dve_step pool_step act_step
            oh_ready rank_ready pos_ready top_ready score_ready xsrc_ready scattered
            max_loaded main_loaded f_ready f_free sin_done c_ready z_done exp_done pv_done pv_evac v_copied
            m_split mt_ready mt_copied m_stored m_loaded
            xb_loaded0 xb_loaded1 xt_ready xbT_ready gu_ready silu_done h_ready ht_ready hT_done out_ready yb_ready y_stored0 y_stored1
            post_loaded o_ready o_done prep_ready prep_done wo_ready wo_done qm_ready qm_done tc_done qe_ready
            qeT_ready qeT_done ff_ready ff_done bo_added bff_added bd_masked gathered xsum
            res0_ready out_stored
            nrm_ready nt_ready flag_ready n_stored n_loaded g_ready g_done g_step
            x1_stored l1_loaded wt1_ready wt1_done v1_ready v1_done lg1_ready gate_ready gates_done scattered1
            slot_loaded0 slot_loaded1 slot_loaded2 slot_loaded3 max1_ready max1_free max1_whole c1_ready p1_done pv1_done head1_out
            v1_copied vu1_cleared m1_split mt1_ready mt1_copied m1_stored m1_loaded
            x1b_loaded0 x1b_loaded1 x1t_ready x1t_done gu1_ready h1_ready h1t_ready h1t_done o1_ready y1_ready
            y1_stored0 y1_stored1 gathered1 bias1_loaded o1t_ready o1n_done bproj_added proj1_ready proj1_done
            fc_ready fc_done mlp_ready mlp_done x1_loaded bmlp_added""".split()
        s = {n: ctx.enter_context(nc.semaphore(n)) for n in names}
        block = ctx.enter_context(nc.Block())

        def dve_link(ins, cnt=[0]):
            cnt[0] += 1
            ins.then_inc(s["dve_step"], 1)
            nc.vector.wait_ge(s["dve_step"], cnt[0])

        def pool_link(ins, cnt=[0]):
            cnt[0] += 1
            ins.then_inc(s["pool_step"], 1)
            nc.gpsimd.wait_ge(s["pool_step"], cnt[0])

        def Zt(u, k):
            return Z[:, (u * KT + k) * S:(u * KT + k + 1) * S]

        FB = (0, 4)


        def sp_max_load(sp, p):
            for t, d in ((QM, q0d), (KM, k0d)):
                sp.dma_start(t[0:R0, :, :], d[bass.ds(p * 32, 32)].rearrange("(u d) j s -> (d j) u s", u=2)).then_inc(s["max_loaded"], 16)

        def sp_main_load(sp, p):
            for t, d in ((QS, q0d), (KS, k0d)):
                sp.dma_start(t[0:R0, :, :], d[bass.ds(p * 32, 32)].rearrange("(u d) j s -> (d j) u s", u=2)).then_inc(s["main_loaded"], 16)
            for t, d in ((FQ, fq0d), (FK, fk0d)):
                sp.dma_start(t[0:RF, :, :], d[bass.ds(p * 16, 16)].rearrange("(u d) j s -> (d j) u s", u=2)).then_inc(s["main_loaded"], 16)

        def sp_m_rows(sp, p, u):
            sp.wait_ge(s["mt_copied"], p * 2 + u + 1)
            sp.dma_start(m0d[bass.ds(p * 2 + u, 1)].rearrange("o r q -> (o r) q"), mrow[:, u, :]).then_inc(s["m_stored"], 16)
            sp.wait_ge(s["m_stored"], p * 32 + 16 * u + 32)
            sp.dma_start(QS[R0:R0 + PARTS, u, :], m0d[bass.ds(p * 2 + u, 1)].rearrange("o (j i) q -> (o j) (i q)", j=PARTS)).then_inc(s["m_loaded"], 16)

        def sp_norm_rows(sp, p, u):
            for i, t in enumerate((FQf, FKf)):
                sp.dma_start(t[NROW:NROW + 1, :], n0d[bass.ds(p * 2 + u + i * UNITS0, 1)]).then_inc(s["n_loaded"], 16)

        def sp_pair(sp, p, flag, last):
            sp_m_rows(sp, p, 1)
            if not last:
                sp.wait_ge(s["f_ready"], p * 32 + 16)
                sp_max_load(sp, p + 1)
            for i in range(NBP):
                if i < XB:
                    sp.wait_ge(s["xt_ready"], p * XB + i + 1)
                    sp.dma_start(xb[:, i % 2, :], xs0[bass.ds(p * (XB * P) + i * P, P)]).then_inc(s[f"xb_loaded{i % 2}"], 16)
                if i >= 1:
                    sp_y_store(sp, p, i - 1)
                if i == 2:
                    with sp.If(flag > 0):
                        sp.wait_ge(s["g_done"], p * 16 + 8)
                        sp_norm_rows(sp, p, 1)
            sp_y_store(sp, p, NBP - 1)
            if not last:
                sp.wait_ge(s["c_ready"], p * 16 + 16)
                sp_main_load(sp, p + 1)
                with sp.If(flag > 0):
                    sp_norm_rows(sp, p + 1, 0)
                sp_m_rows(sp, p + 1, 0)

        def sp_y_store(sp, p, i):
            sp.wait_ge(s["yb_ready"], p * NBP + i + 1)
            row = p * (XB * P) + i * P if i < XB else p * (SHB * P) + (NB0 + i - XB) * P
            sp.dma_start(ys0[bass.ds(row, P)], yb[:, i % 2, :]).then_inc(s[f"y_stored{i % 2}"], 16)

        def sp_weights1(sp):
            rows = lambda n: a["L1_attn_" + n].rearrange("(t p) c -> p t c", p=P)
            for t, src in ((raw_attn.rearrange("p (t c) -> p t c", c=C), rows("w_attn")), (raw_proj, a["L1_attn_w_proj"]),
                           (raw_fc.rearrange("p (t c) -> p t c", c=C), rows("w_fc")), (raw_mlp, a["L1_attn_w_mlp_proj"]),
                           (brow1[:, 0:256], a["L1_attn_b_attn"][0:256].rearrange("(o f) -> o f", o=1)),
                           (brow1[:, 256:768], a["L1_attn_b_fc"].rearrange("(o f) -> o f", o=1)),
                           (bv1_b, a["L1_attn_b_attn"][256:384].partition_broadcast(P)), (bproj_b, a["L1_attn_b_proj"].partition_broadcast(P)),
                           (bmlp_b, a["L1_attn_b_mlp_proj"].partition_broadcast(P)), (rb1_b, a["L1_ffn_router_b"].partition_broadcast(P)),
                           (rw1, a["L1_ffn_router_w"])):
                sp.dma_start(t, src).then_inc(s["l1_loaded"], 16)
            sp.dma_start(w1_all.rearrange("p (e f) -> p e f", f=F1), a["L1_ffn_w1"].rearrange("e c f -> c e f")).then_inc(s["l1_loaded"], 16)
            for e in range(0, E1, 2):
                sp.dma_start(w2_all[:, e * F1:(e + 2) * F1].rearrange("p (e c) -> p e c", c=C),
                             a["L1_ffn_w2"][e:e + 2].rearrange("e (t p) c -> p (e t) c", p=P)).then_inc(s["l1_loaded"], 16)

        L1_LOADS = 16

        def sp_layer1(sp):
            for r in range(4):
                dst, rows = (q1d, k1d)[r % 2], (Q_ROWS, K_ROWS)[r % 2]
                sp.wait_ge(s["p3_ready"], 8 + r + 1)
                for j, n in enumerate(rows):
                    sp.dma_start(dst[(r // 2) * P:(r // 2 + 1) * P, j, :], part[r][:, n, :]).then_inc(s["qk_stored"], 16)
            sp.wait_ge(s["qk_stored"], 2 * 16 * NR * 4)
            sp.wait_ge(s["vu1_cleared"], 1)
            for n in range(4):
                sp_slot_load(sp, n, n)
            sp_m1_rows(sp, 0, 0)
            with sp.Fori(0, UNITS1 // 4 - 1) as g4:
                for w in range(4):
                    sp_unit1(sp, g4, w, False)
            for w in range(4):
                sp_unit1(sp, UNITS1 // 4 - 1, w, True)
            sp.dma_start(b1_row, a["L1_ffn_b1"].rearrange("(o e) f -> o (e f)", o=1)).then_inc(s["bias1_loaded"], 16)
            sp.dma_start(b2_row, a["L1_ffn_b2"].rearrange("(o e) c -> o (e c)", o=1)).then_inc(s["bias1_loaded"], 16)
            sp.wait_ge(s["scattered1"], 16 * TOP1 * NT)
            for i in range(2):
                sp.dma_start(xb[:, i, :], xs1[i * P:(i + 1) * P]).then_inc(s[f"x1b_loaded{i}"], 16)
            sp_block1(sp, 0, 2, True, False)
            sp_block1(sp, 0, 3, True, False)
            with sp.Fori(0, NB1 // 2 - 2) as h:
                for i in range(2):
                    sp_block1(sp, h, i + 4, True, True)
            for i in range(4):
                sp_block1(sp, NB1 // 2 - 2, i + 4, False, True)
            for i in range(2):
                sp.wait_ge(s[f"y1_stored{i}"], 8 * NB1 + 16)
            sp.wait_ge(s["fc_done"], 16)
            sp.wait_ge(s["mlp_ready"], 4)
            sp.dma_start(x1r.rearrange("p t c -> p (t c)"), x1d).then_inc(s["x1_loaded"], 16)
            sp.wait_ge(s["mlp_done"], 1)
            sp.dma_start(out.rearrange("b (k p) c -> p (b k) c", p=P)[:, 0:KT], xn[:, 0:KT]).then_inc(s["out_stored"], 16)
            sp.dma_start(out.rearrange("b (k p) c -> p (b k) c", p=P)[:, KT:NT], xn[:, KT:NT]).then_inc(s["out_stored"], 16)
            sp.wait_ge(s["x1_stored"], 16)
            sp.wait_ge(s["out_stored"], 32)

        def sp_block1(sp, h, i, load, store):
            if load:
                sp.wait_ge(s["x1t_ready"], h * 2 + i - 1)
                sp.dma_start(xb[:, i % 2, :], xs1[bass.ds(h * (2 * P) + i * P, P)]).then_inc(s[f"x1b_loaded{i % 2}"], 16)
            if store:
                sp.wait_ge(s["y1_ready"], h * 2 + i - 3)
                sp.dma_start(ys1[bass.ds(h * (2 * P) + (i - 4) * P, P)], yb[:, i % 2, :]).then_inc(s[f"y1_stored{i % 2}"], 16)

        def sp_slot_load(sp, unit, slot):
            q, k, u = slots[slot]
            for t, d in ((q, q1d), (k, k1d)):
                sp.dma_start(t[0:R1, u, :], d[bass.ds(unit * D1, D1)].rearrange("d j s -> (d j) s")).then_inc(s[f"slot_loaded{slot}"], 16)

        def sp_m1_rows(sp, unit, slot):
            sp.wait_ge(s["mt1_copied"], unit + 1)
            sp.dma_start(m1d[bass.ds(unit, 1)].rearrange("o r q -> (o r) q"), mrow[:, slot % 2, :]).then_inc(s["m1_stored"], 16)
            sp.wait_ge(s["m1_stored"], unit * 16 + 16)
            q, _, u = slots[slot]
            sp.dma_start(q[R1:R1 + PARTS, u, :], m1d[bass.ds(unit, 1)].rearrange("o (j i) q -> (o j) (i q)", j=PARTS)).then_inc(s["m1_loaded"], 16)

        def sp_unit1(sp, g4, w, last):
            if not (last and w == 3):
                sp_m1_rows(sp, g4 * 4 + w + 1, (w + 1) % 4)
            if not last:
                sp.wait_ge(s["c1_ready"], g4 * 32 + w * 8 + 8)
                sp_slot_load(sp, g4 * 4 + w + 4, w)

        @block.sync
        def _(sp):
            x_rows = a["L0_attn_x"].rearrange("b (k p) c -> p (b k) c", p=P)
            for b in range(B):
                sp.dma_start(x_in[:, b * KT:(b + 1) * KT, :], x_rows[:, b * KT:(b + 1) * KT, :]).then_inc(s["x_loaded"], 16)
            for i, n in enumerate(("Wq", "Wk", "Wv")):
                sp.dma_start(wqkv[:, i, :].rearrange("p (n d) -> p n d", n=H0),
                             a["L0_attn_" + n].rearrange("n c d -> c n d")).then_inc(s["wqkv_loaded"], 16)
            sp.wait_ge(s["const"], 1)
            for h in range(H0):
                sp.dma_start(bd[h * D0:(h + 1) * D0, h * NQ:(h + 1) * NQ], a["L0_attn_Wc2q"][h]).then_inc(s["w_small0"], 16)
            for d in range(NB1 // 8):
                sp.dma_start(xs1[d * 1024:(d + 1) * 1024].rearrange("(p r) c -> p (r c)", p=P), zeros).then_inc(s["zeroed"], 16)
            for d in range(NB0 // 8):
                sp.dma_start(xs0[d * 1024:(d + 1) * 1024].rearrange("(p r) c -> p (r c)", p=P), zeros).then_inc(s["zeroed"], 16)
            sp.dma_start(gu_w.rearrange("p (e f) -> p e f", e=E0), a["L0_ffn_gate_up_proj"].rearrange("e c f -> c e f")).then_inc(s["gu_loaded"], 16)
            for t in range(2):
                for e in (0, 8):
                    sp.dma_start(dn_w.rearrange("p (e t c) -> p t e c", e=E0, t=2)[:, t, e:e + 8],
                                 a["L0_ffn_down_proj"].rearrange("e (t p) c -> p t e c", p=P)[:, t, e:e + 8]).then_inc(s["dn_loaded"], 16)
            for r in range(4):
                dst, rows = (q0d, k0d)[r % 2], (Q_ROWS, K_ROWS)[r % 2]
                sp.wait_ge(s["p3_ready"], r + 1)
                for j, n in enumerate(rows):
                    sp.dma_start(dst[(r // 2) * P:(r // 2 + 1) * P, j, :], part[r][:, n, :]).then_inc(s["qk_stored"], 16)
            sp.wait_ge(s["qk_stored"], 16 * NR * 4)
            sp_max_load(sp, 0)
            for r in range(4):
                dst, rows = (fq0d, fk0d)[r % 2], (Q_ROWS, K_ROWS)[r % 2]
                sp.wait_ge(s["p3_ready"], 4 + r + 1)
                for j, n in enumerate(rows):
                    sp.dma_start(dst[(r // 2) * 64:(r // 2 + 1) * 64, j, :], part[r][0:64, n, :]).then_inc(s["f_stored"], 16)
            sp.wait_ge(s["f_stored"], 16 * NR * 4)
            sp.wait_ge(s["flag_ready"], 1)
            for r in range(4):
                row = (r % 2) * UNITS0 + (r // 2) * H0
                sp.dma_start(n0d[row:row + H0].rearrange("h (k q) -> (h k) q", q=P), nT[:, r * P:(r + 1) * P]).then_inc(s["n_stored"], 16)
            sp.wait_ge(s["n_stored"], 64)
            flag = sp.value_load(flag_i[0:1, 0:1], min_val=0, max_val=1)
            sp_main_load(sp, 0)
            with sp.If(flag > 0):
                sp_norm_rows(sp, 0, 0)
            sp_m_rows(sp, 0, 0)
            sp.wait_ge(s["scattered"], 16 * NT)
            with sp.Fori(0, PAIRS0 - 1) as p:
                sp_pair(sp, p, flag, False)
            sp_pair(sp, PAIRS0 - 1, flag, True)
            sp.wait_ge(s["pv_done"], 16 * PAIRS0 + 16)
            sp.dma_start(w1r, a["L0_attn_W1"]).then_inc(s["post_loaded"], 16)
            sp.dma_start(w2r, a["L0_attn_W2"].rearrange("(t p) c -> p t c", p=P)).then_inc(s["post_loaded"], 16)
            sp.dma_start(wqo8, a["L0_attn_Wqo"]).then_inc(s["post_loaded"], 16)
            sp.dma_start(wm, a["L0_attn_Wm"].rearrange("(t p) q -> p t q", p=P)).then_inc(s["post_loaded"], 16)
            for n, c in (("b1", 0), ("bqo", 512)):
                sp.dma_start(brow[:, c:c + 512], a["L0_attn_" + n].rearrange("(o f) -> o f", o=1)).then_inc(s["post_loaded"], 16)
            sp.dma_start(wo, a["L0_attn_Wo"]).then_inc(s["post_loaded"], 16)
            sp_weights1(sp)
            for t, n in ((bo_b, "bo"), (g1_b, "g1"), (be1_b, "beta1"), (g2_b, "g2"), (be2_b, "beta2"), (b2_b, "b2"), (bm_b, "bm")):
                sp.dma_start(t, a["L0_attn_" + n].partition_broadcast(P)).then_inc(s["post_loaded"], 16)
            for h in (0, KT):
                sp.dma_start(xr[:, h:h + KT], x_rows[:, h:h + KT]).then_inc(s["xsum"], 16)
            for i in range(2):
                sp.wait_ge(s[f"y_stored{i}"], 8 * NBP * PAIRS0 + 16)
            for h in (0, KT):
                sp.dma_start(ysh[:, h:h + KT], ys0[NB0 * P:].rearrange("(t p) c -> p t c", p=P)[:, h:h + KT]).then_inc(s["xsum"], 16)
            sp.wait_ge(s["res0_ready"], 1)
            sp.dma_start(x1d, xr.rearrange("p t c -> p (t c)")).then_inc(s["x1_stored"], 16)
            sp_layer1(sp)


        def pool_rstd(pool, n, eps):
            pool.wait_ge(s["ln_stats"], n + 1)
            pool_link(nc.gpsimd.tensor_scalar(ve[:], mv[:, :, 1], eps, None, ALU.add))
            nc.gpsimd.tensor_tensor(rstd[:], ve[:], minus_half[:, 0:NT], ALU.pow).then_inc(s["ln_rstd"], 1)

        def pool_m_split(pool, p, u):
            g = nc.gpsimd
            pool.wait_ge(s["f_free"], p * 32 + 8 * u + 10)
            neg, r1, r2 = msp[:, u, 0, :], msp[:, u, 1, :], msp[:, u, 2, :]
            one = sign[:, 1, 0:KT]
            steps = ((neg, M[:, u, :], sign[:, 0, 0:KT], ALU.mult),
                     (mpart[:, u, 0, :], neg, one, ALU.mult),
                     (r1, neg, mpart[:, u, 0, :], ALU.subtract),
                     (mpart[:, u, 1, :], r1, one, ALU.mult),
                     (r2, r1, mpart[:, u, 1, :], ALU.subtract),
                     (mpart[:, u, 2, :], r2, one, ALU.mult))
            for k, args in enumerate(steps):
                if k:
                    pool.wait_ge(s["m_split"], p * 12 + u * 6 + k)
                g.tensor_tensor(*args).then_inc(s["m_split"], 1)

        def pool_pair(pool, p, last):
            pool.wait_ge(s["pv_done"], p * 16 + 16)
            for u in range(2):
                nc.gpsimd.tensor_tensor(VU[:, u, :, 0:D0],
                                        Vc[:, bass.ds(p * (2 * KT * D0) + u * KT * D0, KT * D0)].rearrange("p (k d) -> p k d", d=D0),
                                        sign[:, 1, :].rearrange("p (k d) -> p k d", d=D0), ALU.mult)\
                    .then_inc(s["v_copied"], 1)
            if not last:
                for u in range(2):
                    pool_m_split(pool, p + 1, u)

        def pool_layer1(pool):
            g = nc.gpsimd
            pool_rstd(pool, 3, 1e-5)
            pool_rstd(pool, 4, 1e-10)
            pool.wait_ge(s["wt1_ready"], 1)
            pool_link(g.memset(VU[:], 0.0))
            pool_link(g.memset(VU[:, :, :, D1:D1 + 1], 1.0))
            pool_link(g.memset(KS[32:64, :, :], 1.0))
            pool_link(g.memset(KM[32:64, :, :], 1.0))
            g.sem_inc(s["vu1_cleared"], 1)
            pool.wait_ge(s["v1_done"], 4)
            pool_vu1(pool, 0, 0)
            pool.wait_ge(s["xsrc_ready"], 2)
            for t in range(NT):
                for k in range(TOP1):
                    g.indirect_dma_start(xs1, bass.IndirectOffsetOnAxis(ap=pos_i[:, k, t:t + 1], axis=0), xn[:, t, :], None)\
                        .then_inc(s["scattered1"], 16)
            for n in range(2):
                pool_m1_split(pool, n, n)
            with pool.Fori(0, UNITS1 // 4 - 1) as g4:
                for w in range(4):
                    pool_unit1(pool, g4, w, False)
            for w in range(4):
                pool_unit1(pool, UNITS1 // 4 - 1, w, True)
            pool.wait_ge(s["scattered1"], 16 * TOP1 * NT)
            g.tensor_tensor(xn[:], xn[:], bproj_b.unsqueeze(1).to_broadcast([P, NT, C]), ALU.add).then_inc(s["bproj_added"], 1)
            pool_rstd(pool, 5, 1e-10)
            for i in range(2):
                pool.wait_ge(s[f"y1_stored{i}"], 8 * NB1 + 16)
            pool.wait_ge(s["mlp_ready"], 4)
            for t in range(NT):
                for k in range(TOP1):
                    g.indirect_dma_start(yg1[:, k, t, :], None, ys1, bass.IndirectOffsetOnAxis(ap=pos_i[:, k, t:t + 1], axis=0))\
                        .then_inc(s["gathered1"], 16)

        def pool_vu1(pool, unit, u):
            nc.gpsimd.tensor_tensor(VU[:, u, :, 0:D1], Vc[:, bass.ds(unit * (KT * D1), KT * D1)].rearrange("p (k d) -> p k d", d=D1),
                                    sign[:, 1, 0:KT * D1].rearrange("p (k d) -> p k d", d=D1), ALU.mult).then_inc(s["v1_copied"], 1)

        def pool_m1_split(pool, unit, u):
            g = nc.gpsimd
            u = u % 2
            pool.wait_ge(s["max1_whole"], unit + 1)
            neg, r1, r2, one = msp[:, u, 0, :], msp[:, u, 1, :], msp[:, u, 2, :], sign[:, 1, 0:KT]
            steps = ((neg, M[:, u, :], sign[:, 0, 0:KT], ALU.mult),
                     (mpart[:, u, 0, :], neg, one, ALU.mult),
                     (r1, neg, mpart[:, u, 0, :], ALU.subtract),
                     (mpart[:, u, 1, :], r1, one, ALU.mult),
                     (r2, r1, mpart[:, u, 1, :], ALU.subtract),
                     (mpart[:, u, 2, :], r2, one, ALU.mult))
            for k, args in enumerate(steps):
                if k:
                    pool.wait_ge(s["m1_split"], unit * 6 + k)
                g.tensor_tensor(*args).then_inc(s["m1_split"], 1)

        def pool_unit1(pool, g4, w, last):
            if not (last and w == 3):
                pool.wait_ge(s["pv1_done"], g4 * 32 + w * 8 + 8)
                pool_vu1(pool, g4 * 4 + w + 1, (w + 1) % 2)
            if not (last and w >= 2):
                pool_m1_split(pool, g4 * 4 + w + 2, w)

        @block.gpsimd
        def _(pool):
            g = nc.gpsimd
            pool_link(g.memset(bd[:], 0.0))
            g.memset(zeros, 0.0).then_inc(s["const"], 1)
            pool.wait_ge(s["const"], 1)
            for t, value in ((ident, 0.0), (identb, 0.0), (onesb, 1.0), (ones_e, 1.0), (ones_row, 1.0), (minus_half, -0.5),
                             (half_pi, math.pi / 2), (scan_keep, 1.0), (VU, 0.0), (lowb, 1.0), (scan_keep[:, :, 0:1], 0.0),
                             (VU[:, :, :, D0:D0 + 1], 1.0), (sign, 1.0), (sign[:, 0:1, :], -1.0), (KS[96:P, :, :], 1.0)):
                pool_link(g.memset(t[:], value))
            for t, side in ((below, -1), (above, 1)):
                pool_link(g.memset(t[:], 0.0))
                pool_link(g.affine_select(out=t[:], in_=t[:], compare_op=ALU.is_ge, fill=NEG, base=0,
                                          pattern=[[side, P]], channel_multiplier=-side))
            for t in (ident, identb):
                pool_link(g.affine_select(out=t[:], in_=t[:], compare_op=ALU.not_equal, fill=1.0, base=0,
                                          pattern=[[-1, P]], channel_multiplier=1))
            pool_link(g.affine_select(out=lowb[:], in_=lowb[:], compare_op=ALU.is_gt, fill=0.0, base=0,
                                      pattern=[[1, P]], channel_multiplier=-1))
            pool_link(g.iota(iota_e[:], [[1, E0]], base=0, channel_multiplier=0, allow_small_or_imprecise_dtypes=True))
            g.iota(iota_b[:], [[1, NB1]], base=0, channel_multiplier=0, allow_small_or_imprecise_dtypes=True).then_inc(s["const"], 1)
            pool.wait_ge(s["const"], 2)
            pool_rstd(pool, 0, 1e-5)
            for r in range(4):
                pool.wait_ge(s["ss_ready"], r + 1)
                g.tensor_tensor(inv[:, r, :], ss[:, r, :], minus_half[:, 0:64], ALU.pow).then_inc(s["inv_ready"], 1)
            pool.wait_ge(s["zeroed"], 16 * (NB0 // 8 + NB1 // 8))
            pool.wait_ge(s["xsrc_ready"], 1)
            for t in range(NT):
                g.indirect_dma_start(xs0, bass.IndirectOffsetOnAxis(ap=pos_i[:, 0, t:t + 1], axis=0), x_in[:, t, :], None)\
                    .then_inc(s["scattered"], 16)
            for u in range(2):
                pool_m_split(pool, 0, u)
            with pool.Fori(0, PAIRS0 - 1) as p:
                pool_pair(pool, p, False)
            pool_pair(pool, PAIRS0 - 1, True)
            for i in range(2):
                pool.wait_ge(s[f"y_stored{i}"], 8 * NBP * PAIRS0 + 16)
            pool.wait_ge(s["pv_done"], 16 * PAIRS0 + 16)
            for t in range(NT):
                g.indirect_dma_start(yg[:, t, :], None, ys0, bass.IndirectOffsetOnAxis(ap=pos_i[:, 0, t:t + 1], axis=0))\
                    .then_inc(s["gathered"], 16)
            pool.wait_ge(s["post_loaded"], 16 * 14)
            g.tensor_tensor(x1p, xn[:], bo_b.unsqueeze(1).to_broadcast([P, NT, C]), ALU.add).then_inc(s["bo_added"], 1)
            pool.wait_ge(s["prep_done"], 3)
            for base, mul, step in ((0, 1, -NQ), (NQ - 1, -1, NQ)):
                pool_link(g.affine_select(out=bdq, in_=bdq, compare_op=ALU.is_ge, fill=0.0, base=base,
                                          pattern=[[step, NT], [0, C]], channel_multiplier=mul))
            g.sem_inc(s["bd_masked"], 1)
            pool_rstd(pool, 1, 1e-5)
            pool.wait_ge(s["gathered"], 16 * NT)
            pool.wait_ge(s["xsum"], 64)
            pool_link(g.tensor_tensor(yg, yg, ysh, ALU.add))
            g.tensor_tensor(xr, xr, yg, ALU.add).then_inc(s["xsum"], 1)
            pool_rstd(pool, 2, 1e-5)
            pool_layer1(pool)

        mm, tr = nc.tensor.matmul, nc.tensor.transpose

        def pe_transposes(pe, src, n):
            for c in range(4):
                pe.wait_ge(s["ln_done"], n + 1)
                for k in range(4):
                    last = tr(bank(c)[:, k * P:(k + 1) * P], src[:, 4 * c + k, :], ident[:])
                last.then_inc(s["tr_ready"], 1)

        def pe_project(pe, r):
            if r >= 2:
                pe.wait_ge(s["qf_ready"], r - 1)
            for half in range(2):
                col = (r // 2) * S + half * 512
                last = mm(bank(4 + 2 * (r % 2) + half), wqkv[:, r % 2, :], xT[:, col:col + 512], start=True, stop=True)
            last.then_inc(s["proj_ready"], 1)

        def pe_rank(pe, n, E):
            pe.wait_ge(s["oh_ready"], n + 1)
            mm(bank(1)[:, 0:NT * E], lowb[:], oh_b[:, 0:NT * E], start=True, stop=True)
            mm(bank(1)[:, NT * E:2 * NT * E], onesb[:], oh_b[:, 0:NT * E], start=True, stop=True).then_inc(s["rank_ready"], 1)

        def pe_max(pe, p, n):
            u, i = n // 8, n % 8
            pe.wait_ge(s["f_free"], p * 32 + n + 1)
            for half in range(2):
                last = mm(bank(FB[n % 2] + half), QM[0:R0, u, i * P:(i + 1) * P],
                          KM[0:R0, u, half * 512:(half + 1) * 512], start=True, stop=True)
            last.then_inc(s["f_ready"], 1)

        def pe_mt(pe, p, u):
            pe.wait_ge(s["m_split"], p * 12 + u * 6 + 6)
            tr(bank(7 - u).bitcast(BF16)[0:PARTS * KT, 0:P],
               mpart[:, u, :, :].rearrange("p j i -> p (j i)"), identb[:]).then_inc(s["mt_ready"], 1)

        def pe_fid(pe, p, n):
            u, k = n // 8, n % 8
            pe.wait_ge(s["f_free"], p * 32 + n + 17)
            for half in range(2):
                last = mm(bank(FB[n % 2] + half), FK[0:RF, u, k * P:(k + 1) * P], FQ[0:RF, u, half * 512:(half + 1) * 512],
                          start=True, stop=True)
            last.then_inc(s["f_ready"], 1)

        def pe_guard(pe, p, n):
            u, k = n // 8, n % 8
            if k == 0:
                pe.wait_ge(s["n_loaded"], p * 64 + u * 32 + 32)
            pe.wait_ge(s["z_done"], p * 16 + max(n, 1))
            for half in range(2):
                last = mm(bank(2 + half), FKf[NROW:NROW + 1, k * P:(k + 1) * P], FQf[NROW:NROW + 1, half * 512:(half + 1) * 512],
                          start=True, stop=True)
            last.then_inc(s["g_ready"], 1)
            pe.wait_ge(s["g_done"], p * 16 + n + 1)

        def pe_phase_a(pe, p, guard):
            expert = {}
            pe_fid(pe, p, 0)
            if guard:
                pe_guard(pe, p, 0)
            for n in range(16):
                u, k = n // 8, n % 8
                if n < 15:
                    pe_fid(pe, p, n + 1)
                    if guard:
                        pe_guard(pe, p, n + 1)
                if k == 0:
                    pe.wait_ge(s["m_loaded"], p * 32 + 16 * u + 16)
                pe.wait_ge(s["z_done"], p * 16 + n + 1)
                for half in range(2):
                    last = mm(bank(2 + half), KS[0:R0 + PARTS, u, k * P:(k + 1) * P],
                              QS[0:R0 + PARTS, u, half * 512:(half + 1) * 512], start=True, stop=True)
                last.then_inc(s["c_ready"], 1)
                if n == 0:
                    pe.wait_ge(s["pv_evac"], p * 2 + 1)
                    pe_mt(pe, p, 1)
                pe_block(pe, p, n, expert)

        def pe_pair(pe, p, flag, last_pair):
            pe.wait_ge(s["main_loaded"], p * 64 + 64)
            with pe.If(flag > 0):
                pe_phase_a(pe, p, True)
            with pe.Else():
                pe_phase_a(pe, p, False)
            for u in range(2):
                pe.wait_ge(s["v_copied"], p * 2 + u + 1)
            pe.wait_ge(s["yb_ready"], p * NBP + NBP)
            for n in range(16):
                if not last_pair:
                    pe_max(pe, p + 1, n)
                u, k = n // 8, n % 8
                pe.wait_ge(s["exp_done"], p * 16 + n + 1)
                if k == 0:
                    pe.wait_ge(s["pv_evac"], p * 2 + u + 1)
                for j in range(4):
                    last = mm(bank(6)[32 * j:32 * j + 32, 0:256], VU[:, u, k, :], Zt(u, k)[:, 256 * j:256 * (j + 1)],
                              start=(k == 0), stop=(k == KT - 1), tile_position=(0, 32 * j))
                last.then_inc(s["pv_done"], 1)
                if n == 11 and not last_pair:
                    pe_mt(pe, p + 1, 0)

        def pe_block(pe, p, n, expert):
            i = (n - 3) // 2
            if n % 2 == 1 and 0 <= i < NBP:
                pe.wait_ge(s["hT_done"], p * NBP + i + 1)
                pe.wait_ge(s["xbT_ready"], p * NBP + min(i + 2, NBP))
                if i >= 1:
                    pe.wait_ge(s["yb_ready"], p * NBP + i)
                for t in range(2):
                    w = dn_w[:, bass.ds(expert[i] * (2 * C) + t * C, C)] if i < XB else dnT[:, t, :]
                    last = mm(bank(7)[:, 256:256 + C], hT[:, i % 2, t * P:(t + 1) * P], w, start=(t == 0), stop=(t == 1))
                last.then_inc(s["out_ready"], 1)
            i = (n - 2) // 2
            if n % 2 == 0 and 0 <= i < NBP:
                pe.wait_ge(s["h_ready"], p * NBP + i + 1)
                for t in range(2):
                    last = tr(bank(6)[:, t * P:(t + 1) * P], hb[:, i % 2, t * P:(t + 1) * P], ident[:])
                last.then_inc(s["ht_ready"], 1)
            i = n // 2
            if n % 2 == 0 and i < XB:
                pe.wait_ge(s[f"xb_loaded{i % 2}"], p * (8 * XB) + 16 * (i // 2) + 16)
                if i == 0:
                    pe.wait_ge(s["mt_copied"], p * 2 + 1)
                else:
                    pe.wait_ge(s["xbT_ready"], p * NBP + i)
                if i >= 2:
                    pe.wait_ge(s["yb_ready"], p * NBP + i - 1)
                tr(bank(7)[:, 0:P], xb[:, i % 2, :], ident[:]).then_inc(s["xt_ready"], 1)
            i = (n - 1) // 2
            if n % 2 == 1 and i < NBP:
                pe.wait_ge(s["xbT_ready"], p * NBP + i + 1)
                if i == 0:
                    pe.wait_ge(s["mt_copied"], p * 2 + 2)
                else:
                    pe.wait_ge(s["hT_done"], p * NBP + i)
                if i < XB:
                    expert[i] = pe.value_load(eb_i[0:1, bass.ds(p * XB + i, 1)], min_val=0, max_val=E0 - 1)
                    w = gu_w[:, bass.ds(expert[i] * (2 * F0), 2 * F0)]
                else:
                    w = guT[:]
                mm(bank(6), xbT[:, i % 2, :], w, start=True, stop=True).then_inc(s["gu_ready"], 1)

        def pe_post0(pe):
            pe.wait_ge(s["post_loaded"], 16 * 14)
            pe.wait_ge(s["prep_done"], 1)
            pe.wait_ge(s["pv_evac"], 2 * PAIRS0 + 1)
            for c in range(4):
                tr(bank(4)[:, c * P:(c + 1) * P], w1r[:, c * P:(c + 1) * P], ident[:])
            for c in range(4):
                mm(bank(5)[:, c * P:(c + 1) * P], wqo8[:, c * P:(c + 1) * P], rep8, start=True, stop=True)
            for c in range(8):
                last = mm(bank(6 + c // 4)[:, (c % 4) * P:(c % 4 + 1) * P], brow[:, c * P:(c + 1) * P], ones_row[:], start=True, stop=True)
            last.then_inc(s["prep_ready"], 1)
            for n in range(8):
                b, hf, hg = n // 4, (n // 2) % 2, n % 2
                if n >= 4:
                    pe.wait_ge(s["o_done"], n - 3)
                for h in range(4):
                    last = tr(bank(n % 4)[:, h * P:(h + 1) * P], OT[:, b * H0 + hg * 4 + h, hf * P:(hf + 1) * P], ident[:])
                last.then_inc(s["o_ready"], 1)
            pe.wait_ge(s["prep_done"], 2)
            for c in range(4):
                mm(bank(6)[:, 0:NQ], w1T[:, c * P:(c + 1) * P], wm[:, c, :], start=(c == 0), stop=(c == 3))
            for c in range(4):
                mm(bank(6)[:, 8:8 + NQ], repcol[:, c * P:(c + 1) * P], wm[:, c, :], start=(c == 0), stop=(c == 3))
            for c in range(4):
                mm(bank(7)[:, 0:P], qoT[:, c * P:(c + 1) * P], w2r[:, c, :], start=(c == 0), stop=(c == 3))
            for c in range(4):
                last = mm(bank(7)[:, P:2 * P], repcol[:, 512 + c * P:512 + (c + 1) * P], w2r[:, c, :], start=(c == 0), stop=(c == 3))
            last.then_inc(s["prep_ready"], 1)
            pe.wait_ge(s["o_done"], 8)
            pe_transposes(pe, attn, 0)
            for c in range(4):
                pe.wait_ge(s["tr_done"], 4 + 4)
                for k in range(4):
                    last = mm(bank(c)[:, k * P:(k + 1) * P], attnT[:, (4 * c + k) * P:(4 * c + k + 1) * P], wo, start=True, stop=True)
                last.then_inc(s["wo_ready"], 1)
            pe.wait_ge(s["wo_done"], 4)
            pe_transposes(pe, x1, 1)
            pe.wait_ge(s["tr_done"], 12)
            pe.wait_ge(s["prep_done"], 3)
            for t in range(NT):
                last = mm(bank(4)[:, t * NQ:(t + 1) * NQ], attnT[:, t * P:(t + 1) * P], w1m, start=True, stop=True)
            last.then_inc(s["qm_ready"], 1)
            pe.wait_ge(s["qe_ready"], 1)
            tr(bank(5)[:, 0:P], qe, ident[:]).then_inc(s["qeT_ready"], 1)
            pe.wait_ge(s["qeT_done"], 1)
            pe.wait_ge(s["bd_masked"], 1)
            for c in range(4):
                mm(bank(c), qeT, bdq[:, 4 * c:4 * c + 4, :].rearrange("p t c -> p (t c)"), start=True, stop=True).then_inc(s["ff_ready"], 1)

        def pe_layer1(pe):
            pe.wait_ge(s["l1_loaded"], 16 * L1_LOADS)
            pe.wait_ge(s["res0_ready"], 1)
            for i in range(12):
                tr(bank(4 + i // 4)[:, (i % 4) * P:(i % 4 + 1) * P], W1[:, i * P:(i + 1) * P], ident[:])
            for i in range(6):
                last = mm(bank(7)[:, i:i + 1], brow1[:, i * P:(i + 1) * P], ones_row[:, 0:1], start=True, stop=True)
            last.then_inc(s["wt1_ready"], 1)
            pe_transposes(pe, xn[:], 3)
            pe.wait_ge(s["tr_done"], 16)
            pe_transposes(pe, lx, 4)
            pe.wait_ge(s["tr_done"], 20)
            pe.wait_ge(s["wt1_done"], 1)
            for c in range(4):
                for k in range(4):
                    last = mm(bank(c)[:, k * P:(k + 1) * P], lxT[:, (4 * c + k) * P:(4 * c + k + 1) * P], wqkv[:, 2, :], start=True, stop=True)
                last.then_inc(s["v1_ready"], 1)
            pe_project1(pe, 0)
            pe_project1(pe, 1)
            pe.wait_ge(s["v1_done"], 1)
            for t in range(NT):
                last = mm(bank(0)[:, t * E1:(t + 1) * E1], xT[:, t * P:(t + 1) * P], rw1, start=True, stop=True)
            last.then_inc(s["lg1_ready"], 1)
            pe_project1(pe, 2)
            pe_project1(pe, 3)
            pe.wait_ge(s["v1_done"], 4)
            pe_rank(pe, 1, E1)
            pe.wait_ge(s["pos_ready"], 2)
            pe.wait_ge(s["qf_ready"], 8)
            for c in range(12):
                pe_max1(pe, 0, 0, c, 32)
            pe_mt1(pe, 0, 0)
            pe.wait_ge(s["mt1_copied"], 1)
            for c in range(12):
                pe_max1(pe, 1, 1, c, 32)
            with pe.Fori(0, UNITS1 // 4 - 1) as g4:
                for w in range(4):
                    pe_unit1(pe, g4, w, False)
            for w in range(4):
                pe_unit1(pe, UNITS1 // 4 - 1, w, True)
            pe.wait_ge(s["bias1_loaded"], 32)
            pe.wait_ge(s["head1_out"], UNITS1 + 1)
            pe.wait_ge(s["x1b_loaded0"], 16)
            tr(bank(4)[:, 0:P], xb[:, 0, :], ident[:]).then_inc(s["x1t_ready"], 1)
            pe_step1(pe, 0, 0, hid=False, res=False)
            pe_step1(pe, 0, 1, res=False)
            with pe.Fori(0, NB1 // 2 - 2) as h:
                for i in range(2):
                    pe_step1(pe, h, i + 2)
            for i in range(4):
                pe_step1(pe, NB1 // 2 - 2, i + 2, gu=i < 2, hid=i < 3, nxt=i < 1)
            pe.wait_ge(s["y1_ready"], NB1)
            for n in range(16):
                b, hf, hg = n // 8, (n // 4) % 2, n % 4
                if n >= 4:
                    pe.wait_ge(s["o1n_done"], n - 3)
                for h in range(4):
                    last = tr(bank(n % 4)[:, h * P:(h + 1) * P], OT1[:, b * H1 + hg * 4 + h, hf * P:(hf + 1) * P], ident[:])
                last.then_inc(s["o1t_ready"], 1)
            pe.wait_ge(s["o1n_done"], 16)
            pe_transposes(pe, attn, 4)
            for c in range(4):
                pe.wait_ge(s["tr_done"], 24)
                for k in range(4):
                    last = mm(bank(c)[:, k * P:(k + 1) * P], attnT[:, (4 * c + k) * P:(4 * c + k + 1) * P], wprojT, start=True, stop=True)
                last.then_inc(s["proj1_ready"], 1)
            pe_transposes(pe, lx2, 5)
            pe.wait_ge(s["tr_done"], 28)
            for n in range(16):
                f, c = n % 4, n // 4
                if n >= 4:
                    pe.wait_ge(s["fc_done"], n - 3)
                mm(bank(4 + n % 4), wfcT[:, f * P:(f + 1) * P], attnT[:, c * 512:(c + 1) * 512], start=True, stop=True).then_inc(s["fc_ready"], 1)
            for c in range(4):
                pe.wait_ge(s["fc_done"], 4 * c + 4)
                for k in range(4):
                    t = 4 * c + k
                    for f in range(4):
                        last = mm(bank(c)[:, k * P:(k + 1) * P], HT[:, f, t * P:(t + 1) * P], wmlpT[:, f * P:(f + 1) * P], start=(f == 0), stop=(f == 3))
                last.then_inc(s["mlp_ready"], 1)

        def pe_project1(pe, r):
            if r >= 2:
                pe.wait_ge(s["qf_ready"], 4 + r - 1)
            for half in range(2):
                col = (r // 2) * S + half * 512
                last = mm(bank(4 + 2 * (r % 2) + half), wqkv[:, r % 2, :], lxT[:, col:col + 512], start=True, stop=True)
            last.then_inc(s["proj_ready"], 1)

        def pe_max1(pe, unit, slot, c, loads):
            q, k, u = slots[slot]
            if c == 0:
                pe.wait_ge(s[f"slot_loaded{slot}"], loads)
            i, half = (c, 0) if c < 4 else (4 + (c - 4) // 2, (c - 4) % 2)
            lo, hi = 512 * half, min(512 * half + 512, (i + 1) * P)
            o = bank(MB[c % 3])
            diagonal = hi == (i + 1) * P
            pe.wait_ge(s["max1_free"], unit * 12 + c + 1)
            last = mm(o[:, 0:hi - lo], q[0:R1, u, i * P:(i + 1) * P], k[0:R1, u, lo:hi], start=True, stop=not diagonal)
            if diagonal:
                last = mm(o[:, hi - lo - P:hi - lo], identb[:], below[:], start=False, stop=True)
            last.then_inc(s["max1_ready"], 1)

        def pe_mt1(pe, unit, slot):
            pe.wait_ge(s["m1_split"], unit * 6 + 6)
            tr(bank(0).bitcast(BF16)[0:PARTS * KT, 0:P],
               mpart[:, slot % 2, :, :].rearrange("p j i -> p (j i)"), identb[:]).then_inc(s["mt1_ready"], 1)

        def pe_pv1(pe, unit, slot, k):
            pe.wait_ge(s["p1_done"], unit * 8 + k + 3)
            if k == 0:
                pe.wait_ge(s["v1_copied"], unit + 1)
                pe.wait_ge(s["head1_out"], unit + 1)
            for j in range(k // 2, 4):
                lo = max(256 * j, P * k)
                last = mm(bank(6)[32 * j:32 * j + 32, lo - 256 * j:256], VU[:, slot % 2, k, :], Z[:, k * S + lo:k * S + 256 * (j + 1)],
                          start=(k == 0), stop=(k == 2 * j + 1), tile_position=(0, 32 * j))
            last.then_inc(s["pv1_done"], 1)

        def pe_unit1(pe, g4, w, last_group):
            unit = g4 * 4 + w
            q, kk, u = slots[w]
            maxima = not (last_group and w >= 2)
            c = 0
            pe.wait_ge(s["m1_loaded"], unit * 16 + 16)
            for k in range(KT):
                if k == 1 and not (last_group and w == 3):
                    pe.wait_ge(s["max1_free"], (unit + 2) * 12 + 4 if maxima else UNITS1 * 12 + 3)
                    pe_mt1(pe, unit + 1, w + 1)
                if maxima:
                    if k == 3:
                        pe.wait_ge(s["mt1_copied"], unit + 2)
                    for _ in range(1 if k < 4 else 2):
                        pe_max1(pe, unit + 2, (w + 2) % 4, c, g4 * 32 + (w + 2) // 4 * 32 + 32)
                        c += 1
                b0 = 2 + 2 * (k % 2)
                pe.wait_ge(s["p1_done"], unit * 8 + k + 1)
                for lo, hi in ((P * k, 512), (max(P * k, 512), S)):
                    if lo < hi:
                        last = mm(bank(b0, 2)[:, lo:hi], kk[0:R1 + PARTS, u, k * P:(k + 1) * P], q[0:R1 + PARTS, u, lo:hi],
                                  start=True, stop=lo != P * k)
                        if lo == P * k:
                            last = mm(bank(b0, 2)[:, lo:lo + P], identb[:], above[:], start=False, stop=True)
                last.then_inc(s["c1_ready"], 1)
                if k >= 1:
                    pe_pv1(pe, unit, w, k - 1)
            pe_pv1(pe, unit, w, KT - 1)

        def pe_step1(pe, h, i, gu=True, hid=True, nxt=True, res=True):
            if gu:
                pe.wait_ge(s["x1t_done"], h * 2 + i + 1)
                expert = pe.value_load(eb_i[0:1, bass.ds(h * 2 + i, 1)], min_val=0, max_val=E1 - 1)
                mm(bank(i % 2), xbT[:, i % 2, :], w1_all[:, bass.ds(expert * F1, F1)], start=True, stop=False)
                mm(bank(i % 2), ones_row[:], b1_row[:, bass.ds(expert * F1, F1)], start=False, stop=True).then_inc(s["gu1_ready"], 1)
            if hid:
                pe.wait_ge(s["h1_ready"], h * 2 + i)
                for t in range(4):
                    last = tr(bank(2 + (i + 1) % 2)[:, t * P:(t + 1) * P], hb1[:, (i + 1) % 2, t * P:(t + 1) * P], ident[:])
                last.then_inc(s["h1t_ready"], 1)
            if nxt:
                pe.wait_ge(s[f"x1b_loaded{(i + 1) % 2}"], h * 16 + 16 * ((i + 1) // 2) + 16)
                tr(bank(4)[:, 0:P], xb[:, (i + 1) % 2, :], ident[:]).then_inc(s["x1t_ready"], 1)
            if res:
                pe.wait_ge(s["h1t_done"], h * 2 + i - 1)
                expert = pe.value_load(eb_i[0:1, bass.ds(h * 2 + i - 2, 1)], min_val=0, max_val=E1 - 1)
                for t in range(4):
                    mm(bank(5 + i % 2)[:, 0:C], hT1[:, i % 2, t * P:(t + 1) * P], w2_all[:, bass.ds(expert * F1 + t * C, C)], start=(t == 0), stop=False)
                mm(bank(5 + i % 2)[:, 0:C], ones_row[:], b2_row[:, bass.ds(expert * C, C)], start=False, stop=True).then_inc(s["o1_ready"], 1)

        @block.tensor
        def _(pe):
            pe.wait_ge(s["const"], 2)
            pe.wait_ge(s["w_raw0"], 16 * 4)
            for i in range(4):
                tr(bank(4)[:, i * P:(i + 1) * P], wst[:, i * P:(i + 1) * P], ident[:])
            for i in range(2):
                tr(bank(5)[:, i * P:(i + 1) * P], wst[:, 512 + i * P:512 + (i + 1) * P], ident[:])
            pe.wait_ge(s["w_small0"], 16 * 12)
            for i in range(2):
                mm(bank(5)[:, 272 + i:273 + i], bqk_row[:, i * P:(i + 1) * P], ones_row[:, 0:1], start=True, stop=True)
            tr(bank(5)[:, 256:256 + E0], wst[0:E0, 768:768 + P], ident[0:E0, 0:E0]).then_inc(s["wt_ready"], 1)
            pe_transposes(pe, xn[:], 0)
            pe.wait_ge(s["wqkv_loaded"], 48)
            pe.wait_ge(s["tr_done"], 4)
            for c in range(4):
                for k in range(4):
                    last = mm(bank(c)[:, k * P:(k + 1) * P], xT[:, (4 * c + k) * P:(4 * c + k + 1) * P], wqkv[:, 2, :], start=True, stop=True)
                last.then_inc(s["v_ready"], 1)
            pe.wait_ge(s["wt_done"], 1)
            pe_project(pe, 0)
            pe_project(pe, 1)
            pe.wait_ge(s["v_done"], 1)
            for t in range(NT):
                last = mm(bank(0)[:, t * E0:(t + 1) * E0], xT[:, t * P:(t + 1) * P], rout[:], start=True, stop=True)
            last.then_inc(s["lg_ready"], 1)
            pe_project(pe, 2)
            pe_project(pe, 3)
            pe.wait_ge(s["w_small0"], 16 * 12)
            pe.wait_ge(s["v_done"], 4)
            pe_rank(pe, 0, E0)
            for r in range(4):
                if r >= 2:
                    pe.wait_ge(s["ss_ready"], r - 1)
                for k in range(KT):
                    last = mm(bank(2 + r % 2)[:, k * 64:(k + 1) * 64], qf[r][:, k * P:(k + 1) * P], bd[:], start=True, stop=True)
                last.then_inc(s["qq_ready"], 1)
            for r in range(4):
                pe.wait_ge(s["qh_ready"], r + 1)
                if r < 2:
                    pe.wait_ge(s["qf_ready"], r + 3)
                else:
                    pe.wait_ge(s["hatT_ready"], r - 1)
                for k in range(KT):
                    last = tr(bank(4 + 2 * (r % 2), 2)[0:64, k * P:(k + 1) * P], qq[r][:, k * 64:(k + 1) * 64], ident[:])
                last.then_inc(s["hat_ready"], 1)
            pe.wait_ge(s["nrm_ready"], 1)
            for r in range(4):
                tr(bank(2)[0:64, r * P:(r + 1) * P], nrm[:, r * 64:(r + 1) * 64], ident[:])
            mm(bank(3)[0:1, 0:1], small[:, 0:1], ones_e[:, 0:1], start=True, stop=True).then_inc(s["nt_ready"], 1)
            pe.wait_ge(s["max_loaded"], 32)
            pe.wait_ge(s["pos_ready"], 1)
            pe.wait_ge(s["hatT_ready"], 4)
            for n in range(16):
                pe_max(pe, 0, n)
            pe_mt(pe, 0, 0)
            pe.wait_ge(s["gu_loaded"], 16)
            pe.wait_ge(s["dn_loaded"], 64)
            pe.wait_ge(s["flag_ready"], 1)
            flag = pe.value_load(flag_i[0:1, 0:1], min_val=0, max_val=1)
            with pe.Fori(0, PAIRS0 - 1) as p:
                pe_pair(pe, p, flag, False)
            pe_pair(pe, PAIRS0 - 1, flag, True)
            pe_post0(pe)
            pe_layer1(pe)


        def act(out_, in_, f=ACT.Copy, **kw):
            return nc.scalar.activation(out_, in_, f, **kw)

        def act_transposed(ac, dst, n):
            for c in range(4):
                ac.wait_ge(s["tr_ready"], 4 * n + c + 1)
                act(dst[:, c * 512:(c + 1) * 512], bank(c)).then_inc(s["tr_done"], 1)

        def act_sin(ac, p, n, guard):
            ac.wait_ge(s["f_ready"], p * 32 + n + 17)
            if guard:
                ac.wait_ge(s["g_done"], p * 16 + n + 1)
            act(snb[:, n % 2, :], bank(FB[n % 2], 2), ACT.Sin, scale=PI_IN).then_inc(s["sin_done"], 1)

        def act_phase_a(ac, p, guard):
            act_sin(ac, p, 0, guard)
            for n in range(16):
                if n < 15:
                    act_sin(ac, p, n + 1, guard)
                act_block(ac, p, n)

        def act_pair(ac, p, flag):
            with ac.If(flag > 0):
                act_phase_a(ac, p, True)
            with ac.Else():
                act_phase_a(ac, p, False)
            for n in range(16):
                u, k = n // 8, n % 8
                ac.wait_ge(s["z_done"], p * 16 + n + 2)
                act(Zt(u, k), Zt(u, k), ACT.Exp, scale=0.05).then_inc(s["exp_done"], 1)
                if n == 11:
                    act_head_out(ac, p, 0)
            act_head_out(ac, p, 1)

        def act_head_out(ac, p, u):
            ac.wait_ge(s["pv_done"], p * 16 + 8 * u + 24)
            act(OT[:, bass.ds(p * 2 + u, 1), :], bank(6)[:, 0:256].unsqueeze(1)).then_inc(s["pv_evac"], 1)

        def act_block(ac, p, n):
            i = (n - 3) // 2
            if n % 2 == 1 and 0 <= i < NBP:
                ac.wait_ge(s["out_ready"], p * NBP + i + 1)
                ac.wait_ge(s[f"y_stored{i % 2}"], p * (8 * NBP) + 16 * (i // 2) + 16)
                act(yb[:, i % 2, :], bank(7)[:, 256:256 + C]).then_inc(s["yb_ready"], 1)
            i = (n - 2) // 2
            if n % 2 == 0 and 0 <= i < NBP:
                ac.wait_ge(s["ht_ready"], p * NBP + i + 1)
                act(hT[:, i % 2, :], bank(6)[:, 0:F0]).then_inc(s["hT_done"], 1)
            i = n // 2
            if n % 2 == 0 and i < NBP:
                if i < XB:
                    ac.wait_ge(s["xt_ready"], p * XB + i + 3)
                    src = bank(7)[:, 0:P]
                else:
                    src = xT[:, bass.ds(p * (SHB * P) + (i - XB) * P, P)]
                    ac.wait_ge(s["gu_ready"], p * NBP + i - 1)
                act(xbT[:, i % 2, :], src).then_inc(s["xbT_ready"], 1)
            i = (n - 1) // 2
            if n % 2 == 1 and i < NBP:
                ac.wait_ge(s["gu_ready"], p * NBP + i + 1)
                act(sg[:], bank(6)[:, 0:F0], ACT.Silu).then_inc(s["silu_done"], 1)

        def act_layer1(ac):
            ac.wait_ge(s["wt1_ready"], 1)
            act(wqkv[:, :, :].rearrange("p i c -> p (i c)"), bank(4)[:, 0:384])
            act(wprojT, bank(4)[:, 384:512])
            act(wfcT, bank(5))
            act(wmlpT, bank(6))
            act(bcols, bank(7)[:, 0:6]).then_inc(s["wt1_done"], 1)
            act_transposed(ac, xT, 3)
            act_transposed(ac, lxT, 4)
            ac.wait_ge(s["x1_stored"], 16)
            ac.wait_ge(s["wt1_done"], 1)
            for r in range(4):
                ac.wait_ge(s["proj_ready"], 4 + r + 1)
                act(qf[r], bank(4 + 2 * (r % 2), 2), ACT.Identity, bias=bcols[:, r % 2:r % 2 + 1]).then_inc(s["qf_ready"], 1)
                ac.wait_ge(s["qf_ready"], 4 + r + 1)
                act(part[r][:, 0, :], qf[r]).then_inc(s["p1_ready"], 1)
                ac.wait_ge(s["res_ready"], 8 + r + 1)
                act(part[r][:, 1, :], res[r]).then_inc(s["p2_ready"], 1)
            ac.wait_ge(s["gate_ready"], 1)
            act(score[:, 1, :], score[:, 0, :], ACT.Exp).then_inc(s["gates_done"], 1)
            with ac.Fori(0, UNITS1 // 4) as g4:
                for w in range(4):
                    act_unit1(ac, g4, w)
            ac.wait_ge(s["x1t_ready"], 1)
            act(xbT[:, 0, :], bank(4)[:, 0:P]).then_inc(s["x1t_done"], 1)
            act_step1(ac, 0, 0, hid=False, res=False)
            act_step1(ac, 0, 1, res=False)
            with ac.Fori(0, NB1 // 2 - 2) as h:
                for i in range(2):
                    act_step1(ac, h, i + 2)
            for i in range(4):
                act_step1(ac, NB1 // 2 - 2, i + 2, gu=i < 2, hid=i < 3, nxt=i < 1)
            act_transposed(ac, attnT, 5)
            act_transposed(ac, attnT, 6)
            for n in range(16):
                f, c = n % 4, n // 4
                ac.wait_ge(s["fc_ready"], n + 1)
                act(HT[:, f, c * 512:(c + 1) * 512], bank(4 + n % 4), ACT.Gelu_apprx_tanh, bias=bcols[:, 2 + f:3 + f]).then_inc(s["fc_done"], 1)

        def act_unit1(ac, g4, w):
            for k in range(KT):
                ac.wait_ge(s["c1_ready"], g4 * 32 + w * 8 + k + 1)
                ac.wait_ge(s["pv1_done"], g4 * 32 + w * 8 + k + 1)
                act(Z[:, k * S + k * P:(k + 1) * S], bank(2 + 2 * (k % 2), 2)[:, k * P:S], ACT.Exp, scale=1 / math.sqrt(D1))\
                    .then_inc(s["p1_done"], 1)
            ac.wait_ge(s["pv1_done"], g4 * 32 + w * 8 + 16)
            act(OT1[:, bass.ds(g4 * 4 + w, 1), :], bank(6)[:, 0:256].unsqueeze(1)).then_inc(s["head1_out"], 1)

        def act_step1(ac, h, i, gu=True, hid=True, nxt=True, res=True):
            if gu:
                ac.wait_ge(s["gu1_ready"], h * 2 + i + 1)
                act(hb1[:, i % 2, :], bank(i % 2), ACT.Gelu).then_inc(s["h1_ready"], 1)
            if hid:
                ac.wait_ge(s["h1t_ready"], h * 2 + i)
                act(hT1[:, (i + 1) % 2, :], bank(2 + (i + 1) % 2)).then_inc(s["h1t_done"], 1)
            if nxt:
                ac.wait_ge(s["x1t_ready"], h * 2 + i + 2)
                act(xbT[:, (i + 1) % 2, :], bank(4)[:, 0:P]).then_inc(s["x1t_done"], 1)
            if res:
                ac.wait_ge(s["o1_ready"], h * 2 + i - 1)
                ac.wait_ge(s[f"y1_stored{i % 2}"], h * 16 + 16 * (i // 2))
                act(yb[:, i % 2, :], bank(5 + i % 2)[:, 0:C]).then_inc(s["y1_ready"], 1)

        @block.scalar
        def _(ac):
            for n, cols in (("w_gate", 0), ("w_up", 256)):
                ac.dma_start(wst[:, cols:cols + 256].rearrange("p (t c) -> p t c", t=2),
                             a["L0_ffn_" + n].rearrange("(t p) c -> p t c", p=P)).then_inc(s["w_raw0"], 16)
            ac.dma_start(wst[:, 512:768], a["L0_ffn_w_down"]).then_inc(s["w_raw0"], 16)
            ac.dma_start(wst[0:E0, 768:768 + P], a["L0_ffn_w_router"]).then_inc(s["w_raw0"], 16)
            for i, n in enumerate(("bq", "bk")):
                ac.dma_start(bqk_row[:, i * P:(i + 1) * P], a["L0_attn_" + n].rearrange("(o n) d -> o (n d)", o=1)).then_inc(s["w_small0"], 16)
            ac.dma_start(bv_b, a["L0_attn_bv"].rearrange("n d -> (n d)").partition_broadcast(P)).then_inc(s["w_small0"], 16)
            ac.dma_start(bc2q_b, a["L0_attn_bc2q"].rearrange("n q -> (n q)").partition_broadcast(P)).then_inc(s["w_small0"], 16)
            ac.sem_inc(s["pv_evac"], 1)
            ac.wait_ge(s["wt_ready"], 1)
            act(guT[:], bank(4))
            act(dnT[:, :, :].rearrange("p t c -> p (t c)"), bank(5)[:, 0:256])
            act(bqk[:], bank(5)[:, 272:274])
            act(rout[:], bank(5)[:, 256:256 + E0]).then_inc(s["wt_done"], 1)
            act_transposed(ac, xT, 0)
            ac.wait_ge(s["w_small0"], 16 * 12)
            for r in range(4):
                scale = QSCALE0 if r % 2 == 0 else 1.0
                ac.wait_ge(s["proj_ready"], r + 1)
                act(qf[r], bank(4 + 2 * (r % 2), 2), ACT.Identity, bias=bqk[:, r % 2:r % 2 + 1]).then_inc(s["qf_ready"], 1)
                ac.wait_ge(s["qf_ready"], r + 1)
                act(part[r][:, 0, :], qf[r], scale=scale).then_inc(s["p1_ready"], 1)
                ac.wait_ge(s["res_ready"], r + 1)
                act(part[r][:, 1, :], res[r]).then_inc(s["p2_ready"], 1)
                if r == 2:
                    ac.wait_ge(s["top_ready"], 1)
                    act(score[:, 0, :], mx8[:, :, 0], ACT.Sigmoid).then_inc(s["score_ready"], 1)
            for r in range(4):
                ac.wait_ge(s["hat_ready"], r + 1)
                ac.wait_ge(s["p3_ready"], r + 1)
                act(qf[r][0:64, :], bank(4 + 2 * (r % 2), 2)[0:64, :]).then_inc(s["hatT_ready"], 1)
                ac.wait_ge(s["hatT_ready"], r + 1)
                ac.wait_ge(s["qk_stored"], 16 * NR * 4)
                act(part[r][0:64, 0, :], qf[r][0:64, :]).then_inc(s["p1_ready"], 1)
                ac.wait_ge(s["res_ready"], 4 + r + 1)
                act(part[r][0:64, 1, :], res[r][0:64, :]).then_inc(s["p2_ready"], 1)
            ac.wait_ge(s["flag_ready"], 1)
            flag = ac.value_load(flag_i[0:1, 0:1], min_val=0, max_val=1)
            with ac.Fori(0, PAIRS0 - 1) as p:
                act_pair(ac, p, flag)
            act_pair(ac, PAIRS0 - 1, flag)
            ac.wait_ge(s["prep_ready"], 1)
            act(w1T, bank(4))
            act(qoT, bank(5))
            act(repcol, bank(6, 2)).then_inc(s["prep_done"], 1)
            ac.wait_ge(s["prep_ready"], 2)
            act(w1m, bank(6)[:, 0:NQ])
            act(bdq, bank(7)[:, 0:P].unsqueeze(1).to_broadcast([P, NT, C])).then_inc(s["prep_done"], 1)
            act_transposed(ac, attnT, 1)
            act_transposed(ac, attnT, 2)
            ac.wait_ge(s["qm_done"], 1)
            act(qt, qm, ACT.Tanh)
            act(qc, qc, ACT.Sin, scale=-2 * math.pi, bias=half_pi[:]).then_inc(s["tc_done"], 1)
            ac.wait_ge(s["qeT_ready"], 1)
            act(qeT, bank(5)[:, 0:P]).then_inc(s["qeT_done"], 1)
            act_layer1(ac)

        v = nc.vector

        def dve_layernorm(dve, dst, src, n):
            for t in range(NT):
                last = v.bn_stats(st[:, t, :], src[:, t, :])
            dve_link(last)
            for t in range(NT):
                last = v.bn_aggr(mv[:, t, :], st[:, t, :])
            last.then_inc(s["ln_stats"], 1)
            dve.wait_ge(s["ln_rstd"], n + 1)
            for t in range(NT):
                last = v.tensor_scalar(dst[:, t, :], src[:, t, :], mv[:, t, 0:1], rstd[:, t:t + 1], ALU.subtract, ALU.mult)
            last.then_inc(s["ln_done"], 1)

        def dve_split(dve, n, rows, scale, src):
            r = n % 4
            dve.wait_ge(s["p1_ready"], n + 1)
            v.scalar_tensor_tensor(out=res[r][0:rows, :], in0=src[0:rows, :], scalar=scale, in1=part[r][0:rows, 0, :],
                                   op0=ALU.mult, op1=ALU.subtract).then_inc(s["res_ready"], 1)
            dve.wait_ge(s["p2_ready"], n + 1)
            v.tensor_tensor(part[r][0:rows, 2, :], res[r][0:rows, :], part[r][0:rows, 1, :], ALU.subtract).then_inc(s["p3_ready"], 1)

        def dve_top(dve, n, E, K):
            l3 = lg[:, 0:NT * E].rearrange("p (t e) -> p t e", e=E)
            for t in range(NT):
                last = v.max(mx8[:, t, :], l3[:, t, :])
            last.then_inc(s["top_ready"], 1)
            dve.wait_ge(s["top_ready"], n + 1)
            for t in range(NT):
                last = v.max_index(ix8[:, t, :], mx8[:, t, :], l3[:, t, :])
            dve_link(last)
            dve_link(v.tensor_copy(ixf[:, :, 0:K], ix8[:, :, 0:K]))
            o3 = oh.rearrange("p (k t e) -> p k t e", k=K, e=E)
            for k in range(K):
                last = v.tensor_tensor(o3[:, k], iota_e[:, 0:E].unsqueeze(1).to_broadcast([P, NT, E]),
                                       ixf[:, :, k:k + 1].to_broadcast([P, NT, E]), ALU.is_equal)
            dve_link(last)
            if K == 1:
                v.tensor_copy(oh_b[:, 0:NT * E], oh).then_inc(s["oh_ready"], 1)
            else:
                v.tensor_tensor(oh_b[:, 0:NT * E], oh[:, 0:NT * E], oh[:, NT * E:2 * NT * E], ALU.add).then_inc(s["oh_ready"], 1)

        def dve_positions(dve, n, E, K, NB):
            t3 = tot[:, 0:NT * E].rearrange("p (e t) -> p e t", t=NT)
            c3 = cum[:, 0:NT * E].rearrange("p (e t) -> p e t", t=NT)
            rk = lg[:, 0:NT * E].rearrange("p (t e) -> p t e", e=E)
            dve.wait_ge(s["rank_ready"], n + 1)
            dve_link(v.tensor_copy(t3, bank(1)[:, NT * E:2 * NT * E].rearrange("p (t e) -> p e t", e=E)))
            dve_link(v.tensor_tensor_scan(cum[:, 0:NT * E], scan_keep[:, 0:E, :].rearrange("p e t -> p (e t)"), tot[:, 0:NT * E],
                                          0.0, ALU.mult, ALU.add))
            dve_link(v.tensor_scalar(nbk[:, 0:E], c3[:, :, NT - 1], 1.0 / P, (P - 1) / P - 0.5 + 1 / 256, ALU.mult, ALU.add))
            dve_link(v.tensor_scalar(nbk[:, 0:E], nbk[:, 0:E], ROUND, ROUND, ALU.add, ALU.subtract))
            dve_link(v.tensor_tensor_scan(incl[:, 0:E], ones_e[:, 0:E], nbk[:, 0:E], 0.0, ALU.mult, ALU.add))
            v.tensor_tensor(t3, c3, t3, ALU.subtract)
            dve_link(v.tensor_tensor(basex[:, 0:E], incl[:, 0:E], nbk[:, 0:E], ALU.subtract))
            dve_link(v.tensor_scalar(basex[:, 0:E], basex[:, 0:E], float(P), None, ALU.mult))
            dve_link(v.tensor_tensor(rk, bank(1)[:, 0:NT * E].rearrange("p (t e) -> p t e", e=E),
                                     tot[:, 0:NT * E].rearrange("p (e t) -> p t e", t=NT), ALU.add))
            dve_link(v.tensor_tensor(rk, rk, basex[:, 0:E].unsqueeze(1).to_broadcast([P, NT, E]), ALU.add))
            o3 = oh.rearrange("p (k t e) -> p k t e", k=K, e=E)
            for k in range(K):
                dve_link(v.tensor_tensor(c3.rearrange("p e t -> p (e t)").rearrange("p (t e) -> p t e", e=E), rk, o3[:, k], ALU.mult))
                dve_link(v.tensor_reduce(posf[:, k * NT:(k + 1) * NT], cum[:, 0:NT * E].rearrange("p (t e) -> p t e", e=E), axis=AX.X, op=ALU.add))
                v.tensor_copy(pos_i[:, k, :], posf[:, k * NT:(k + 1) * NT])
            cmp_ = sq[0:1, 0:NB * E].rearrange("p (b e) -> p b e", e=E)
            dve_link(v.tensor_tensor(cmp_, incl[0:1, 0:E].unsqueeze(1).to_broadcast([1, NB, E]),
                                     iota_b[0:1, 0:NB].unsqueeze(2).to_broadcast([1, NB, E]), ALU.is_le))
            dve_link(v.tensor_reduce(tot[0:1, 0:NB], cmp_, axis=AX.X, op=ALU.add))
            v.tensor_scalar(eb_i[0:1, 0:NB], tot[0:1, 0:NB], float(E - 1), None, ALU.min).then_inc(s["pos_ready"], 1)
            dve.wait_ge(s["pos_ready"], n + 1)
            dve.sem_inc(s["xsrc_ready"], 1)

        def dve_max(dve, p, n):
            dve.wait_ge(s["f_ready"], p * 32 + n + 1)
            v.reduce_max(M[:, n // 8, n % 8:n % 8 + 1], bank(FB[n % 2], 2), AX.X).then_inc(s["f_free"], 1)

        def dve_mt_copy(dve, p, u):
            dve.wait_ge(s["mt_ready"], p * 2 + u + 1)
            if not (isinstance(p, int) and p == 0):
                dve.wait_ge(s["m_stored"], p * 32 + 16 * u)
            v.tensor_copy(mrow[:, u, :], bank(7 - u).bitcast(BF16)[0:PARTS * KT, 0:P]).then_inc(s["mt_copied"], 1)

        def dve_guard(dve, p, n):
            f = bank(FB[n % 2], 2)
            dve.wait_ge(s["f_ready"], p * 32 + n + 17)
            dve.wait_ge(s["g_ready"], p * 16 + n + 1)
            for half in range(2):
                last = v.tensor_scalar(Zt(n // 8, n % 8)[:, half * 512:(half + 1) * 512], bank(2 + half), 1 / EPS_COS, 1.0, ALU.mult, ALU.min)
            last.then_inc(s["g_step"], 1)
            dve.wait_ge(s["g_step"], p * 16 + n + 1)
            v.tensor_tensor(f, f, Zt(n // 8, n % 8), ALU.mult).then_inc(s["g_done"], 1)

        def dve_phase_a(dve, p, guard):
            if guard:
                dve.wait_ge(s["pv_done"], p * 16 + 1)
                dve_guard(dve, p, 0)
            for n in range(16):
                u, k = n // 8, n % 8
                if guard and n < 15:
                    dve.wait_ge(s["pv_done"], p * 16 + n + 2)
                    dve_guard(dve, p, n + 1)
                dve.wait_ge(s["pv_done"], p * 16 + n + 1)
                dve.wait_ge(s["sin_done"], p * 16 + n + 1)
                v.scalar_tensor_tensor(out=Zt(u, k), in0=snb[:, n % 2, :], scalar=10.0, in1=bank(FB[n % 2], 2),
                                       op0=ALU.add, op1=ALU.mult).then_inc(s["f_free"], 1)
                dve.wait_ge(s["c_ready"], p * 16 + n + 1)
                dve.wait_ge(s["f_free"], p * 32 + n + 19)
                v.tensor_tensor(Zt(u, k), Zt(u, k), bank(2, 2), ALU.add).then_inc(s["z_done"], 1)
                if n == 0:
                    dve_mt_copy(dve, p, 1)
                i = (n - 1) // 2
                if n % 2 == 1 and i < NBP:
                    dve.wait_ge(s["silu_done"], p * NBP + i + 1)
                    v.tensor_tensor(hb[:, i % 2, :], sg[:], bank(6)[:, F0:2 * F0], ALU.mult).then_inc(s["h_ready"], 1)

        def dve_pair(dve, p, flag, last):
            with dve.If(flag > 0):
                dve_phase_a(dve, p, True)
            with dve.Else():
                dve_phase_a(dve, p, False)
            if not last:
                for n in range(16):
                    dve_max(dve, p + 1, n)
                    if n == 13:
                        dve_mt_copy(dve, p + 1, 0)

        def dve_post0(dve):
            dve.wait_ge(s["post_loaded"], 16 * 14)
            v.tensor_copy(rep8.rearrange("p (t q) -> p t q", q=NQ), ident[0:8, 0:8].unsqueeze(1).to_broadcast([8, NT, NQ])).then_inc(s["prep_done"], 1)
            for n in range(8):
                b, hf, hg = n // 4, (n // 2) % 2, n % 2
                dve.wait_ge(s["o_ready"], n + 1)
                src = bank(n % 4).rearrange("p (h j c) -> p h j c", h=4, j=4)
                rc = rec[:, 0:16].rearrange("p (h j) -> p h j", h=4)
                dve_link(v.reciprocal(rc, src[:, :, :, D0]))
                dst = attn[:, b * KT:(b + 1) * KT, hg * 64:(hg + 1) * 64].rearrange("p (j f) (h d) -> p f h j d", f=2, h=4)[:, hf]
                for h in range(4):
                    last = v.tensor_tensor(dst[:, h], src[:, h, :, 0:D0], rc[:, h, :].unsqueeze(2).to_broadcast([P, 4, D0]), ALU.mult)
                last.then_inc(s["o_done"], 1)
                dve.wait_ge(s["o_done"], n + 1)
            dve.wait_ge(s["prep_done"], 3)
            v.tensor_tensor(bmm, bm_b, bank(6)[:, 8:8 + NQ], ALU.add)
            v.tensor_tensor(bff, b2_b, bank(7)[:, P:2 * P], ALU.add).then_inc(s["prep_done"], 1)
            dve.wait_ge(s["bo_added"], 1)
            for c in range(4):
                dve.wait_ge(s["wo_ready"], c + 1)
                xc = x1p[:, 4 * c:4 * c + 4, :]
                v.tensor_tensor(xc, xc, bank(c).rearrange("p (t c) -> p t c", c=C), ALU.add).then_inc(s["wo_done"], 1)
            dve.wait_ge(s["wo_done"], 4)
            dve_ln_affine(dve, x1, x1p, 1, g1_b, be1_b, x1)
            dve.wait_ge(s["qm_ready"], 1)
            dve_link(v.tensor_tensor(qm.rearrange("p (t q) -> p t q", q=NQ), bank(4)[:, 0:P].rearrange("p (t q) -> p t q", q=NQ),
                                     bmm.unsqueeze(1).to_broadcast([P, NT, NQ]), ALU.add))
            dve_link(v.tensor_scalar(qt, qm, 0.125, None, ALU.mult))
            dve_link(v.tensor_scalar(qc, qt, ROUND, ROUND, ALU.add, ALU.subtract))
            dve_link(v.tensor_tensor(qc, qt, qc, ALU.subtract))
            dve_link(v.scalar_tensor_tensor(out=qc, in0=qc, scalar=-1.0, in1=qc, op0=ALU.mult, op1=ALU.max))
            v.tensor_scalar(qc, qc, 0.5, None, ALU.min).then_inc(s["qm_done"], 1)
            dve.wait_ge(s["tc_done"], 1)
            v.tensor_tensor(qe, qt, qc, ALU.mult).then_inc(s["qe_ready"], 1)
            dve_link(v.tensor_tensor(x1, x1, bff.unsqueeze(1).to_broadcast([P, NT, C]), ALU.add))
            for c in range(4):
                dve.wait_ge(s["ff_ready"], c + 1)
                xc = x1[:, 4 * c:4 * c + 4, :]
                last = v.tensor_tensor(xc, xc, bank(c).rearrange("p (t c) -> p t c", c=C), ALU.add)
            dve_link(last)
            dve_ln_affine(dve, x1p, x1, 2, g2_b, be2_b, x1p)
            dve.wait_ge(s["xsum"], 65)
            v.tensor_tensor(xr, xr, x1p, ALU.add).then_inc(s["res0_ready"], 1)

        def dve_ln_affine(dve, dst, src, n, gain, shift, last_dst):
            for t in range(NT):
                last = v.bn_stats(st[:, t, :], src[:, t, :])
            dve_link(last)
            for t in range(NT):
                last = v.bn_aggr(mv[:, t, :], st[:, t, :])
            last.then_inc(s["ln_stats"], 1)
            dve.wait_ge(s["ln_rstd"], n + 1)
            for t in range(NT):
                last = v.tensor_scalar(dst[:, t, :], src[:, t, :], mv[:, t, 0:1], rstd[:, t:t + 1], ALU.subtract, ALU.mult)
            dve_link(last)
            dve_link(v.tensor_tensor(dst, dst, gain.unsqueeze(1).to_broadcast([P, NT, C]), ALU.mult))
            ins = v.tensor_tensor(dst, dst, shift.unsqueeze(1).to_broadcast([P, NT, C]), ALU.add)
            ins.then_inc(s["ln_done"], 1)
            dve.wait_ge(s["ln_done"], n + 1)

        def dve_layer1(dve):
            dve.wait_ge(s["res0_ready"], 1)
            dve_layernorm(dve, xn[:], xr, 3)
            dve.wait_ge(s["ln_done"], 4)
            dve_layernorm(dve, lx, xn[:], 4)
            for c in range(4):
                dve.wait_ge(s["v1_ready"], c + 1)
                b, k0 = c // 2, (c % 2) * 4
                dst = Vc[:, :].rearrange("p (u k d) -> p k u d", k=KT, d=D1)[:, k0:k0 + 4, b * H1:(b + 1) * H1, :]
                for k in range(4):
                    last = v.tensor_tensor(dst[:, k], bank(c)[:, k * P:(k + 1) * P].rearrange("p (h d) -> p h d", d=D1),
                                           bv1_b.rearrange("p (h d) -> p h d", d=D1), ALU.add)
                last.then_inc(s["v1_done"], 1)
            dve.wait_ge(s["lg1_ready"], 1)
            dve_link(v.tensor_tensor(lg[:, 0:NT * E1].rearrange("p (t e) -> p t e", e=E1),
                                     bank(0)[:, 0:NT * E1].rearrange("p (t e) -> p t e", e=E1),
                                     rb1_b.unsqueeze(1).to_broadcast([P, NT, E1]), ALU.add))
            dve_top(dve, 1, E1, TOP1)
            v.tensor_tensor(score[:, 0, :], mx8[:, :, 1], mx8[:, :, 0], ALU.subtract).then_inc(s["gate_ready"], 1)
            for r in range(2):
                dve_split(dve, 8 + r, P, 1.0, qf[r])
            dve_positions(dve, 1, E1, TOP1, NB1)
            for r in range(2, 4):
                dve_split(dve, 8 + r, P, 1.0, qf[r])
            dve.wait_ge(s["gates_done"], 1)
            dve_link(v.tensor_scalar(score[:, 0, :], score[:, 1, :], 1.0, None, ALU.add))
            dve_link(v.reciprocal(score[:, 0, :], score[:, 0, :]))
            dve_link(v.tensor_tensor(score[:, 1, :], score[:, 1, :], score[:, 0, :], ALU.mult))
            for c in range(12):
                dve_max1(dve, 0, 0, c)
            dve_mt1_copy(dve, 0, 0, False)
            for c in range(12):
                dve_max1(dve, 1, 1, c)
            for w in range(4):
                dve_unit1(dve, 0, w, False)
            with dve.Fori(1, UNITS1 // 4 - 1) as g4:
                for w in range(4):
                    dve_unit1(dve, g4, w, False)
            for w in range(4):
                dve_unit1(dve, UNITS1 // 4 - 1, w, True)
            for n in range(16):
                b, hf, hg = n // 8, (n // 4) % 2, n % 4
                dve.wait_ge(s["o1t_ready"], n + 1)
                src = bank(n % 4).rearrange("p (h j c) -> p h j c", h=4, j=4)
                rc = rec[:, 0:16].rearrange("p (h j) -> p h j", h=4)
                dve_link(v.reciprocal(rc, src[:, :, :, D1]))
                dst = attn[:, b * KT:(b + 1) * KT, hg * 32:(hg + 1) * 32].rearrange("p (j f) (h d) -> p f h j d", f=2, h=4)[:, hf]
                for h in range(4):
                    last = v.tensor_tensor(dst[:, h], src[:, h, :, 0:D1], rc[:, h, :].unsqueeze(2).to_broadcast([P, 4, D1]), ALU.mult)
                last.then_inc(s["o1n_done"], 1)
                dve.wait_ge(s["o1n_done"], n + 1)
            dve.wait_ge(s["bproj_added"], 1)
            for c in range(4):
                dve.wait_ge(s["proj1_ready"], c + 1)
                xc = xn[:, 4 * c:4 * c + 4, :]
                v.tensor_tensor(xc, xc, bank(c).rearrange("p (t c) -> p t c", c=C), ALU.add).then_inc(s["proj1_done"], 1)
            dve.wait_ge(s["proj1_done"], 4)
            dve_layernorm(dve, lx2, xn[:], 5)
            dve.wait_ge(s["ln_done"], 6)
            dve_link(v.tensor_tensor(xn[:], xn[:], bmlp_b.unsqueeze(1).to_broadcast([P, NT, C]), ALU.add))
            for c in range(4):
                dve.wait_ge(s["mlp_ready"], c + 1)
                xc = xn[:, 4 * c:4 * c + 4, :]
                last = v.tensor_tensor(xc, xc, bank(c).rearrange("p (t c) -> p t c", c=C), ALU.add)
            dve_link(last)
            dve.wait_ge(s["x1_loaded"], 16)
            dve_link(v.tensor_tensor(xn[:], xn[:], x1r, ALU.add))
            dve.wait_ge(s["gathered1"], 16 * TOP1 * NT)
            for k in range(TOP1):
                for t in range(NT):
                    last = v.scalar_tensor_tensor(out=xn[:, t, :], in0=yg1[:, k, t, :], scalar=score[:, k, t:t + 1], in1=xn[:, t, :],
                                                  op0=ALU.mult, op1=ALU.add)
                if k == 0:
                    dve_link(last)
            last.then_inc(s["mlp_done"], 1)

        def dve_max1(dve, unit, u, c):
            u = u % 2
            i, half = (c, 0) if c < 4 else (4 + (c - 4) // 2, (c - 4) % 2)
            width = min(512, (i + 1) * P - 512 * half)
            dve.wait_ge(s["max1_ready"], unit * 12 + c + 1)
            dst = M2[:, u, i - 4:i - 3] if half else M[:, u, i:i + 1]
            v.reduce_max(dst, bank(MB[c % 3])[:, 0:width], AX.X).then_inc(s["max1_free"], 1)
            if c == 11:
                dve.wait_ge(s["max1_free"], unit * 12 + 15)
                v.tensor_tensor(M[:, u, 4:8], M[:, u, 4:8], M2[:, u, :], ALU.max).then_inc(s["max1_whole"], 1)

        def dve_mt1_copy(dve, unit, u, stored=True):
            dve.wait_ge(s["mt1_ready"], unit + 1)
            if stored:
                dve.wait_ge(s["m1_stored"], unit * 16 - 16)
            v.tensor_copy(mrow[:, u % 2, :], bank(0).bitcast(BF16)[0:PARTS * KT, 0:P]).then_inc(s["mt1_copied"], 1)

        def dve_unit1(dve, g4, w, last_group):
            unit = g4 * 4 + w
            maxima = not (last_group and w >= 2)
            c = 0
            for k in range(KT):
                if k == 1 and not (last_group and w == 3):
                    dve_mt1_copy(dve, unit + 1, w + 1, not (isinstance(unit, int) and unit == 0))
                if maxima:
                    for _ in range(1 if k < 4 else 2):
                        dve_max1(dve, unit + 2, w, c)
                        c += 1

        @block.vector
        def _(dve):
            dve.sem_inc(s["f_free"], 2)
            dve.sem_inc(s["z_done"], 1)
            dve.sem_inc(s["pv_done"], 16)
            dve.sem_inc(s["m_stored"], 16)
            dve.sem_inc(s["xt_ready"], 2)
            for i in range(2):
                dve.sem_inc(s[f"y_stored{i}"], 16)
                dve.sem_inc(s[f"y1_stored{i}"], 16)
            dve.sem_inc(s["max1_free"], 3)
            dve.sem_inc(s["p1_done"], 2)
            dve.sem_inc(s["pv1_done"], 8)
            dve.sem_inc(s["head1_out"], 1)
            dve.wait_ge(s["x_loaded"], 32)
            dve_layernorm(dve, xn[:], x_in, 0)
            dve.wait_ge(s["w_small0"], 16 * 12)
            for c in range(4):
                dve.wait_ge(s["v_ready"], c + 1)
                b, k0 = c // 2, (c % 2) * 4
                dst = Vc[:, :].rearrange("p (u k d) -> p k u d", k=KT, d=D0)[:, k0:k0 + 4, b * H0:(b + 1) * H0, :]
                for k in range(4):
                    last = v.tensor_tensor(dst[:, k], bank(c)[:, k * P:(k + 1) * P].rearrange("p (h d) -> p h d", d=D0),
                                           bv_b.rearrange("p (h d) -> p h d", d=D0), ALU.add)
                last.then_inc(s["v_done"], 1)
            dve.wait_ge(s["lg_ready"], 1)
            dve_link(v.tensor_copy(lg, bank(0)[:, 0:256]))
            dve_top(dve, 0, E0, 1)
            for r in range(4):
                dve_split(dve, r, P, QSCALE0 if r % 2 == 0 else 1.0, qf[r])
            dve.wait_ge(s["score_ready"], 1)
            v.tensor_tensor(x_in, xn[:], score[:, 0, :].unsqueeze(2).to_broadcast([P, NT, C]), ALU.mult)
            dve_positions(dve, 0, E0, 1, NB0)
            for r in range(4):
                dve.wait_ge(s["qq_ready"], r + 1)
                dve_link(v.tensor_tensor(qq[r].rearrange("p (k c) -> p k c", c=64), bank(2 + r % 2).rearrange("p (k c) -> p k c", c=64),
                                         bc2q_b.unsqueeze(1).to_broadcast([P, KT, 64]), ALU.add))
                dve_link(v.tensor_tensor(sq, qq[r], qq[r], ALU.mult))
                dve_link(v.tensor_reduce(ss[:, r, :], sq.rearrange("p (g q) -> p g q", q=NQ), axis=AX.X, op=ALU.add))
                v.tensor_scalar(ss[:, r, :], ss[:, r, :], 1e-37, None, ALU.max).then_inc(s["ss_ready"], 1)
            for r in range(4):
                dve.wait_ge(s["inv_ready"], r + 1)
                v.tensor_tensor(qq[r].rearrange("p (g q) -> p g q", q=NQ), qq[r].rearrange("p (g q) -> p g q", q=NQ),
                                inv[:, r, :].unsqueeze(2).to_broadcast([P, 64, NQ]), ALU.mult).then_inc(s["qh_ready"], 1)
            for r in range(4):
                dve_split(dve, 4 + r, 64, 1.0, qf[r])
            v.tensor_tensor(nrm.rearrange("p (r h k) -> p r k h", r=4, h=H0), ss[:, :, :].rearrange("p r (k h) -> p r k h", h=H0),
                            inv[:, :, :].rearrange("p r (k h) -> p r k h", h=H0), ALU.mult)
            dve_link(v.tensor_reduce(small[:, 1:2], ss[:, :, :].rearrange("p r g -> p (r g)"), axis=AX.X, op=ALU.min))
            v.tensor_scalar(small[:, 0:1], small[:, 1:2], EPS_COS * 1.01, None, ALU.is_lt).then_inc(s["nrm_ready"], 1)
            dve.wait_ge(s["nt_ready"], 1)
            v.tensor_copy(nT, bank(2)[0:64, :])
            v.tensor_scalar(flag_i[:], bank(3)[0:1, 0:1], 1.0, None, ALU.min).then_inc(s["flag_ready"], 1)
            for n in range(16):
                dve_max(dve, 0, n)
            dve_mt_copy(dve, 0, 0)
            dve.wait_ge(s["flag_ready"], 1)
            flag = dve.value_load(flag_i[0:1, 0:1], min_val=0, max_val=1)
            with dve.Fori(0, PAIRS0 - 1) as p:
                dve_pair(dve, p, flag, False)
            dve_pair(dve, PAIRS0 - 1, flag, True)
            dve_post0(dve)
            dve_layer1(dve)


_OUT = ((B, S, C), "float32")


def kernel(**inputs):
    import concourse.bacc as bacc
    from concourse.bass_utils import run_bass_kernel_spmd

    nc = bacc.Bacc("TRN2", target_bir_lowering=False, num_devices=1)
    arrays, args = {}, {}
    for name, value in inputs.items():
        arr = np.ascontiguousarray(value)
        arrays["in_" + name] = arr
        args[name] = nc.dram_tensor("in_" + name, arr.shape, mybir.dt.from_np(arr.dtype), kind="ExternalInput").ap()
    out = nc.dram_tensor("out_x", _OUT[0], mybir.dt.from_np(np.dtype(_OUT[1])), kind="ExternalOutput").ap()
    build(nc, args, out)
    result = run_bass_kernel_spmd(nc, [arrays], core_ids=[0])
    return result.results[0]["out_x"]
```

```python
from contextlib import ExitStack
import math

import numpy as np
import concourse.bass as bass
from concourse import mybir

ALU = mybir.AluOpType
ACT = mybir.ActivationFunctionType
AX = mybir.AxisListType
F32 = mybir.dt.float32
BF16 = mybir.dt.bfloat16
U32 = mybir.dt.uint32
I32 = mybir.dt.int32

P = 128
B, S, C = 2, 1024, 128
NT = B * S // P
KT = S // P
NEG = -1e30
ROUND = 12582912.0
PARTS = 3
Q_ROWS = (0, 0, 1, 1, 0, 2)
K_ROWS = (0, 1, 0, 1, 2, 0)
NR = len(Q_ROWS)

H0, D0, NQ = 8, 16, 8
R0 = NR * D0
RF = NR * NQ
KPAD = 96
UNITS0 = B * H0
PAIRS0 = UNITS0 // 2
QSCALE0 = 10.0 / math.sqrt(D0)
EPS_COS = 1e-8
PI_IN = math.pi * (1 - 8e-7)
E0, F0 = 16, 256
NB0 = NT + E0
XB, SHB = NB0 // PAIRS0, NT // PAIRS0
NBP = XB + SHB
AHEAD = 3
MAX_CHUNKS = [(i, half) for i in range(KT - 1, -1, -1) for half in range(1 + i // 4)]
H1, D1 = 16, 8
R1 = NR * D1
UNITS1 = B * H1
E1, F1, TOP1 = 8, 512, 2
NB1 = TOP1 * NT + E1


def build(nc, a, out):
    with ExitStack() as ctx:
        def sb(name, shape, dt=F32):
            return ctx.enter_context(nc.sbuf_tensor(name, shape, dt))

        def dram(name, shape, dt=F32):
            return nc.dram_tensor(name, shape, dt, kind="Internal").ap()

        q0d = dram("q0d", (B * H0 * D0, NR, S), BF16)
        k0d = dram("k0d", (B * H0 * D0, NR, S), BF16)
        fq0d = dram("fq0d", (B * H0 * NQ, NR, S), BF16)
        fk0d = dram("fk0d", (B * H0 * NQ, NR, S), BF16)
        n0d = dram("n0d", (2 * UNITS0, S))
        m0d = dram("m0d", (UNITS0, PARTS * KT, P), BF16)
        xs0 = dram("xs0", (NB0 * P, C))
        q1d = dram("q1d", (UNITS1 * D1, NR, S), BF16)
        k1d = dram("k1d", (UNITS1 * D1, NR, S), BF16)
        m1d = dram("m1d", (UNITS1, PARTS * KT, P), BF16)
        xs1 = dram("xs1", (NB1 * P, C))
        ys1 = dram("ys1", (NB1 * P, C))
        x1d = dram("x1d", (P, NT * C))
        ys0 = dram("ys0", ((NB0 + NT) * P, C))

        xn = sb("xn", [P, NT, C])
        xT = sb("xT", [P, NT * P])
        W = sb("W", [P, 12288])
        gu_w = W[:, 0:E0 * 2 * F0]
        dn_w = W[:, E0 * 2 * F0:E0 * 2 * F0 + E0 * 2 * C]
        Z = sb("Z", [P, 16384])
        OT = sb("OT", [P, UNITS0, 256])
        snb = sb("snb", [P, 2, S])
        QM = sb("QM", [P, 2, S], BF16)
        KM = sb("KM", [P, 2, S], BF16)
        QS = sb("QS", [P, 2, S], BF16)
        KS = sb("KS", [P, 2, S], BF16)
        FQ = sb("FQ", [P, 2, S], BF16)
        FK = sb("FK", [P, 2, S], BF16)
        Vc = sb("Vc", [P, UNITS0 * KT * D0])
        VU = sb("VU", [P, 2, KT, 32])
        ident = sb("ident", [P, P])
        identb = sb("identb", [P, P], BF16)
        onesb = sb("onesb", [P, P], BF16)
        lowb = sb("lowb", [P, P], BF16)
        ones_row = sb("ones_row", [1, P])
        iota_e = sb("iota_e", [P, E0])
        iota_b = sb("iota_b", [P, NB1])
        ones_e = sb("ones_e", [P, E0])
        minus_half = sb("minus_half", [P, 64])
        below = sb("below", [P, P], BF16)
        above = sb("above", [P, P], BF16)
        sign = sb("sign", [P, 2, KT * D0])
        half_pi = sb("half_pi", [P, 1])
        scan_keep = sb("scan_keep", [P, E0, NT])
        wqkv = sb("wqkv", [P, 3, P])
        bqk = sb("bqk", [P, 2])
        bd = sb("bd", [P, H0 * NQ])
        guT = sb("guT", [P, 2 * F0])
        dnT = sb("dnT", [P, 2, C])
        rout = sb("rout", [P, E0])
        mv = sb("mv", [P, NT, 2])
        st = sb("st", [P, NT, 6])
        ve = sb("ve", [P, NT])
        rstd = sb("rstd", [P, NT])
        rstd2 = sb("rstd2", [P, NT])
        M = sb("M", [P, 2, KT])
        msp = sb("msp", [P, 2, 4, KT])
        mpart = sb("mpart", [P, 2, PARTS, KT], BF16)
        mrow = sb("mrow", [PARTS * KT, 2, P], BF16)
        inv = sb("inv", [P, 4, KT * H0])
        ss = sb("ss", [P, 4, KT * H0])
        flag_i = sb("flag_i", [1, 1], I32)
        eb_i = sb("eb_i", [1, 64], I32)
        pos_i = sb("pos_i", [P, TOP1, NT], U32)
        score = sb("score", [P, TOP1, NT])
        xb = sb("xb", [P, 2, C])
        xbT = sb("xbT", [P, 2, P])
        sg = sb("sg", [P, F0])
        hb = sb("hb", [P, 2, F0])
        hT = sb("hT", [P, 2, F0])
        yb = sb("yb", [P, 2, C])

        PS = ctx.enter_context(nc.psum_tensor("PS", [P, 8, 512], F32))

        def bank(i, n=1):
            return PS[:, i:i + n, :].rearrange("p b c -> p (b c)")

        qf = [Z[:, r * S:(r + 1) * S] for r in range(4)]
        res = [Z[:, (4 + r) * S:(5 + r) * S] for r in range(4)]
        part = [Z[:, 8192 + 1536 * r:8192 + 1536 * (r + 1)].bitcast(BF16).rearrange("p (j s) -> p j s", j=3)
                for r in range(4)]
        qq = [Z[:, 14336 + 512 * r:14336 + 512 * (r + 1)] for r in range(4)]
        QSf = QS[:, :, :].rearrange("p a s -> p (a s)").bitcast(F32)
        nT, nrm, small = QSf[0:64, 0:512], QSf[:, 512:768], QSf[:, 768:770]
        OTf = OT[:, :, :].rearrange("p u s -> p (u s)")
        x_in = OTf[:, 0:2048].rearrange("p (t c) -> p t c", c=C)
        sq = OTf[:, 2048:2560]
        R = OTf[:, 2560:4096]
        lg = R[:, 0:256]
        mx8 = R[:, 256:384].rearrange("p (t k) -> p t k", k=8)
        ix8 = R[:, 384:512].bitcast(U32).rearrange("p (t k) -> p t k", k=8)
        ixf = R[:, 512:544].rearrange("p (t k) -> p t k", k=2)
        oh = R[:, 544:800]
        oh_b = R[:, 800:928].bitcast(BF16)
        tot = R[:, 928:1184]
        cum = R[:, 1184:1440]
        nbk, incl = R[:, 1440:1456], R[:, 1456:1472]
        basex, posf = R[:, 1472:1488], R[:, 1488:1520]
        zeros = snb[:, 1, :]
        wst = snb[:, :, :].rearrange("p a s -> p (a s)")

        attn = Z[:, 0:2048].rearrange("p (t c) -> p t c", c=C)
        attnT = Z[:, 2048:4096]
        x1p = Z[:, 4096:6144].rearrange("p (t c) -> p t c", c=C)
        x1 = Z[:, 6144:8192].rearrange("p (t c) -> p t c", c=C)
        bdq = Z[:, 8192:10240].rearrange("p (t c) -> p t c", c=C)
        xr = Vc[:, :].rearrange("p (t c) -> p t c", c=C)
        yg = xT[:, :].rearrange("p (t c) -> p t c", c=C)
        ysh = [t[:, :, :].rearrange("p a s -> p (a s)").bitcast(F32).rearrange("p (t c) -> p t c", c=C)
               for t in (QS, KS)]
        NROW = 64
        QMf = QM[:, :, :].rearrange("p a s -> p (a s)").bitcast(F32)
        KMf = KM[:, :, :].rearrange("p a s -> p (a s)").bitcast(F32)
        FQf = FQ[:, :, :].rearrange("p a s -> p (a s)").bitcast(F32)
        FKf = FK[:, :, :].rearrange("p a s -> p (a s)").bitcast(F32)
        w1r, w2r = QMf[:, 0:512], QMf[:, 512:1024].rearrange("p (t c) -> p t c", c=C)
        w1T, qoT = KMf[:, 0:512], KMf[:, 512:1024]
        wo, bo_b = FQf[:, 0:128], FQf[:, 128:256]
        g1_b, be1_b, g2_b, be2_b, b2_b, bff = [FQf[:, 256 + 128 * i:384 + 128 * i] for i in range(6)]
        wm = FKf[:, 0:32].rearrange("p (t q) -> p t q", q=NQ)
        w1m, bm_b, bmm = FKf[:, 32:40], FKf[:, 40:48], FKf[:, 48:56]
        b1_row, bqo_row = [t[0:1, :, :].rearrange("p a f -> p (a f)") for t in (hb, hT)]
        bv_b, bc2q_b = FQf[:, 256:384], FQf[:, 384:448]
        bqk_row = FQf[0:1, 0:2 * P]
        wqo8 = FKf[0:8, 512:1024]
        rep8 = FKf[0:8, 64:192]
        qm = snb[:, 0, 0:128]
        qt = snb[:, 0, 128:256]
        qc = snb[:, 0, 256:384]
        qe = snb[:, 0, 384:512]
        qeT = snb[:, 0, 512:640]
        repcol = snb[:, 1, :]
        rec = snb[:, 0, 640:672]

        w1_all = W[:, 0:E1 * F1]
        w2_all = W[:, E1 * F1:2 * E1 * F1]
        W1 = W[:, 2 * E1 * F1:12288]
        raw_attn, raw_proj, raw_fc, raw_mlp = W1[:, 0:384], W1[:, 384:512], W1[:, 512:1024], W1[:, 1024:1536]
        wprojT, wfcT, wmlpT = W1[:, 1536:1664], W1[:, 1664:2176], W1[:, 2176:2688]
        bv1_b, bproj_b, bmlp_b, rb1_b, rw1 = W1[:, 2688:2816], W1[:, 2816:2944], W1[:, 2944:3072], W1[:, 3072:3080], W1[:, 3080:3088]
        bcols = W1[:, 3088:3094]
        brow1 = W1[0:1, 3200:3968]
        b1_b, b2_b1 = OTf, FQf
        lx = snb[:, :, :].rearrange("p a (t c) -> p (a t) c", c=C)
        lxT = OTf[:, 0:2048]
        slots = [(QS, KS, 0), (QS, KS, 1), (QM, KM, 0), (QM, KM, 1)]
        M2 = msp[:, :, 3, 0:4]
        OT1 = Z[:, 8192:16384].rearrange("p (u s) -> p u s", s=256)
        hb1 = snb[:, 0, :].rearrange("p (i f) -> p i f", i=2)
        hT1 = snb[:, 1, :].rearrange("p (i f) -> p i f", i=2)
        HT = Z[:, 8192:16384].rearrange("p (f s) -> p f s", f=4)
        lx2 = x1p
        yg1 = W[:, 0:4096].rearrange("p (k t c) -> p k t c", k=2, c=C)
        x1r = W[:, 4096:6144].rearrange("p (t c) -> p t c", c=C)
        MB = (0, 1, 7)
        MAX_STEPS = (7, 5)
        MT = 3

        names = """const x_loaded wqkv_loaded w_raw0 w_small0 gu_loaded dn_loaded zeroed
            ln_stats ln_rstd ln_done tr_ready tr_done wt_ready wt_done
            v_ready v_done lg_ready proj_ready qf_ready p1_ready res_ready p2_ready p3_ready qk_stored
            qq_ready ss_ready inv_ready qh_ready hat_ready hatT_ready f_stored dve_step pool_step
            oh_ready rank_ready pos_ready top_ready score_ready xsrc_ready scattered
            max_loaded main_loaded f_ready f_free sin_done c_ready z_done exp_done pv_done pv_evac v_copied
            m_split mt_ready mt_copied m_stored m_loaded
            xb_loaded0 xb_loaded1 xt_ready xbT_ready gu_ready silu_done h_ready ht_ready hT_done out_ready yb_ready y_stored0 y_stored1
            post_loaded o_ready o_done prep_ready prep_done wo_ready wo_done qm_ready qm_done tc_done qe_ready
            qeT_ready qeT_done ff_ready bo_added bd_masked gathered xsum
            res0_ready out_stored
            pad_cleared nrm_ready nt_ready flag_ready n_stored n_loaded g_ready g_done g_step
            x1_stored l1_loaded wt1_ready wt1_done v1_ready v1_done lg1_ready gate_ready gates_done scattered1
            slot_loaded0 slot_loaded1 slot_loaded2 slot_loaded3 max1_ready max1_free max1_whole c1_ready p1_done pv1_done head1_out
            v1_copied vu1_cleared m1_split mt1_ready mt1_copied m1_stored m1_loaded
            x1b_loaded0 x1b_loaded1 x1t_ready x1t_done gu1_ready b1_added h1_ready h1t_ready h1t_done o1_ready y1_ready
            y1_stored0 y1_stored1 gathered1 bias1_loaded o1t_ready o1n_done bproj_added proj1_ready proj1_done
            fc_ready fc_done mlp_ready mlp_done x1_loaded""".split()
        s = {n: ctx.enter_context(nc.semaphore(n)) for n in names}
        block = ctx.enter_context(nc.Block())

        def dve_link(ins, cnt=[0]):
            cnt[0] += 1
            ins.then_inc(s["dve_step"], 1)
            nc.vector.wait_ge(s["dve_step"], cnt[0])

        def pool_link(ins, cnt=[0]):
            cnt[0] += 1
            ins.then_inc(s["pool_step"], 1)
            nc.gpsimd.wait_ge(s["pool_step"], cnt[0])

        def Zt(u, k):
            return Z[:, (u * KT + k) * S:(u * KT + k + 1) * S]

        FB = (0, 4)


        def sp_max_load(sp, p):
            for t, d in ((QM, q0d), (KM, k0d)):
                sp.dma_start(t[0:R0, :, :], d[bass.ds(p * 32, 32)].rearrange("(u d) j s -> (d j) u s", u=2)).then_inc(s["max_loaded"], 16)

        def sp_main_load(sp, p):
            for t, d in ((QS, q0d), (KS, k0d)):
                sp.dma_start(t[0:R0, :, :], d[bass.ds(p * 32, 32)].rearrange("(u d) j s -> (d j) u s", u=2)).then_inc(s["main_loaded"], 16)
            for t, d in ((FQ, fq0d), (FK, fk0d)):
                sp.dma_start(t[0:RF, :, :], d[bass.ds(p * 16, 16)].rearrange("(u d) j s -> (d j) u s", u=2)).then_inc(s["main_loaded"], 16)

        def sp_m_rows(sp, p, u):
            sp.wait_ge(s["mt_copied"], p * 2 + u + 1)
            sp.dma_start(m0d[bass.ds(p * 2 + u, 1)].rearrange("o r q -> (o r) q"), mrow[:, u, :]).then_inc(s["m_stored"], 16)
            sp.wait_ge(s["m_stored"], p * 32 + 16 * u + 32)
            sp.dma_start(QS[R0:R0 + PARTS, u, :], m0d[bass.ds(p * 2 + u, 1)].rearrange("o (j i) q -> (o j) (i q)", j=PARTS)).then_inc(s["m_loaded"], 16)

        def sp_norm_rows(sp, p, u):
            for i, t in enumerate((FQf, FKf)):
                sp.dma_start(t[NROW:NROW + 1, :], n0d[bass.ds(p * 2 + u + i * UNITS0, 1)]).then_inc(s["n_loaded"], 16)

        def sp_pair(sp, p, flag, last):
            sp_m_rows(sp, p, 1)
            sp.wait_ge(s["f_ready"], p * 32 + 16)
            if not last:
                sp_max_load(sp, p + 1)
            else:
                sp.dma_start(w1r, a["L0_attn_W1"]).then_inc(s["post_loaded"], 16)
                sp.dma_start(w2r, a["L0_attn_W2"].rearrange("(t p) c -> p t c", p=P)).then_inc(s["post_loaded"], 16)
                sp.wait_ge(s["v_copied"], UNITS0)
                for h in (0, KT):
                    sp.dma_start(xr[:, h:h + KT], a["L0_attn_x"][h // KT].rearrange("(k p) c -> p k c", p=P)).then_inc(s["xsum"], 16)
            for i in range(2, XB):
                sp_x_load(sp, p, i)
            for i in range(NBP):
                if i >= 1:
                    sp_y_store(sp, p, i - 1)
                if i == 2:
                    with sp.If(flag > 0):
                        sp.wait_ge(s["g_done"], p * 16 + 8)
                        sp_norm_rows(sp, p, 1)
            sp_y_store(sp, p, NBP - 1)
            if not last:
                for i in range(2):
                    sp_x_load(sp, p + 1, i)
                sp.wait_ge(s["c_ready"], p * 16 + 16)
                sp_main_load(sp, p + 1)
                with sp.If(flag > 0):
                    sp_norm_rows(sp, p + 1, 0)
                sp_m_rows(sp, p + 1, 0)

        def sp_x_load(sp, p, i):
            sp.wait_ge(s["xt_ready"], p * XB + i + 1)
            sp.dma_start(xb[:, i % 2, :], xs0[bass.ds(p * (XB * P) + i * P, P)]).then_inc(s[f"xb_loaded{i % 2}"], 16)

        def sp_y_store(sp, p, i):
            sp.wait_ge(s["yb_ready"], p * NBP + i + 1)
            row = p * (XB * P) + i * P if i < XB else p * (SHB * P) + (NB0 + i - XB) * P
            sp.dma_start(ys0[bass.ds(row, P)], yb[:, i % 2, :]).then_inc(s[f"y_stored{i % 2}"], 16)

        def sp_weights1(sp):
            rows = lambda n: a["L1_attn_" + n].rearrange("(t p) c -> p t c", p=P)
            for t, src in ((raw_attn.rearrange("p (t c) -> p t c", c=C), rows("w_attn")), (raw_proj, a["L1_attn_w_proj"]),
                           (raw_fc.rearrange("p (t c) -> p t c", c=C), rows("w_fc")), (raw_mlp, a["L1_attn_w_mlp_proj"]),
                           (brow1[:, 0:256], a["L1_attn_b_attn"][0:256].rearrange("(o f) -> o f", o=1)),
                           (brow1[:, 256:768], a["L1_attn_b_fc"].rearrange("(o f) -> o f", o=1)),
                           (bv1_b, a["L1_attn_b_attn"][256:384].partition_broadcast(P)), (bproj_b, a["L1_attn_b_proj"].partition_broadcast(P)),
                           (bmlp_b, a["L1_attn_b_mlp_proj"].partition_broadcast(P)), (rb1_b, a["L1_ffn_router_b"].partition_broadcast(P)),
                           (rw1, a["L1_ffn_router_w"])):
                sp.dma_start(t, src).then_inc(s["l1_loaded"], 16)
            sp.dma_start(w1_all.rearrange("p (e f) -> p e f", f=F1), a["L1_ffn_w1"].rearrange("e c f -> c e f")).then_inc(s["l1_loaded"], 16)
            for e in range(0, E1, 2):
                sp.dma_start(w2_all[:, e * F1:(e + 2) * F1].rearrange("p (e c) -> p e c", c=C),
                             a["L1_ffn_w2"][e:e + 2].rearrange("e (t p) c -> p (e t) c", p=P)).then_inc(s["l1_loaded"], 16)

        L1_LOADS = 16

        def sp_layer1(sp):
            for r in range(4):
                dst, rows = (q1d, k1d)[r % 2], (Q_ROWS, K_ROWS)[r % 2]
                sp.wait_ge(s["p3_ready"], 8 + r + 1)
                for j, n in enumerate(rows):
                    sp.dma_start(dst[(r // 2) * P:(r // 2 + 1) * P, j, :], part[r][:, n, :]).then_inc(s["qk_stored"], 16)
                if r == 1:
                    sp.wait_ge(s["qk_stored"], 16 * NR * 6)
                    sp.wait_ge(s["vu1_cleared"], 1)
                    for n in range(4):
                        sp_slot_load(sp, n, n)
            sp.wait_ge(s["qk_stored"], 16 * NR * 8)
            sp_m1_rows(sp, 0, 0)
            sp.wait_ge(s["pos_ready"], 2)
            sp.dma_start(b1_b, a["L1_ffn_b1"].rearrange("e f -> (e f)").partition_broadcast(P)).then_inc(s["bias1_loaded"], 16)
            sp.dma_start(b2_b1, a["L1_ffn_b2"].rearrange("e c -> (e c)").partition_broadcast(P)).then_inc(s["bias1_loaded"], 16)
            with sp.Fori(0, UNITS1 // 4 - 1) as g4:
                for w in range(4):
                    sp_unit1(sp, g4, w, False)
            sp.wait_ge(s["scattered1"], 16 * TOP1 * NT)
            for i in range(2):
                sp.dma_start(xb[:, i, :], xs1[i * P:(i + 1) * P]).then_inc(s[f"x1b_loaded{i}"], 16)
            for w in range(4):
                sp_unit1(sp, UNITS1 // 4 - 1, w, True)
            sp_block1(sp, 0, 2, True, False)
            sp_block1(sp, 0, 3, True, False)
            with sp.Fori(0, NB1 // 2 - 3, 2) as h:
                for i in range(4):
                    sp_block1(sp, h, i + 4, True, True)
            for i in range(4):
                sp_block1(sp, NB1 // 2 - 2, i + 4, False, True)
            for i in range(2):
                sp.wait_ge(s[f"y1_stored{i}"], 8 * NB1 + 16)
            sp.dma_start(x1r.rearrange("p t c -> p (t c)"), x1d).then_inc(s["x1_loaded"], 16)
            for c in range(4):
                sp.wait_ge(s["mlp_done"], c + 1)
                sp.dma_start(out.rearrange("b (k p) c -> p (b k) c", p=P)[:, 4 * c:4 * c + 4], xn[:, 4 * c:4 * c + 4]).then_inc(s["out_stored"], 16)
            sp.wait_ge(s["x1_stored"], 16)
            sp.wait_ge(s["out_stored"], 64)

        def sp_block1(sp, h, i, load, store):
            if load:
                sp.wait_ge(s["x1t_ready"], h * 2 + i - 1)
                sp.dma_start(xb[:, i % 2, :], xs1[bass.ds(h * (2 * P) + i * P, P)]).then_inc(s[f"x1b_loaded{i % 2}"], 16)
            if store:
                sp.wait_ge(s["y1_ready"], h * 2 + i - 1)
                sp.dma_start(ys1[bass.ds(h * (2 * P) + (i - 4) * P, P)], yb[:, i % 2, :]).then_inc(s[f"y1_stored{i % 2}"], 16)

        def sp_slot_load(sp, unit, slot):
            q, k, u = slots[slot]
            for t, d in ((q, q1d), (k, k1d)):
                sp.dma_start(t[0:R1, u, :], d[bass.ds(unit * D1, D1)].rearrange("d j s -> (d j) s")).then_inc(s[f"slot_loaded{slot}"], 16)

        def sp_m1_rows(sp, unit, slot):
            sp.wait_ge(s["mt1_copied"], unit + 1)
            sp.dma_start(m1d[bass.ds(unit, 1)].rearrange("o r q -> (o r) q"), mrow[:, slot % 2, :]).then_inc(s["m1_stored"], 16)
            sp.wait_ge(s["m1_stored"], unit * 16 + 16)
            q, _, u = slots[slot]
            sp.dma_start(q[KPAD:KPAD + PARTS, u, :], m1d[bass.ds(unit, 1)].rearrange("o (j i) q -> (o j) (i q)", j=PARTS)).then_inc(s["m1_loaded"], 16)

        def sp_unit1(sp, g4, w, last):
            if not (last and w == 3):
                sp_m1_rows(sp, g4 * 4 + w + 1, (w + 1) % 4)
            if not last:
                sp.wait_ge(s["c1_ready"], g4 * 32 + w * 8 + 8)
                sp_slot_load(sp, g4 * 4 + w + 4, w)

        @block.sync
        def _(sp):
            x_rows = a["L0_attn_x"].rearrange("b (k p) c -> p (b k) c", p=P)
            for b in range(B):
                sp.dma_start(x_in[:, b * KT:(b + 1) * KT, :], x_rows[:, b * KT:(b + 1) * KT, :]).then_inc(s["x_loaded"], 16)
            for i, n in enumerate(("Wq", "Wk", "Wv")):
                sp.dma_start(wqkv[:, i, :].rearrange("p (n d) -> p n d", n=H0),
                             a["L0_attn_" + n].rearrange("n c d -> c n d")).then_inc(s["wqkv_loaded"], 16)
            sp.wait_ge(s["const"], 1)
            for h in range(H0):
                sp.dma_start(bd[h * D0:(h + 1) * D0, h * NQ:(h + 1) * NQ], a["L0_attn_Wc2q"][h]).then_inc(s["w_small0"], 16)
            for d in range(NB1 // 8):
                sp.dma_start(xs1[d * 1024:(d + 1) * 1024].rearrange("(p r) c -> p (r c)", p=P), zeros).then_inc(s["zeroed"], 16)
            for d in range(NB0 // 8):
                sp.dma_start(xs0[d * 1024:(d + 1) * 1024].rearrange("(p r) c -> p (r c)", p=P), zeros).then_inc(s["zeroed"], 16)
            sp.dma_start(gu_w.rearrange("p (e f) -> p e f", e=E0), a["L0_ffn_gate_up_proj"].rearrange("e c f -> c e f")).then_inc(s["gu_loaded"], 16)
            for t in range(2):
                for e in (0, 8):
                    sp.dma_start(dn_w.rearrange("p (e t c) -> p t e c", e=E0, t=2)[:, t, e:e + 8],
                                 a["L0_ffn_down_proj"].rearrange("e (t p) c -> p t e c", p=P)[:, t, e:e + 8]).then_inc(s["dn_loaded"], 16)
            for r in range(4):
                dst, rows = (q0d, k0d)[r % 2], (Q_ROWS, K_ROWS)[r % 2]
                sp.wait_ge(s["p3_ready"], r + 1)
                for j, n in enumerate(rows):
                    sp.dma_start(dst[(r // 2) * P:(r // 2 + 1) * P, j, :], part[r][:, n, :]).then_inc(s["qk_stored"], 16)
            sp.wait_ge(s["qk_stored"], 16 * NR * 4)
            sp_max_load(sp, 0)
            for r in range(4):
                dst, rows = (fq0d, fk0d)[r % 2], (Q_ROWS, K_ROWS)[r % 2]
                sp.wait_ge(s["p3_ready"], 4 + r + 1)
                for j, n in enumerate(rows):
                    sp.dma_start(dst[(r // 2) * 64:(r // 2 + 1) * 64, j, :], part[r][0:64, n, :]).then_inc(s["f_stored"], 16)
            sp.wait_ge(s["f_stored"], 16 * NR * 4)
            sp.wait_ge(s["flag_ready"], 1)
            for r in range(4):
                row = (r % 2) * UNITS0 + (r // 2) * H0
                sp.dma_start(n0d[row:row + H0].rearrange("h (k q) -> (h k) q", q=P), nT[:, r * P:(r + 1) * P]).then_inc(s["n_stored"], 16)
            sp.wait_ge(s["n_stored"], 64)
            flag = sp.value_load(flag_i[0:1, 0:1], min_val=0, max_val=1)
            sp.wait_ge(s["pad_cleared"], 1)
            sp_main_load(sp, 0)
            with sp.If(flag > 0):
                sp_norm_rows(sp, 0, 0)
            sp_m_rows(sp, 0, 0)
            sp.wait_ge(s["scattered"], 16 * NT)
            for i in range(2):
                sp_x_load(sp, 0, i)
            with sp.Fori(0, PAIRS0 - 1) as p:
                sp_pair(sp, p, flag, False)
            sp_pair(sp, PAIRS0 - 1, flag, True)
            sp.wait_ge(s["c_ready"], 16 * PAIRS0)
            sp.dma_start(wqo8, a["L0_attn_Wqo"]).then_inc(s["post_loaded"], 16)
            sp.dma_start(wm, a["L0_attn_Wm"].rearrange("(t p) q -> p t q", p=P)).then_inc(s["post_loaded"], 16)
            sp.dma_start(wo, a["L0_attn_Wo"]).then_inc(s["post_loaded"], 16)
            for t, n in ((bo_b, "bo"), (g1_b, "g1"), (be1_b, "beta1"), (g2_b, "g2"), (be2_b, "beta2"), (b2_b, "b2"), (bm_b, "bm")):
                sp.dma_start(t, a["L0_attn_" + n].partition_broadcast(P)).then_inc(s["post_loaded"], 16)
            sp.wait_ge(s["out_ready"], NBP * PAIRS0)
            for n, t in (("b1", b1_row), ("bqo", bqo_row)):
                sp.dma_start(t, a["L0_attn_" + n].rearrange("(o f) -> o f", o=1)).then_inc(s["post_loaded"], 16)
            for i in range(2):
                sp.wait_ge(s[f"y_stored{i}"], 8 * NBP * PAIRS0 + 16)
            for h in range(2):
                sp.dma_start(ysh[h], ys0[NB0 * P:].rearrange("(t p) c -> p t c", p=P)[:, h * KT:(h + 1) * KT]).then_inc(s["xsum"], 16)
            sp_weights1(sp)
            sp.wait_ge(s["res0_ready"], 1)
            sp.dma_start(x1d, xr.rearrange("p t c -> p (t c)")).then_inc(s["x1_stored"], 16)
            sp_layer1(sp)


        def pool_rstd(pool, n, eps):
            pool.wait_ge(s["ln_stats"], n + 1)
            pool_link(nc.gpsimd.tensor_scalar(ve[:], mv[:, :, 1], eps, None, ALU.add))
            nc.gpsimd.tensor_tensor(rstd[:], ve[:], minus_half[:, 0:NT], ALU.pow).then_inc(s["ln_rstd"], 1)

        def pool_m_split(pool, p, u):
            g = nc.gpsimd
            pool.wait_ge(s["f_free"], p * 32 + 8 * u + 10)
            neg, r1, r2 = msp[:, u, 0, :], msp[:, u, 1, :], msp[:, u, 2, :]
            one = sign[:, 1, 0:KT]
            steps = ((neg, M[:, u, :], sign[:, 0, 0:KT], ALU.mult),
                     (mpart[:, u, 0, :], neg, one, ALU.mult),
                     (r1, neg, mpart[:, u, 0, :], ALU.subtract),
                     (mpart[:, u, 1, :], r1, one, ALU.mult),
                     (r2, r1, mpart[:, u, 1, :], ALU.subtract),
                     (mpart[:, u, 2, :], r2, one, ALU.mult))
            for k, args in enumerate(steps):
                if k:
                    pool.wait_ge(s["m_split"], p * 12 + u * 6 + k)
                g.tensor_tensor(*args).then_inc(s["m_split"], 1)

        def pool_pair(pool, p, last):
            pool.wait_ge(s["pv_done"], p * 16 + 16)
            for u in range(2):
                nc.gpsimd.tensor_tensor(VU[:, u, :, 0:D0],
                                        Vc[:, bass.ds(p * (2 * KT * D0) + u * KT * D0, KT * D0)].rearrange("p (k d) -> p k d", d=D0),
                                        sign[:, 1, :].rearrange("p (k d) -> p k d", d=D0), ALU.mult)\
                    .then_inc(s["v_copied"], 1)
            if not last:
                for u in range(2):
                    pool_m_split(pool, p + 1, u)

        def pool_layer1(pool):
            g = nc.gpsimd
            pool_rstd(pool, 3, 1e-5)
            pool.wait_ge(s["ln_rstd"], 4)
            pool_link(g.tensor_tensor(ve[:], mv[:, :, 1], rstd[:], ALU.mult))
            pool_link(g.tensor_tensor(ve[:], ve[:], rstd[:], ALU.mult))
            pool_link(g.tensor_scalar(ve[:], ve[:], 1e-10, None, ALU.add))
            g.tensor_tensor(rstd2[:], ve[:], minus_half[:, 0:NT], ALU.pow).then_inc(s["ln_rstd"], 1)
            pool.wait_ge(s["wt1_ready"], 1)
            pool_link(g.memset(VU[:], 0.0))
            pool_link(g.memset(VU[:, :, :, D1:D1 + 1], 1.0))
            for tile in (QS, KS, QM, KM):
                for lo in (32, 64):
                    pool_link(g.memset(tile[lo:lo + 32, :, :], 0.0))
            pool_link(g.memset(KM[KPAD:P, :, :], 1.0))
            pool_link(g.memset(KS[KPAD:P, :, :], 1.0))
            g.sem_inc(s["vu1_cleared"], 1)
            pool.wait_ge(s["v1_done"], 4)
            pool_vu1(pool, 0, 0)
            for n in range(2):
                pool_m1_split(pool, n, n)
            pool.wait_ge(s["xsrc_ready"], 2)
            for n in range(8):
                pool_unit1(pool, n // 4, n % 4, False)
                for q in range(4 * n, 4 * n + 4):
                    t, k = q // 2, q % 2
                    g.indirect_dma_start(xs1, bass.IndirectOffsetOnAxis(ap=pos_i[:, k, t:t + 1], axis=0), xn[:, t, :], None)\
                        .then_inc(s["scattered1"], 16)
            with pool.Fori(2, UNITS1 // 4 - 1) as g4:
                for w in range(4):
                    pool_unit1(pool, g4, w, False)
            for w in range(4):
                pool_unit1(pool, UNITS1 // 4 - 1, w, True)
            pool.wait_ge(s["scattered1"], 16 * TOP1 * NT)
            g.tensor_tensor(xn[:], xn[:], bproj_b.unsqueeze(1).to_broadcast([P, NT, C]), ALU.add).then_inc(s["bproj_added"], 1)
            for i in range(2):
                pool.wait_ge(s[f"y1_stored{i}"], 8 * NB1 + 16)
            for t in range(NT):
                if t == 12:
                    pool_rstd(pool, 4, 1e-10)
                for k in range(TOP1):
                    g.indirect_dma_start(yg1[:, k, t, :], None, ys1, bass.IndirectOffsetOnAxis(ap=pos_i[:, k, t:t + 1], axis=0))\
                        .then_inc(s["gathered1"], 16)

        def pool_vu1(pool, unit, u):
            nc.gpsimd.tensor_tensor(VU[:, u, :, 0:D1], Vc[:, bass.ds(unit * (KT * D1), KT * D1)].rearrange("p (k d) -> p k d", d=D1),
                                    sign[:, 1, 0:KT * D1].rearrange("p (k d) -> p k d", d=D1), ALU.mult).then_inc(s["v1_copied"], 1)

        def pool_m1_split(pool, unit, u):
            g = nc.gpsimd
            u = u % 2
            pool.wait_ge(s["max1_whole"], unit + 1)
            neg, r1, r2, one = msp[:, u, 0, :], msp[:, u, 1, :], msp[:, u, 2, :], sign[:, 1, 0:KT]
            steps = ((neg, M[:, u, :], sign[:, 0, 0:KT], ALU.mult),
                     (mpart[:, u, 0, :], neg, one, ALU.mult),
                     (r1, neg, mpart[:, u, 0, :], ALU.subtract),
                     (mpart[:, u, 1, :], r1, one, ALU.mult),
                     (r2, r1, mpart[:, u, 1, :], ALU.subtract),
                     (mpart[:, u, 2, :], r2, one, ALU.mult))
            for k, args in enumerate(steps):
                if k:
                    pool.wait_ge(s["m1_split"], unit * 6 + k)
                g.tensor_tensor(*args).then_inc(s["m1_split"], 1)

        def pool_unit1(pool, g4, w, last):
            if not (last and w == 3):
                pool.wait_ge(s["pv1_done"], g4 * 32 + w * 8 + 8)
                pool_vu1(pool, g4 * 4 + w + 1, (w + 1) % 2)
            if not (last and w >= 2):
                pool_m1_split(pool, g4 * 4 + w + 2, w)

        @block.gpsimd
        def _(pool):
            g = nc.gpsimd
            pool_link(g.memset(bd[:], 0.0))
            g.memset(zeros, 0.0).then_inc(s["const"], 1)
            pool.wait_ge(s["const"], 1)
            for t, value in ((ident, 0.0), (identb, 0.0), (onesb, 1.0), (ones_e, 1.0), (ones_row, 1.0), (minus_half, -0.5),
                             (half_pi, math.pi / 2), (scan_keep, 1.0), (VU, 0.0), (lowb, 1.0), (scan_keep[:, :, 0:1], 0.0),
                             (VU[:, :, :, D0:D0 + 1], 1.0), (sign, 1.0), (sign[:, 0:1, :], -1.0), (KS[KPAD:P, :, :], 1.0)):
                pool_link(g.memset(t[:], value))
            for t, side in ((below, -1), (above, 1)):
                pool_link(g.memset(t[:], 0.0))
                pool_link(g.affine_select(out=t[:], in_=t[:], compare_op=ALU.is_ge, fill=NEG, base=0,
                                          pattern=[[side, P]], channel_multiplier=-side))
            for t in (ident, identb):
                pool_link(g.affine_select(out=t[:], in_=t[:], compare_op=ALU.not_equal, fill=1.0, base=0,
                                          pattern=[[-1, P]], channel_multiplier=1))
            pool_link(g.affine_select(out=lowb[:], in_=lowb[:], compare_op=ALU.is_gt, fill=0.0, base=0,
                                      pattern=[[1, P]], channel_multiplier=-1))
            pool_link(g.iota(iota_e[:], [[1, E0]], base=0, channel_multiplier=0, allow_small_or_imprecise_dtypes=True))
            g.iota(iota_b[:], [[1, NB1]], base=0, channel_multiplier=0, allow_small_or_imprecise_dtypes=True).then_inc(s["const"], 1)
            pool.wait_ge(s["const"], 2)
            pool_rstd(pool, 0, 1e-5)
            pool.wait_ge(s["ss_ready"], 4)
            pool.wait_ge(s["ln_rstd"], 1)
            for tile in (FQ, FK):
                for lo in (32, 64):
                    pool_link(g.memset(tile[lo:lo + 32, :, :], 0.0))
            g.sem_inc(s["pad_cleared"], 1)
            pool.wait_ge(s["zeroed"], 16 * (NB0 // 8 + NB1 // 8))
            pool.wait_ge(s["xsrc_ready"], 1)
            for t in range(NT):
                g.indirect_dma_start(xs0, bass.IndirectOffsetOnAxis(ap=pos_i[:, 0, t:t + 1], axis=0), x_in[:, t, :], None)\
                    .then_inc(s["scattered"], 16)
            for u in range(2):
                pool_m_split(pool, 0, u)
            with pool.Fori(0, PAIRS0 - 1) as p:
                pool_pair(pool, p, False)
            pool_pair(pool, PAIRS0 - 1, True)
            for i in range(2):
                pool.wait_ge(s[f"y_stored{i}"], 8 * NBP * PAIRS0 + 16)
            pool.wait_ge(s["xbT_ready"], NBP * PAIRS0)
            for t in range(NT):
                g.indirect_dma_start(yg[:, t, :], None, ys0, bass.IndirectOffsetOnAxis(ap=pos_i[:, 0, t:t + 1], axis=0))\
                    .then_inc(s["gathered"], 16)
            pool.wait_ge(s["pv_done"], 16 * PAIRS0 + 16)
            pool.wait_ge(s["post_loaded"], 16 * 14)
            g.tensor_tensor(x1p, xn[:], bo_b.unsqueeze(1).to_broadcast([P, NT, C]), ALU.add).then_inc(s["bo_added"], 1)
            pool.wait_ge(s["prep_done"], 3)
            for base, mul, step in ((0, 1, -NQ), (NQ - 1, -1, NQ)):
                pool_link(g.affine_select(out=bdq, in_=bdq, compare_op=ALU.is_ge, fill=0.0, base=base,
                                          pattern=[[step, NT], [0, C]], channel_multiplier=mul))
            g.sem_inc(s["bd_masked"], 1)
            pool_rstd(pool, 1, 1e-5)
            pool.wait_ge(s["gathered"], 16 * NT)
            pool.wait_ge(s["xsum"], 64)
            for h in range(2):
                pool_link(g.tensor_tensor(yg[:, h * KT:(h + 1) * KT], yg[:, h * KT:(h + 1) * KT], ysh[h], ALU.add))
            g.tensor_tensor(xr, xr, yg, ALU.add).then_inc(s["xsum"], 1)
            pool_rstd(pool, 2, 1e-5)
            pool_layer1(pool)

        mm, tr = nc.tensor.matmul, nc.tensor.transpose

        def pe_transposes(pe, src, n):
            for c in range(4):
                pe.wait_ge(s["ln_done"], 4 * n + c + 1)
                for k in range(4):
                    last = tr(bank(c)[:, k * P:(k + 1) * P], src[:, 4 * c + k, :], ident[:])
                last.then_inc(s["tr_ready"], 1)

        def pe_project(pe, r):
            if r >= 2:
                pe.wait_ge(s["qf_ready"], r - 1)
            for half in range(2):
                col = (r // 2) * S + half * 512
                last = mm(bank(4 + 2 * (r % 2) + half), wqkv[:, r % 2, :], xT[:, col:col + 512], start=True, stop=True)
            last.then_inc(s["proj_ready"], 1)

        def pe_rank(pe, n, E, b=1):
            pe.wait_ge(s["oh_ready"], n + 1)
            mm(bank(b)[:, 0:NT * E], lowb[:], oh_b[:, 0:NT * E], start=True, stop=True)
            mm(bank(b)[:, NT * E:2 * NT * E], onesb[:], oh_b[:, 0:NT * E], start=True, stop=True).then_inc(s["rank_ready"], 1)

        def pe_max(pe, p, n):
            u, i = n // 8, n % 8
            if n == 0:
                pe.wait_ge(s["max_loaded"], p * 32 + 32)
            pe.wait_ge(s["f_free"], p * 32 + n + 1)
            for half in range(2):
                last = mm(bank(FB[n % 2] + half), QM[0:R0, u, i * P:(i + 1) * P],
                          KM[0:R0, u, half * 512:(half + 1) * 512], start=True, stop=True)
            last.then_inc(s["f_ready"], 1)

        def pe_mt(pe, p, u):
            pe.wait_ge(s["m_split"], p * 12 + u * 6 + 6)
            tr(bank(7 - u).bitcast(BF16)[0:PARTS * KT, 0:P],
               mpart[:, u, :, :].rearrange("p j i -> p (j i)"), identb[:]).then_inc(s["mt_ready"], 1)

        def pe_fid(pe, p, n, guard):
            u, k = n // 8, n % 8
            rows = RF if guard else KPAD
            pe.wait_ge(s["f_free"], p * 32 + n + 17)
            for half in range(2):
                last = mm(bank(FB[n % 2] + half), FK[0:rows, u, k * P:(k + 1) * P], FQ[0:rows, u, half * 512:(half + 1) * 512],
                          start=True, stop=True)
            last.then_inc(s["f_ready"], 1)

        def pe_guard(pe, p, n):
            u, k = n // 8, n % 8
            if k == 0:
                pe.wait_ge(s["n_loaded"], p * 64 + u * 32 + 32)
            pe.wait_ge(s["z_done"], p * 16 + max(n, 1))
            for half in range(2):
                last = mm(bank(2 + half), FKf[NROW:NROW + 1, k * P:(k + 1) * P], FQf[NROW:NROW + 1, half * 512:(half + 1) * 512],
                          start=True, stop=True)
            last.then_inc(s["g_ready"], 1)
            pe.wait_ge(s["g_done"], p * 16 + n + 1)

        def pe_phase_a(pe, p, guard, last_pair):
            expert = {}
            ahead = 1 if guard else AHEAD
            for n in range(ahead):
                pe_fid(pe, p, n, guard)
                if guard:
                    pe_guard(pe, p, n)
            for n in range(16):
                u, k = n // 8, n % 8
                if n + ahead < 16:
                    pe_fid(pe, p, n + ahead, guard)
                    if guard:
                        pe_guard(pe, p, n + 1)
                elif not last_pair:
                    pe_max(pe, p + 1, n + ahead - 16)
                if k == 0:
                    pe.wait_ge(s["m_loaded"], p * 32 + 16 * u + 16)
                pe.wait_ge(s["z_done"], p * 16 + n + 1)
                for half in range(2):
                    last = mm(bank(2 + half), KS[0:R0 + PARTS, u, k * P:(k + 1) * P],
                              QS[0:R0 + PARTS, u, half * 512:(half + 1) * 512], start=True, stop=True)
                last.then_inc(s["c_ready"], 1)
                if n == 0:
                    pe.wait_ge(s["pv_evac"], p * 2 + 1)
                    pe_mt(pe, p, 1)
                pe_block(pe, p, n, expert)
            if not last_pair:
                for n in range(ahead, AHEAD):
                    pe_max(pe, p + 1, n)

        def pe_pair(pe, p, flag, last_pair):
            pe.wait_ge(s["main_loaded"], p * 64 + 64)
            with pe.If(flag > 0):
                pe_phase_a(pe, p, True, last_pair)
            with pe.Else():
                pe_phase_a(pe, p, False, last_pair)
            for u in range(2):
                pe.wait_ge(s["v_copied"], p * 2 + u + 1)
            for n in range(16):
                if not last_pair and n + AHEAD < 16:
                    pe_max(pe, p + 1, n + AHEAD)
                u, k = n // 8, n % 8
                pe.wait_ge(s["exp_done"], p * 16 + n + 1)
                if k == 0:
                    pe.wait_ge(s["pv_evac"], p * 2 + u + 1)
                for j in range(4):
                    last = mm(bank(6)[32 * j:32 * j + 32, 0:256], VU[:, u, k, :], Zt(u, k)[:, 256 * j:256 * (j + 1)],
                              start=(k == 0), stop=(k == KT - 1), tile_position=(0, 32 * j))
                last.then_inc(s["pv_done"], 1)
                if n + AHEAD == 9 and not last_pair:
                    pe.wait_ge(s["yb_ready"], p * NBP + NBP)
                    pe_mt(pe, p + 1, 0)

        def pe_block(pe, p, n, expert):
            i = (n - 3) // 2
            if n % 2 == 1 and 0 <= i < NBP:
                pe.wait_ge(s["hT_done"], p * NBP + i + 1)
                pe.wait_ge(s["xbT_ready"], p * NBP + min(i + 2, NBP))
                if i >= 1:
                    pe.wait_ge(s["yb_ready"], p * NBP + i)
                for t in range(2):
                    w = dn_w[:, bass.ds(expert[i] * (2 * C) + t * C, C)] if i < XB else dnT[:, t, :]
                    last = mm(bank(7)[:, 256:256 + C], hT[:, i % 2, t * P:(t + 1) * P], w, start=(t == 0), stop=(t == 1))
                last.then_inc(s["out_ready"], 1)
            i = (n - 2) // 2
            if n % 2 == 0 and 0 <= i < NBP:
                pe.wait_ge(s["h_ready"], p * NBP + i + 1)
                for t in range(2):
                    last = tr(bank(6)[:, t * P:(t + 1) * P], hb[:, i % 2, t * P:(t + 1) * P], ident[:])
                last.then_inc(s["ht_ready"], 1)
            i = n // 2
            if n % 2 == 0 and i < XB:
                pe.wait_ge(s[f"xb_loaded{i % 2}"], p * (8 * XB) + 16 * (i // 2) + 16)
                if i == 0:
                    pe.wait_ge(s["mt_copied"], p * 2 + 1)
                else:
                    pe.wait_ge(s["xbT_ready"], p * NBP + i)
                if i >= 2:
                    pe.wait_ge(s["yb_ready"], p * NBP + i - 1)
                tr(bank(7)[:, 0:P], xb[:, i % 2, :], ident[:]).then_inc(s["xt_ready"], 1)
            i = (n - 1) // 2
            if n % 2 == 1 and i < NBP:
                if i < XB:
                    expert[i] = pe.value_load(eb_i[0:1, bass.ds(p * XB + i, 1)], min_val=0, max_val=E0 - 1)
                pe.wait_ge(s["xbT_ready"], p * NBP + i + 1)
                if i == 0:
                    pe.wait_ge(s["mt_copied"], p * 2 + 2)
                else:
                    pe.wait_ge(s["hT_done"], p * NBP + i)
                if i < XB:
                    w = gu_w[:, bass.ds(expert[i] * (2 * F0), 2 * F0)]
                else:
                    w = guT[:]
                mm(bank(6), xbT[:, i % 2, :], w, start=True, stop=True).then_inc(s["gu_ready"], 1)

        def pe_post0(pe):
            pe.wait_ge(s["post_loaded"], 16 * 14)
            pe.wait_ge(s["prep_done"], 1)
            pe.wait_ge(s["pv_evac"], 2 * PAIRS0 + 1)
            for c in range(4):
                tr(bank(4)[:, c * P:(c + 1) * P], w1r[:, c * P:(c + 1) * P], ident[:])
            for c in range(4):
                mm(bank(5)[:, c * P:(c + 1) * P], wqo8[:, c * P:(c + 1) * P], rep8, start=True, stop=True)
            for c in range(8):
                last = mm(bank(6 + c // 4)[:, (c % 4) * P:(c % 4 + 1) * P], (b1_row if c < 4 else bqo_row)[:, (c % 4) * P:(c % 4 + 1) * P],
                          ones_row[:], start=True, stop=True)
            last.then_inc(s["prep_ready"], 1)
            for n in range(8):
                b, hf, hg = n // 4, (n // 2) % 2, n % 2
                if n >= 4:
                    pe.wait_ge(s["o_done"], n - 3)
                for h in range(4):
                    last = tr(bank(n % 4)[:, h * P:(h + 1) * P], OT[:, b * H0 + hg * 4 + h, hf * P:(hf + 1) * P], ident[:])
                last.then_inc(s["o_ready"], 1)
            pe.wait_ge(s["prep_done"], 2)
            for c in range(4):
                mm(bank(6)[:, 0:NQ], w1T[:, c * P:(c + 1) * P], wm[:, c, :], start=(c == 0), stop=(c == 3))
            for c in range(4):
                mm(bank(6)[:, 8:8 + NQ], repcol[:, c * P:(c + 1) * P], wm[:, c, :], start=(c == 0), stop=(c == 3))
            for c in range(4):
                mm(bank(7)[:, 0:P], qoT[:, c * P:(c + 1) * P], w2r[:, c, :], start=(c == 0), stop=(c == 3))
            for c in range(4):
                last = mm(bank(7)[:, P:2 * P], repcol[:, 512 + c * P:512 + (c + 1) * P], w2r[:, c, :], start=(c == 0), stop=(c == 3))
            last.then_inc(s["prep_ready"], 1)
            pe.wait_ge(s["o_done"], 8)
            pe_transposes(pe, attn, 0)
            for c in range(4):
                pe.wait_ge(s["tr_done"], 4 + c + 1)
                for k in range(4):
                    last = mm(bank(c)[:, k * P:(k + 1) * P], attnT[:, (4 * c + k) * P:(4 * c + k + 1) * P], wo, start=True, stop=True)
                last.then_inc(s["wo_ready"], 1)
            pe.wait_ge(s["wo_done"], 4)
            pe_transposes(pe, x1, 1)
            pe.wait_ge(s["prep_done"], 3)
            for t in range(NT):
                if t % 4 == 0:
                    pe.wait_ge(s["tr_done"], 8 + t // 4 + 1)
                last = mm(bank(4)[:, t * NQ:(t + 1) * NQ], attnT[:, t * P:(t + 1) * P], w1m, start=True, stop=True)
            last.then_inc(s["qm_ready"], 1)
            pe.wait_ge(s["qe_ready"], 1)
            tr(bank(5)[:, 0:P], qe, ident[:]).then_inc(s["qeT_ready"], 1)
            pe.wait_ge(s["qeT_done"], 1)
            pe.wait_ge(s["bd_masked"], 1)
            for c in range(4):
                mm(bank(c), qeT, bdq[:, 4 * c:4 * c + 4, :].rearrange("p t c -> p (t c)"), start=True, stop=True).then_inc(s["ff_ready"], 1)

        def pe_layer1(pe):
            pe.wait_ge(s["l1_loaded"], 16 * L1_LOADS)
            pe.wait_ge(s["res0_ready"], 1)
            for i in range(12):
                tr(bank(4 + i // 4)[:, (i % 4) * P:(i % 4 + 1) * P], W1[:, i * P:(i + 1) * P], ident[:])
            for i in range(6):
                last = mm(bank(7)[:, i:i + 1], brow1[:, i * P:(i + 1) * P], ones_row[:, 0:1], start=True, stop=True)
            last.then_inc(s["wt1_ready"], 1)
            pe_transposes(pe, xn[:], 3)
            pe.wait_ge(s["tr_done"], 16)
            pe_transposes(pe, lx, 4)
            pe.wait_ge(s["wt1_done"], 1)
            for c in range(4):
                pe.wait_ge(s["tr_done"], 16 + c + 1)
                for k in range(4):
                    last = mm(bank(c)[:, k * P:(k + 1) * P], lxT[:, (4 * c + k) * P:(4 * c + k + 1) * P], wqkv[:, 2, :], start=True, stop=True)
                last.then_inc(s["v1_ready"], 1)
            for r in range(4):
                pe_project1(pe, r)
            pe.wait_ge(s["v1_done"], 4)
            pe.wait_ge(s["qf_ready"], 8)
            for t in range(NT):
                last = mm(bank(6)[:, t * E1:(t + 1) * E1], xT[:, t * P:(t + 1) * P], rw1, start=True, stop=True)
            last.then_inc(s["lg1_ready"], 1)
            for c in range(12):
                pe_max1(pe, 0, 0, c, 32)
            pe_mt1(pe, 0, 0)
            pe.wait_ge(s["mt1_copied"], 1)
            for c in range(12):
                pe_max1(pe, 1, 1, c, 32)
            pe_rank(pe, 1, E1, 6)
            for w in range(4):
                pe_unit1(pe, 0, w, False)
            with pe.Fori(1, UNITS1 // 4 - 1) as g4:
                for w in range(4):
                    pe_unit1(pe, g4, w, False)
            for w in range(4):
                pe_unit1(pe, UNITS1 // 4 - 1, w, True)
            pe_pv1(pe, UNITS1 - 1, 3, KT - 1)
            pe.wait_ge(s["head1_out"], UNITS1 + 1)
            pe.wait_ge(s["x1b_loaded0"], 16)
            tr(bank(4)[:, 0:P], xb[:, 0, :], ident[:]).then_inc(s["x1t_ready"], 1)
            known = {}
            pe_step1(pe, 0, 0, known, hid=False, res=False)
            pe_step1(pe, 0, 1, known, res=False)
            with pe.Fori(0, NB1 // 2 - 3, 2) as h:
                known = {}
                for i in range(4):
                    pe_step1(pe, h, i + 2, known)
            known = {}
            for i in range(4):
                pe_step1(pe, NB1 // 2 - 2, i + 2, known, gu=i < 2, hid=i < 3, nxt=i < 1)
            pe.wait_ge(s["y1_ready"], NB1 + 2)
            for n in range(16):
                b, hf, hg = n // 8, (n // 4) % 2, n % 4
                if n >= 4:
                    pe.wait_ge(s["o1n_done"], n - 3)
                for h in range(4):
                    last = tr(bank(n % 4)[:, h * P:(h + 1) * P], OT1[:, b * H1 + hg * 4 + h, hf * P:(hf + 1) * P], ident[:])
                last.then_inc(s["o1t_ready"], 1)
            pe.wait_ge(s["o1n_done"], 16)
            pe_transposes(pe, attn, 4)
            for c in range(4):
                pe.wait_ge(s["tr_done"], 20 + c + 1)
                for k in range(4):
                    last = mm(bank(c)[:, k * P:(k + 1) * P], attnT[:, (4 * c + k) * P:(4 * c + k + 1) * P], wprojT, start=True, stop=True)
                last.then_inc(s["proj1_ready"], 1)
            pe_transposes(pe, lx2, 5)
            for n in range(16):
                f, c = n % 4, n // 4
                if f == 0:
                    pe.wait_ge(s["tr_done"], 24 + c + 1)
                if n >= 4:
                    pe.wait_ge(s["fc_done"], n - 3)
                mm(bank(4 + n % 4), wfcT[:, f * P:(f + 1) * P], attnT[:, c * 512:(c + 1) * 512], start=True, stop=True).then_inc(s["fc_ready"], 1)
            for c in range(4):
                pe.wait_ge(s["fc_done"], 4 * c + 4)
                for k in range(4):
                    t = 4 * c + k
                    for f in range(4):
                        last = mm(bank(c)[:, k * P:(k + 1) * P], HT[:, f, t * P:(t + 1) * P], wmlpT[:, f * P:(f + 1) * P], start=(f == 0), stop=(f == 3))
                last.then_inc(s["mlp_ready"], 1)

        def pe_project1(pe, r):
            if r >= 2:
                pe.wait_ge(s["qf_ready"], 4 + r - 1)
            for half in range(2):
                col = (r // 2) * S + half * 512
                last = mm(bank(4 + 2 * (r % 2) + half), wqkv[:, r % 2, :], lxT[:, col:col + 512], start=True, stop=True)
            last.then_inc(s["proj_ready"], 1)

        def pe_max1(pe, unit, slot, c, loads):
            q, k, u = slots[slot]
            if c == 0:
                pe.wait_ge(s[f"slot_loaded{slot}"], loads)
            i, half = MAX_CHUNKS[c]
            lo, hi = 512 * half, min(512 * half + 512, (i + 1) * P)
            o = bank(MB[c % 3])
            diagonal = hi == (i + 1) * P
            pe.wait_ge(s["max1_free"], unit * 12 + c + 1)
            last = mm(o[:, 0:hi - lo], q[0:KPAD, u, i * P:(i + 1) * P], k[0:KPAD, u, lo:hi], start=True, stop=not diagonal)
            if diagonal:
                last = mm(o[:, hi - lo - P:hi - lo], identb[:], below[:], start=False, stop=True)
            last.then_inc(s["max1_ready"], 1)

        def pe_mt1(pe, unit, slot):
            pe.wait_ge(s["m1_split"], unit * 6 + 6)
            tr(bank(MB[MT % 3]).bitcast(BF16)[0:PARTS * KT, 0:P],
               mpart[:, slot % 2, :, :].rearrange("p j i -> p (j i)"), identb[:]).then_inc(s["mt1_ready"], 1)

        def pe_pv1(pe, unit, slot, k):
            pe.wait_ge(s["p1_done"], unit * 8 + k + 3)
            if k == 0:
                pe.wait_ge(s["v1_copied"], unit + 1)
                if isinstance(unit, int) and unit == 0:
                    pe.wait_ge(s["pos_ready"], 2)
                pe.wait_ge(s["head1_out"], unit + 1)
            for j in range(k // 2, 4):
                lo = max(256 * j, P * k)
                last = mm(bank(6)[32 * j:32 * j + 32, lo - 256 * j:256], VU[:, slot % 2, k, :], Z[:, k * S + lo:k * S + 256 * (j + 1)],
                          start=(k == 0), stop=(k == 2 * j + 1), tile_position=(0, 32 * j))
            last.then_inc(s["pv1_done"], 1)

        def pe_unit1(pe, g4, w, last_group):
            unit = g4 * 4 + w
            q, kk, u = slots[w]
            maxima = not (last_group and w >= 2)
            c = 0
            for k in range(KT):
                if k < MAX_STEPS[0]:
                    if maxima:
                        pe_max1(pe, unit + 2, (w + 2) % 4, c, g4 * 32 + (w + 2) // 4 * 32 + 32)
                    c += 1
                if c == MT and not (last_group and w == 3):
                    pe.wait_ge(s["max1_free"], (unit + 2) * 12 + MT + 1 if maxima else UNITS1 * 12 + 3)
                    pe_mt1(pe, unit + 1, w + 1)
                if k == 0:
                    pe.wait_ge(s["m1_loaded"], unit * 16 + 16)
                b0 = 2 + 2 * (k % 2)
                pe.wait_ge(s["p1_done"], unit * 8 + k + 1)
                for lo, hi in ((P * k, 512), (max(P * k, 512), S)):
                    if lo < hi:
                        last = mm(bank(b0, 2)[:, lo:hi], kk[0:KPAD + PARTS, u, k * P:(k + 1) * P], q[0:KPAD + PARTS, u, lo:hi],
                                  start=True, stop=lo != P * k)
                        if lo == P * k:
                            last = mm(bank(b0, 2)[:, lo:lo + P], identb[:], above[:], start=False, stop=True)
                last.then_inc(s["c1_ready"], 1)
                if k >= 1:
                    pe_pv1(pe, unit, w, k - 1)
                elif not (isinstance(g4, int) and g4 == w == 0):
                    pe_pv1(pe, unit - 1, w + 1, KT - 1)
                if k < MAX_STEPS[1]:
                    if maxima:
                        if c == MT:
                            pe.wait_ge(s["mt1_copied"], unit + 2)
                        pe_max1(pe, unit + 2, (w + 2) % 4, c, 0)
                    c += 1

        def block_expert1(eng, h, i, known):
            if i not in known:
                known[i] = eng.value_load(eb_i[0:1, bass.ds(h * 2 + i, 1)], min_val=0, max_val=E1 - 1)
            return known[i]

        def pe_step1(pe, h, i, known, gu=True, hid=True, nxt=True, res=True):
            if gu:
                expert = block_expert1(pe, h, i, known)
                pe.wait_ge(s["x1t_done"], h * 2 + i + 1)
                mm(bank(i % 2), xbT[:, i % 2, :], w1_all[:, bass.ds(expert * F1, F1)], start=True, stop=True).then_inc(s["gu1_ready"], 1)
            if nxt:
                pe.wait_ge(s[f"x1b_loaded{(i + 1) % 2}"], h * 16 + 16 * ((i + 1) // 2) + 16)
                tr(bank(4)[:, 0:P], xb[:, (i + 1) % 2, :], ident[:]).then_inc(s["x1t_ready"], 1)
            if hid:
                pe.wait_ge(s["h1_ready"], h * 2 + i)
                for t in range(4):
                    last = tr(bank(2 + (i + 1) % 2)[:, t * P:(t + 1) * P], hb1[:, (i + 1) % 2, t * P:(t + 1) * P], ident[:])
                last.then_inc(s["h1t_ready"], 1)
            if res:
                expert = block_expert1(pe, h, i - 2, known)
                pe.wait_ge(s["h1t_done"], h * 2 + i - 1)
                pe.wait_ge(s["y1_ready"], h * 2 + i - 1)
                for t in range(4):
                    last = mm(bank(5 + i % 2)[:, 0:C], hT1[:, i % 2, t * P:(t + 1) * P], w2_all[:, bass.ds(expert * F1 + t * C, C)],
                              start=(t == 0), stop=(t == 3))
                last.then_inc(s["o1_ready"], 1)

        @block.tensor
        def _(pe):
            pe.wait_ge(s["const"], 2)
            pe.wait_ge(s["w_raw0"], 16 * 4)
            for i in range(4):
                tr(bank(4)[:, i * P:(i + 1) * P], wst[:, i * P:(i + 1) * P], ident[:])
            for i in range(2):
                tr(bank(5)[:, i * P:(i + 1) * P], wst[:, 512 + i * P:512 + (i + 1) * P], ident[:])
            pe.wait_ge(s["w_small0"], 16 * 12)
            for i in range(2):
                mm(bank(5)[:, 272 + i:273 + i], bqk_row[:, i * P:(i + 1) * P], ones_row[:, 0:1], start=True, stop=True)
            tr(bank(5)[:, 256:256 + E0], wst[0:E0, 768:768 + P], ident[0:E0, 0:E0]).then_inc(s["wt_ready"], 1)
            pe_transposes(pe, xn[:], 0)
            pe.wait_ge(s["wqkv_loaded"], 48)
            pe.wait_ge(s["tr_done"], 4)
            for c in range(4):
                for k in range(4):
                    last = mm(bank(c)[:, k * P:(k + 1) * P], xT[:, (4 * c + k) * P:(4 * c + k + 1) * P], wqkv[:, 2, :], start=True, stop=True)
                last.then_inc(s["v_ready"], 1)
            pe.wait_ge(s["wt_done"], 1)
            pe_project(pe, 0)
            pe_project(pe, 1)
            pe.wait_ge(s["v_done"], 1)
            for t in range(NT):
                last = mm(bank(0)[:, t * E0:(t + 1) * E0], xT[:, t * P:(t + 1) * P], rout[:], start=True, stop=True)
            last.then_inc(s["lg_ready"], 1)
            pe_project(pe, 2)
            pe_project(pe, 3)
            pe.wait_ge(s["w_small0"], 16 * 12)
            pe.wait_ge(s["v_done"], 4)
            pe_rank(pe, 0, E0)
            for r in range(4):
                if r >= 2:
                    pe.wait_ge(s["ss_ready"], r - 1)
                for k in range(KT):
                    last = mm(bank(2 + r % 2)[:, k * 64:(k + 1) * 64], qf[r][:, k * P:(k + 1) * P], bd[:], start=True, stop=True)
                last.then_inc(s["qq_ready"], 1)
            for r in range(4):
                pe.wait_ge(s["qh_ready"], r + 1)
                if r < 2:
                    pe.wait_ge(s["qf_ready"], r + 3)
                else:
                    pe.wait_ge(s["hatT_ready"], r - 1)
                for k in range(KT):
                    last = tr(bank(4 + 2 * (r % 2), 2)[0:64, k * P:(k + 1) * P], qq[r][:, k * 64:(k + 1) * 64], ident[:])
                last.then_inc(s["hat_ready"], 1)
            pe.wait_ge(s["nrm_ready"], 1)
            for r in range(4):
                tr(bank(2)[0:64, r * P:(r + 1) * P], nrm[:, r * 64:(r + 1) * 64], ident[:])
            mm(bank(3)[0:1, 0:1], small[:, 0:1], ones_e[:, 0:1], start=True, stop=True).then_inc(s["nt_ready"], 1)
            pe.wait_ge(s["pos_ready"], 1)
            pe.wait_ge(s["hatT_ready"], 4)
            for n in range(16):
                pe_max(pe, 0, n)
            pe_mt(pe, 0, 0)
            pe.wait_ge(s["gu_loaded"], 16)
            pe.wait_ge(s["dn_loaded"], 64)
            pe.wait_ge(s["flag_ready"], 1)
            flag = pe.value_load(flag_i[0:1, 0:1], min_val=0, max_val=1)
            with pe.Fori(0, PAIRS0 - 1) as p:
                pe_pair(pe, p, flag, False)
            pe_pair(pe, PAIRS0 - 1, flag, True)
            pe_post0(pe)
            pe_layer1(pe)


        def act(out_, in_, f=ACT.Copy, **kw):
            return nc.scalar.activation(out_, in_, f, **kw)

        def act_transposed(ac, dst, n):
            for c in range(4):
                ac.wait_ge(s["tr_ready"], 4 * n + c + 1)
                act(dst[:, c * 512:(c + 1) * 512], bank(c)).then_inc(s["tr_done"], 1)

        def act_sin(ac, p, n, guard):
            ac.wait_ge(s["f_ready"], p * 32 + n + 17)
            if guard:
                ac.wait_ge(s["g_done"], p * 16 + n + 1)
            act(snb[:, n % 2, :], bank(FB[n % 2], 2), ACT.Sin, scale=PI_IN).then_inc(s["sin_done"], 1)

        def act_phase_a(ac, p, guard):
            ahead = 1 if guard else AHEAD
            for n in range(ahead):
                act_sin(ac, p, n, guard)
            if not (isinstance(p, int) and p == 0):
                act_head_out(ac, p - 1, 1)
            for n in range(16):
                if n + ahead < 16:
                    act_sin(ac, p, n + ahead, guard)
                act_block(ac, p, n)

        def act_pair(ac, p, flag):
            with ac.If(flag > 0):
                act_phase_a(ac, p, True)
            with ac.Else():
                act_phase_a(ac, p, False)
            for n in range(16):
                u, k = n // 8, n % 8
                ac.wait_ge(s["z_done"], p * 16 + n + 2)
                act(Zt(u, k), Zt(u, k), ACT.Exp, scale=0.05).then_inc(s["exp_done"], 1)
                if n == 3:
                    act_block_out(ac, p, NBP - 1)
            act_head_out(ac, p, 0)

        def act_head_out(ac, p, u):
            ac.wait_ge(s["pv_done"], p * 16 + 8 * u + 24)
            act(OT[:, bass.ds(p * 2 + u, 1), :], bank(6)[:, 0:256].unsqueeze(1)).then_inc(s["pv_evac"], 1)

        def act_block_out(ac, p, i):
            ac.wait_ge(s["out_ready"], p * NBP + i + 1)
            ac.wait_ge(s[f"y_stored{i % 2}"], p * (8 * NBP) + 16 * (i // 2) + 16)
            act(yb[:, i % 2, :], bank(7)[:, 256:256 + C]).then_inc(s["yb_ready"], 1)

        def act_block(ac, p, n):
            i = (n - 3) // 2
            if n % 2 == 1 and 0 <= i < NBP - 1:
                act_block_out(ac, p, i)
            i = (n - 2) // 2
            if n % 2 == 0 and 0 <= i < NBP:
                ac.wait_ge(s["ht_ready"], p * NBP + i + 1)
                act(hT[:, i % 2, :], bank(6)[:, 0:F0]).then_inc(s["hT_done"], 1)
            i = n // 2
            if n % 2 == 0 and i < NBP:
                if i < XB:
                    ac.wait_ge(s["xt_ready"], p * XB + i + 3)
                    src = bank(7)[:, 0:P]
                else:
                    src = xT[:, bass.ds(p * (SHB * P) + (i - XB) * P, P)]
                    ac.wait_ge(s["gu_ready"], p * NBP + i - 1)
                act(xbT[:, i % 2, :], src).then_inc(s["xbT_ready"], 1)
            i = (n - 1) // 2
            if n % 2 == 1 and i < NBP:
                ac.wait_ge(s["gu_ready"], p * NBP + i + 1)
                act(sg[:], bank(6)[:, 0:F0], ACT.Silu).then_inc(s["silu_done"], 1)

        def act_split(ac, layer, bias):
            for r in range(5):
                if r < 4:
                    scale = QSCALE0 if layer == 0 and r % 2 == 0 else 1.0
                    ac.wait_ge(s["proj_ready"], 4 * layer + r + 1)
                    act(qf[r], bank(4 + 2 * (r % 2), 2), ACT.Identity, bias=bias[:, r % 2:r % 2 + 1]).then_inc(s["qf_ready"], 1)
                    ac.wait_ge(s["qf_ready"], 4 * layer + r + 1)
                    act(part[r][:, 0, :], qf[r], scale=scale).then_inc(s["p1_ready"], 1)
                if r >= 1:
                    ac.wait_ge(s["res_ready"], 8 * layer + r)
                    act(part[r - 1][:, 1, :], res[r - 1]).then_inc(s["p2_ready"], 1)

        def act_layer1(ac):
            ac.wait_ge(s["wt1_ready"], 1)
            act(wqkv[:, :, :].rearrange("p i c -> p (i c)"), bank(4)[:, 0:384])
            act(wprojT, bank(4)[:, 384:512])
            act(wfcT, bank(5))
            act(wmlpT, bank(6))
            act(bcols, bank(7)[:, 0:6]).then_inc(s["wt1_done"], 1)
            act_transposed(ac, xT, 3)
            act_transposed(ac, lxT, 4)
            ac.wait_ge(s["wt1_done"], 1)
            act_split(ac, 1, bcols)
            ac.wait_ge(s["gate_ready"], 1)
            act(score[:, 1, :], score[:, 0, :], ACT.Exp).then_inc(s["gates_done"], 1)
            for w in range(4):
                act_unit1(ac, 0, w)
            with ac.Fori(1, UNITS1 // 4) as g4:
                for w in range(4):
                    act_unit1(ac, g4, w)
            act_head1_out(ac, UNITS1 - 1)
            ac.wait_ge(s["x1t_ready"], 1)
            act(xbT[:, 0, :], bank(4)[:, 0:P]).then_inc(s["x1t_done"], 1)
            act_step1(ac, 0, 0, hid=False)
            act_step1(ac, 0, 1)
            with ac.Fori(0, NB1 // 2 - 3, 2) as h:
                for i in range(4):
                    act_step1(ac, h, i + 2)
            for i in range(3):
                act_step1(ac, NB1 // 2 - 2, i + 2, gu=i < 2, hid=i < 3, nxt=i < 1)
            act_transposed(ac, attnT, 5)
            act_transposed(ac, attnT, 6)
            for n in range(16):
                f, c = n % 4, n // 4
                ac.wait_ge(s["fc_ready"], n + 1)
                act(HT[:, f, c * 512:(c + 1) * 512], bank(4 + n % 4), ACT.Gelu_apprx_tanh, bias=bcols[:, 2 + f:3 + f]).then_inc(s["fc_done"], 1)

        def act_unit1(ac, g4, w):
            for k in range(KT):
                ac.wait_ge(s["c1_ready"], g4 * 32 + w * 8 + k + 1)
                ac.wait_ge(s["pv1_done"], g4 * 32 + w * 8 + k + 1)
                act(Z[:, k * S + k * P:(k + 1) * S], bank(2 + 2 * (k % 2), 2)[:, k * P:S], ACT.Exp, scale=1 / math.sqrt(D1))\
                    .then_inc(s["p1_done"], 1)
                if k == 0 and not (isinstance(g4, int) and w == 0):
                    act_head1_out(ac, g4 * 4 + w - 1)

        def act_head1_out(ac, unit):
            ac.wait_ge(s["pv1_done"], unit * 8 + 16)
            act(OT1[:, bass.ds(unit, 1), :], bank(6)[:, 0:256].unsqueeze(1)).then_inc(s["head1_out"], 1)

        def act_step1(ac, h, i, gu=True, hid=True, nxt=True):
            if nxt:
                ac.wait_ge(s["x1t_ready"], h * 2 + i + 2)
                act(xbT[:, (i + 1) % 2, :], bank(4)[:, 0:P]).then_inc(s["x1t_done"], 1)
            if hid:
                ac.wait_ge(s["h1t_ready"], h * 2 + i)
                act(hT1[:, (i + 1) % 2, :], bank(2 + (i + 1) % 2)).then_inc(s["h1t_done"], 1)
            if gu:
                ac.wait_ge(s["b1_added"], h * 2 + i + 1)
                act(hb1[:, i % 2, :], hb1[:, i % 2, :], ACT.Gelu).then_inc(s["h1_ready"], 1)

        @block.scalar
        def _(ac):
            for n, cols in (("w_gate", 0), ("w_up", 256)):
                ac.dma_start(wst[:, cols:cols + 256].rearrange("p (t c) -> p t c", t=2),
                             a["L0_ffn_" + n].rearrange("(t p) c -> p t c", p=P)).then_inc(s["w_raw0"], 16)
            ac.dma_start(wst[:, 512:768], a["L0_ffn_w_down"]).then_inc(s["w_raw0"], 16)
            ac.dma_start(wst[0:E0, 768:768 + P], a["L0_ffn_w_router"]).then_inc(s["w_raw0"], 16)
            for i, n in enumerate(("bq", "bk")):
                ac.dma_start(bqk_row[:, i * P:(i + 1) * P], a["L0_attn_" + n].rearrange("(o n) d -> o (n d)", o=1)).then_inc(s["w_small0"], 16)
            ac.dma_start(bv_b, a["L0_attn_bv"].rearrange("n d -> (n d)").partition_broadcast(P)).then_inc(s["w_small0"], 16)
            ac.dma_start(bc2q_b, a["L0_attn_bc2q"].rearrange("n q -> (n q)").partition_broadcast(P)).then_inc(s["w_small0"], 16)
            ac.sem_inc(s["pv_evac"], 1)
            ac.wait_ge(s["wt_ready"], 1)
            act(guT[:], bank(4))
            act(dnT[:, :, :].rearrange("p t c -> p (t c)"), bank(5)[:, 0:256])
            act(bqk[:], bank(5)[:, 272:274])
            act(rout[:], bank(5)[:, 256:256 + E0]).then_inc(s["wt_done"], 1)
            act_transposed(ac, xT, 0)
            ac.wait_ge(s["w_small0"], 16 * 12)
            act_split(ac, 0, bqk)
            ac.wait_ge(s["top_ready"], 1)
            act(score[:, 0, :], mx8[:, :, 0], ACT.Sigmoid).then_inc(s["score_ready"], 1)
            ac.wait_ge(s["ss_ready"], 4)
            act(inv[:, :, :].rearrange("p r g -> p (r g)"), ss[:, :, :].rearrange("p r g -> p (r g)"), ACT.Sqrt).then_inc(s["inv_ready"], 1)
            for r in range(5):
                if r < 4:
                    ac.wait_ge(s["hat_ready"], r + 1)
                    ac.wait_ge(s["p3_ready"], r + 1)
                    act(qf[r][0:64, :], bank(4 + 2 * (r % 2), 2)[0:64, :]).then_inc(s["hatT_ready"], 1)
                    ac.wait_ge(s["hatT_ready"], r + 1)
                    ac.wait_ge(s["qk_stored"], 16 * NR * 4)
                    act(part[r][0:64, 0, :], qf[r][0:64, :]).then_inc(s["p1_ready"], 1)
                if r >= 1:
                    ac.wait_ge(s["res_ready"], 4 + r)
                    act(part[r - 1][0:64, 1, :], res[r - 1][0:64, :]).then_inc(s["p2_ready"], 1)
            ac.wait_ge(s["flag_ready"], 1)
            flag = ac.value_load(flag_i[0:1, 0:1], min_val=0, max_val=1)
            act_pair(ac, 0, flag)
            with ac.Fori(1, PAIRS0) as p:
                act_pair(ac, p, flag)
            act_head_out(ac, PAIRS0 - 1, 1)
            ac.wait_ge(s["prep_ready"], 1)
            act(w1T, bank(4))
            act(qoT, bank(5))
            act(repcol, bank(6, 2)).then_inc(s["prep_done"], 1)
            ac.wait_ge(s["prep_ready"], 2)
            act(w1m, bank(6)[:, 0:NQ])
            act(bdq, bank(7)[:, 0:P].unsqueeze(1).to_broadcast([P, NT, C])).then_inc(s["prep_done"], 1)
            act_transposed(ac, attnT, 1)
            act_transposed(ac, attnT, 2)
            ac.wait_ge(s["qm_done"], 1)
            act(qt, qm, ACT.Tanh)
            act(qc, qc, ACT.Sin, scale=-2 * math.pi, bias=half_pi[:]).then_inc(s["tc_done"], 1)
            ac.wait_ge(s["qeT_ready"], 1)
            act(qeT, bank(5)[:, 0:P]).then_inc(s["qeT_done"], 1)
            act_layer1(ac)

        v = nc.vector

        def dve_layernorm(dve, dst, src, n, rs=None):
            for t in range(NT):
                last = v.bn_stats(st[:, t, :], src[:, t, :])
            dve_link(last)
            for t in range(NT):
                last = v.bn_aggr(mv[:, t, :], st[:, t, :])
            last.then_inc(s["ln_stats"], 1)
            dve.wait_ge(s["ln_rstd"], (n if rs is None else rs) + 1)
            for t in range(NT):
                last = v.tensor_scalar(dst[:, t, :], src[:, t, :], mv[:, t, 0:1], rstd[:, t:t + 1], ALU.subtract, ALU.mult)
                if t % 4 == 3:
                    last.then_inc(s["ln_done"], 1)

        def dve_split(dve, n, rows, scale, src):
            r = n % 4
            dve.wait_ge(s["p1_ready"], n + 1)
            v.scalar_tensor_tensor(out=res[r][0:rows, :], in0=src[0:rows, :], scalar=scale, in1=part[r][0:rows, 0, :],
                                   op0=ALU.mult, op1=ALU.subtract).then_inc(s["res_ready"], 1)

        def dve_split_end(dve, n, rows):
            r = n % 4
            dve.wait_ge(s["p2_ready"], n + 1)
            v.tensor_tensor(part[r][0:rows, 2, :], res[r][0:rows, :], part[r][0:rows, 1, :], ALU.subtract).then_inc(s["p3_ready"], 1)

        def dve_top(dve, n, E, K):
            l3 = lg[:, 0:NT * E].rearrange("p (t e) -> p t e", e=E)
            for t in range(NT):
                last = v.max(mx8[:, t, :], l3[:, t, :])
            last.then_inc(s["top_ready"], 1)
            dve.wait_ge(s["top_ready"], n + 1)
            for t in range(NT):
                last = v.max_index(ix8[:, t, :], mx8[:, t, :], l3[:, t, :])
            dve_link(last)
            dve_link(v.tensor_copy(ixf[:, :, 0:K], ix8[:, :, 0:K]))
            o3 = oh.rearrange("p (k t e) -> p k t e", k=K, e=E)
            for k in range(K):
                last = v.tensor_tensor(o3[:, k], iota_e[:, 0:E].unsqueeze(1).to_broadcast([P, NT, E]),
                                       ixf[:, :, k:k + 1].to_broadcast([P, NT, E]), ALU.is_equal)
            dve_link(last)
            if K == 1:
                v.tensor_copy(oh_b[:, 0:NT * E], oh).then_inc(s["oh_ready"], 1)
            else:
                v.tensor_tensor(oh_b[:, 0:NT * E], oh[:, 0:NT * E], oh[:, NT * E:2 * NT * E], ALU.add).then_inc(s["oh_ready"], 1)

        def dve_positions(dve, n, E, K, NB, ranks=1):
            t3 = tot[:, 0:NT * E].rearrange("p (e t) -> p e t", t=NT)
            c3 = cum[:, 0:NT * E].rearrange("p (e t) -> p e t", t=NT)
            rk = lg[:, 0:NT * E].rearrange("p (t e) -> p t e", e=E)
            dve.wait_ge(s["rank_ready"], n + 1)
            dve_link(v.tensor_copy(t3, bank(ranks)[:, NT * E:2 * NT * E].rearrange("p (t e) -> p e t", e=E)))
            dve_link(v.tensor_tensor_scan(cum[:, 0:NT * E], scan_keep[:, 0:E, :].rearrange("p e t -> p (e t)"), tot[:, 0:NT * E],
                                          0.0, ALU.mult, ALU.add))
            dve_link(v.tensor_scalar(nbk[:, 0:E], c3[:, :, NT - 1], 1.0 / P, (P - 1) / P - 0.5 + 1 / 256, ALU.mult, ALU.add))
            dve_link(v.tensor_scalar(nbk[:, 0:E], nbk[:, 0:E], ROUND, ROUND, ALU.add, ALU.subtract))
            dve_link(v.tensor_tensor_scan(incl[:, 0:E], ones_e[:, 0:E], nbk[:, 0:E], 0.0, ALU.mult, ALU.add))
            v.tensor_tensor(t3, c3, t3, ALU.subtract)
            dve_link(v.tensor_tensor(basex[:, 0:E], incl[:, 0:E], nbk[:, 0:E], ALU.subtract))
            dve_link(v.tensor_scalar(basex[:, 0:E], basex[:, 0:E], float(P), None, ALU.mult))
            dve_link(v.tensor_tensor(rk, bank(ranks)[:, 0:NT * E].rearrange("p (t e) -> p t e", e=E),
                                     tot[:, 0:NT * E].rearrange("p (e t) -> p t e", t=NT), ALU.add))
            dve_link(v.tensor_tensor(rk, rk, basex[:, 0:E].unsqueeze(1).to_broadcast([P, NT, E]), ALU.add))
            o3 = oh.rearrange("p (k t e) -> p k t e", k=K, e=E)
            for k in range(K):
                dve_link(v.tensor_tensor(c3.rearrange("p e t -> p (e t)").rearrange("p (t e) -> p t e", e=E), rk, o3[:, k], ALU.mult))
                dve_link(v.tensor_reduce(posf[:, k * NT:(k + 1) * NT], cum[:, 0:NT * E].rearrange("p (t e) -> p t e", e=E), axis=AX.X, op=ALU.add))
                v.tensor_copy(pos_i[:, k, :], posf[:, k * NT:(k + 1) * NT])
            cmp_ = sq[0:1, 0:NB * E].rearrange("p (b e) -> p b e", e=E)
            dve_link(v.tensor_tensor(cmp_, incl[0:1, 0:E].unsqueeze(1).to_broadcast([1, NB, E]),
                                     iota_b[0:1, 0:NB].unsqueeze(2).to_broadcast([1, NB, E]), ALU.is_le))
            dve_link(v.tensor_reduce(tot[0:1, 0:NB], cmp_, axis=AX.X, op=ALU.add))
            v.tensor_scalar(eb_i[0:1, 0:NB], tot[0:1, 0:NB], float(E - 1), None, ALU.min).then_inc(s["pos_ready"], 1)
            dve.wait_ge(s["pos_ready"], n + 1)
            dve.sem_inc(s["xsrc_ready"], 1)

        def dve_max(dve, p, n):
            dve.wait_ge(s["f_ready"], p * 32 + n + 1)
            v.reduce_max(M[:, n // 8, n % 8:n % 8 + 1], bank(FB[n % 2], 2), AX.X).then_inc(s["f_free"], 1)

        def dve_mt_copy(dve, p, u):
            dve.wait_ge(s["mt_ready"], p * 2 + u + 1)
            if not (isinstance(p, int) and p == 0):
                dve.wait_ge(s["m_stored"], p * 32 + 16 * u)
            v.tensor_copy(mrow[:, u, :], bank(7 - u).bitcast(BF16)[0:PARTS * KT, 0:P]).then_inc(s["mt_copied"], 1)

        def dve_guard(dve, p, n):
            f = bank(FB[n % 2], 2)
            dve.wait_ge(s["f_ready"], p * 32 + n + 17)
            dve.wait_ge(s["g_ready"], p * 16 + n + 1)
            for half in range(2):
                last = v.tensor_scalar(Zt(n // 8, n % 8)[:, half * 512:(half + 1) * 512], bank(2 + half), 1 / EPS_COS, 1.0, ALU.mult, ALU.min)
            last.then_inc(s["g_step"], 1)
            dve.wait_ge(s["g_step"], p * 16 + n + 1)
            v.tensor_tensor(f, f, Zt(n // 8, n % 8), ALU.mult).then_inc(s["g_done"], 1)

        def dve_curve(dve, p, n):
            dve.wait_ge(s["pv_done"], p * 16 + n + 1)
            dve.wait_ge(s["sin_done"], p * 16 + n + 1)
            v.scalar_tensor_tensor(out=Zt(n // 8, n % 8), in0=snb[:, n % 2, :], scalar=10.0, in1=bank(FB[n % 2], 2),
                                   op0=ALU.add, op1=ALU.mult).then_inc(s["f_free"], 1)

        def dve_phase_a(dve, p, guard, last):
            if guard:
                dve.wait_ge(s["pv_done"], p * 16 + 1)
                dve_guard(dve, p, 0)
            ahead = 1 if guard else AHEAD
            for n in range(ahead - 1):
                dve_curve(dve, p, n)
            for n in range(16):
                u, k = n // 8, n % 8
                if guard and n < 15:
                    dve.wait_ge(s["pv_done"], p * 16 + n + 2)
                    dve_guard(dve, p, n + 1)
                if n + ahead <= 16:
                    dve_curve(dve, p, n + ahead - 1)
                i = (n - 2) // 2
                if n % 2 == 0 and 0 <= i < NBP:
                    dve.wait_ge(s["silu_done"], p * NBP + i + 1)
                    v.tensor_tensor(hb[:, i % 2, :], sg[:], bank(6)[:, F0:2 * F0], ALU.mult).then_inc(s["h_ready"], 1)
                dve.wait_ge(s["c_ready"], p * 16 + n + 1)
                dve.wait_ge(s["f_free"], p * 32 + n + 19)
                v.tensor_tensor(Zt(u, k), Zt(u, k), bank(2, 2), ALU.add).then_inc(s["z_done"], 1)
                if n + ahead >= 16 and not last:
                    dve_max(dve, p + 1, n + ahead - 16)
                if n == 0:
                    dve_mt_copy(dve, p, 1)

            if not last:
                for n in range(ahead, AHEAD):
                    dve_max(dve, p + 1, n)

        def dve_pair(dve, p, flag, last):
            with dve.If(flag > 0):
                dve_phase_a(dve, p, True, last)
            with dve.Else():
                dve_phase_a(dve, p, False, last)
            if not last:
                for n in range(AHEAD, 16):
                    dve_max(dve, p + 1, n)
                    if n == 9:
                        dve_mt_copy(dve, p + 1, 0)

        def dve_post0(dve):
            dve.wait_ge(s["post_loaded"], 16 * 14)
            v.tensor_copy(rep8.rearrange("p (t q) -> p t q", q=NQ), ident[0:8, 0:8].unsqueeze(1).to_broadcast([8, NT, NQ])).then_inc(s["prep_done"], 1)
            for n in range(8):
                b, hf, hg = n // 4, (n // 2) % 2, n % 2
                dve.wait_ge(s["o_ready"], n + 1)
                src = bank(n % 4).rearrange("p (h j c) -> p h j c", h=4, j=4)
                rc = rec[:, 0:16].rearrange("p (h j) -> p h j", h=4)
                dve_link(v.reciprocal(rc, src[:, :, :, D0]))
                dst = attn[:, b * KT:(b + 1) * KT, hg * 64:(hg + 1) * 64].rearrange("p (j f) (h d) -> p f h j d", f=2, h=4)[:, hf]
                for h in range(4):
                    last = v.tensor_tensor(dst[:, h], src[:, h, :, 0:D0], rc[:, h, :].unsqueeze(2).to_broadcast([P, 4, D0]), ALU.mult)
                last.then_inc(s["o_done"], 1)
                dve.wait_ge(s["o_done"], n + 1)
            dve.wait_ge(s["prep_done"], 3)
            v.tensor_tensor(bmm, bm_b, bank(6)[:, 8:8 + NQ], ALU.add)
            v.tensor_tensor(bff, b2_b, bank(7)[:, P:2 * P], ALU.add).then_inc(s["prep_done"], 1)
            dve.wait_ge(s["bo_added"], 1)
            for c in range(4):
                dve.wait_ge(s["wo_ready"], c + 1)
                xc = x1p[:, 4 * c:4 * c + 4, :]
                v.tensor_tensor(xc, xc, bank(c).rearrange("p (t c) -> p t c", c=C), ALU.add).then_inc(s["wo_done"], 1)
            dve.wait_ge(s["wo_done"], 4)
            dve_ln_affine(dve, x1, x1p, 1, g1_b, be1_b)
            dve.wait_ge(s["qm_ready"], 1)
            dve_link(v.tensor_tensor(qm.rearrange("p (t q) -> p t q", q=NQ), bank(4)[:, 0:P].rearrange("p (t q) -> p t q", q=NQ),
                                     bmm.unsqueeze(1).to_broadcast([P, NT, NQ]), ALU.add))
            dve_link(v.tensor_scalar(qt, qm, 0.125, None, ALU.mult))
            dve_link(v.tensor_scalar(qc, qt, ROUND, ROUND, ALU.add, ALU.subtract))
            dve_link(v.tensor_tensor(qc, qt, qc, ALU.subtract))
            dve_link(v.scalar_tensor_tensor(out=qc, in0=qc, scalar=-1.0, in1=qc, op0=ALU.mult, op1=ALU.max))
            v.tensor_scalar(qc, qc, 0.5, None, ALU.min).then_inc(s["qm_done"], 1)
            dve.wait_ge(s["tc_done"], 1)
            v.tensor_tensor(qe, qt, qc, ALU.mult).then_inc(s["qe_ready"], 1)
            dve_link(v.tensor_tensor(x1, x1, bff.unsqueeze(1).to_broadcast([P, NT, C]), ALU.add))
            for c in range(4):
                dve.wait_ge(s["ff_ready"], c + 1)
                xc = x1[:, 4 * c:4 * c + 4, :]
                last = v.tensor_tensor(xc, xc, bank(c).rearrange("p (t c) -> p t c", c=C), ALU.add)
            dve_link(last)
            dve_ln_affine(dve, x1p, x1, 2, g2_b, be2_b)
            dve.wait_ge(s["xsum"], 65)
            v.tensor_tensor(xr, xr, x1p, ALU.add).then_inc(s["res0_ready"], 1)

        def dve_ln_affine(dve, dst, src, n, gain, shift):
            for t in range(NT):
                last = v.bn_stats(st[:, t, :], src[:, t, :])
            dve_link(last)
            for t in range(NT):
                last = v.bn_aggr(mv[:, t, :], st[:, t, :])
            last.then_inc(s["ln_stats"], 1)
            dve.wait_ge(s["ln_rstd"], n + 1)
            for c in range(4):
                for t in range(4 * c, 4 * c + 4):
                    last = v.tensor_scalar(dst[:, t, :], src[:, t, :], mv[:, t, 0:1], rstd[:, t:t + 1], ALU.subtract, ALU.mult)
                dve_link(last)
                d = dst[:, 4 * c:4 * c + 4, :]
                dve_link(v.tensor_tensor(d, d, gain.unsqueeze(1).to_broadcast([P, 4, C]), ALU.mult))
                v.tensor_tensor(d, d, shift.unsqueeze(1).to_broadcast([P, 4, C]), ALU.add).then_inc(s["ln_done"], 1)
            dve.wait_ge(s["ln_done"], 4 * n + 4)

        def dve_layer1(dve):
            dve.wait_ge(s["res0_ready"], 1)
            dve_layernorm(dve, xn[:], xr, 3)
            dve.wait_ge(s["ln_done"], 16)
            dve.wait_ge(s["ln_rstd"], 5)
            for t in range(NT):
                last = v.tensor_scalar(lx[:, t, :], xn[:, t, :], rstd2[:, t:t + 1], None, ALU.mult)
                if t % 4 == 3:
                    last.then_inc(s["ln_done"], 1)
            dve.wait_ge(s["x1_stored"], 16)
            for c in range(4):
                dve.wait_ge(s["v1_ready"], c + 1)
                b, k0 = c // 2, (c % 2) * 4
                dst = Vc[:, :].rearrange("p (u k d) -> p k u d", k=KT, d=D1)[:, k0:k0 + 4, b * H1:(b + 1) * H1, :]
                for k in range(4):
                    last = v.tensor_tensor(dst[:, k], bank(c)[:, k * P:(k + 1) * P].rearrange("p (h d) -> p h d", d=D1),
                                           bv1_b.rearrange("p (h d) -> p h d", d=D1), ALU.add)
                last.then_inc(s["v1_done"], 1)
            for r in range(5):
                if r < 4:
                    dve_split(dve, 8 + r, P, 1.0, qf[r])
                if r >= 1:
                    dve_split_end(dve, 8 + r - 1, P)
            for c in range(12):
                dve_max1(dve, 0, 0, c)
            dve_mt1_copy(dve, 0, 0, False)
            for c in range(12):
                dve_max1(dve, 1, 1, c)
            dve.wait_ge(s["lg1_ready"], 1)
            dve_link(v.tensor_tensor(lg[:, 0:NT * E1].rearrange("p (t e) -> p t e", e=E1),
                                     bank(6)[:, 0:NT * E1].rearrange("p (t e) -> p t e", e=E1),
                                     rb1_b.unsqueeze(1).to_broadcast([P, NT, E1]), ALU.add))
            dve_top(dve, 1, E1, TOP1)
            v.tensor_tensor(score[:, 0, :], mx8[:, :, 1], mx8[:, :, 0], ALU.subtract).then_inc(s["gate_ready"], 1)
            dve_positions(dve, 1, E1, TOP1, NB1, 6)
            dve.wait_ge(s["gates_done"], 1)
            dve_link(v.tensor_scalar(score[:, 0, :], score[:, 1, :], 1.0, None, ALU.add))
            dve_link(v.reciprocal(score[:, 0, :], score[:, 0, :]))
            dve_link(v.tensor_tensor(score[:, 1, :], score[:, 1, :], score[:, 0, :], ALU.mult))
            for w in range(4):
                dve_unit1(dve, 0, w, False)
            with dve.Fori(1, UNITS1 // 4 - 1) as g4:
                for w in range(4):
                    dve_unit1(dve, g4, w, False)
            for w in range(4):
                dve_unit1(dve, UNITS1 // 4 - 1, w, True)
            dve.wait_ge(s["bias1_loaded"], 32)
            known = {}
            dve_step1(dve, 0, 0, known, res=False)
            dve_step1(dve, 0, 1, known, res=False)
            with dve.Fori(0, NB1 // 2 - 3, 2) as h:
                known = {}
                for i in range(4):
                    dve_step1(dve, h, i + 2, known)
            known = {}
            for i in range(4):
                dve_step1(dve, NB1 // 2 - 2, i + 2, known, gu=i < 2)
            for n in range(16):
                b, hf, hg = n // 8, (n // 4) % 2, n % 4
                dve.wait_ge(s["o1t_ready"], n + 1)
                src = bank(n % 4).rearrange("p (h j c) -> p h j c", h=4, j=4)
                rc = rec[:, 0:16].rearrange("p (h j) -> p h j", h=4)
                dve_link(v.reciprocal(rc, src[:, :, :, D1]))
                dst = attn[:, b * KT:(b + 1) * KT, hg * 32:(hg + 1) * 32].rearrange("p (j f) (h d) -> p f h j d", f=2, h=4)[:, hf]
                for h in range(4):
                    last = v.tensor_tensor(dst[:, h], src[:, h, :, 0:D1], rc[:, h, :].unsqueeze(2).to_broadcast([P, 4, D1]), ALU.mult)
                last.then_inc(s["o1n_done"], 1)
                dve.wait_ge(s["o1n_done"], n + 1)
            dve.wait_ge(s["bproj_added"], 1)
            for c in range(4):
                dve.wait_ge(s["proj1_ready"], c + 1)
                xc = xn[:, 4 * c:4 * c + 4, :]
                v.tensor_tensor(xc, xc, bank(c).rearrange("p (t c) -> p t c", c=C), ALU.add).then_inc(s["proj1_done"], 1)
            dve.wait_ge(s["proj1_done"], 4)
            dve_layernorm(dve, lx2, xn[:], 4, 5)
            dve.wait_ge(s["ln_done"], 24)
            dve_link(v.tensor_tensor(xn[:], xn[:], bmlp_b.unsqueeze(1).to_broadcast([P, NT, C]), ALU.add))
            dve.wait_ge(s["x1_loaded"], 16)
            dve_link(v.tensor_tensor(xn[:], xn[:], x1r, ALU.add))
            dve.wait_ge(s["gathered1"], 16 * TOP1 * NT)
            for k in range(TOP1):
                for t in range(NT):
                    last = v.scalar_tensor_tensor(out=xn[:, t, :], in0=yg1[:, k, t, :], scalar=score[:, k, t:t + 1], in1=xn[:, t, :],
                                                  op0=ALU.mult, op1=ALU.add)
                dve_link(last)
            for c in range(4):
                dve.wait_ge(s["mlp_ready"], c + 1)
                xc = xn[:, 4 * c:4 * c + 4, :]
                v.tensor_tensor(xc, xc, bank(c).rearrange("p (t c) -> p t c", c=C), ALU.add).then_inc(s["mlp_done"], 1)

        def dve_step1(dve, h, i, known, gu=True, res=True):
            if gu:
                expert = block_expert1(dve, h, i, known)
                dve.wait_ge(s["gu1_ready"], h * 2 + i + 1)
                v.tensor_tensor(hb1[:, i % 2, :], bank(i % 2), b1_b[:, bass.ds(expert * F1, F1)], ALU.add).then_inc(s["b1_added"], 1)
            if res:
                expert = block_expert1(dve, h, i - 2, known)
                dve.wait_ge(s["o1_ready"], h * 2 + i - 1)
                dve.wait_ge(s[f"y1_stored{i % 2}"], h * 16 + 16 * (i // 2))
                v.tensor_tensor(yb[:, i % 2, :], bank(5 + i % 2)[:, 0:C], b2_b1[:, bass.ds(expert * C, C)], ALU.add).then_inc(s["y1_ready"], 1)

        def dve_max1(dve, unit, u, c):
            u = u % 2
            i, half = MAX_CHUNKS[c]
            width = min(512, (i + 1) * P - 512 * half)
            dve.wait_ge(s["max1_ready"], unit * 12 + c + 1)
            dst = M2[:, u, i - 4:i - 3] if half else M[:, u, i:i + 1]
            v.reduce_max(dst, bank(MB[c % 3])[:, 0:width], AX.X).then_inc(s["max1_free"], 1)
            if c == 11:
                dve.wait_ge(s["max1_free"], unit * 12 + 15)
                v.tensor_tensor(M[:, u, 4:8], M[:, u, 4:8], M2[:, u, :], ALU.max).then_inc(s["max1_whole"], 1)

        def dve_mt1_copy(dve, unit, u, stored=True):
            dve.wait_ge(s["mt1_ready"], unit + 1)
            if stored:
                dve.wait_ge(s["m1_stored"], unit * 16 - 16)
            v.tensor_copy(mrow[:, u % 2, :], bank(MB[MT % 3]).bitcast(BF16)[0:PARTS * KT, 0:P]).then_inc(s["mt1_copied"], 1)

        def dve_unit1(dve, g4, w, last_group):
            unit = g4 * 4 + w
            maxima = not (last_group and w >= 2)
            c = 0
            for k in range(KT):
                for _ in range((k < MAX_STEPS[0]) + (k < MAX_STEPS[1])):
                    if c == MT and not (last_group and w == 3):
                        dve_mt1_copy(dve, unit + 1, w + 1, not (isinstance(unit, int) and unit == 0))
                    if maxima:
                        dve_max1(dve, unit + 2, w, c)
                    c += 1

        @block.vector
        def _(dve):
            dve.sem_inc(s["f_free"], 2)
            dve.sem_inc(s["z_done"], 1)
            dve.sem_inc(s["pv_done"], 16)
            dve.sem_inc(s["m_stored"], 16)
            dve.sem_inc(s["xt_ready"], 2)
            for i in range(2):
                dve.sem_inc(s[f"y_stored{i}"], 16)
                dve.sem_inc(s[f"y1_stored{i}"], 16)
            dve.sem_inc(s["max1_free"], 3)
            dve.sem_inc(s["p1_done"], 2)
            dve.sem_inc(s["pv1_done"], 8)
            dve.sem_inc(s["y1_ready"], 2)
            dve.sem_inc(s["head1_out"], 1)
            dve.wait_ge(s["x_loaded"], 32)
            dve_layernorm(dve, xn[:], x_in, 0)
            dve.wait_ge(s["w_small0"], 16 * 12)
            for c in range(4):
                dve.wait_ge(s["v_ready"], c + 1)
                b, k0 = c // 2, (c % 2) * 4
                dst = Vc[:, :].rearrange("p (u k d) -> p k u d", k=KT, d=D0)[:, k0:k0 + 4, b * H0:(b + 1) * H0, :]
                for k in range(4):
                    last = v.tensor_tensor(dst[:, k], bank(c)[:, k * P:(k + 1) * P].rearrange("p (h d) -> p h d", d=D0),
                                           bv_b.rearrange("p (h d) -> p h d", d=D0), ALU.add)
                last.then_inc(s["v_done"], 1)
            dve.wait_ge(s["lg_ready"], 1)
            dve_link(v.tensor_copy(lg, bank(0)[:, 0:256]))
            dve_top(dve, 0, E0, 1)
            for r in range(5):
                if r < 4:
                    dve_split(dve, r, P, QSCALE0 if r % 2 == 0 else 1.0, qf[r])
                if r >= 1:
                    dve_split_end(dve, r - 1, P)
            dve.wait_ge(s["score_ready"], 1)
            v.tensor_tensor(x_in, xn[:], score[:, 0, :].unsqueeze(2).to_broadcast([P, NT, C]), ALU.mult)
            dve_positions(dve, 0, E0, 1, NB0)
            for r in range(4):
                dve.wait_ge(s["qq_ready"], r + 1)
                dve_link(v.tensor_tensor(qq[r].rearrange("p (k c) -> p k c", c=64), bank(2 + r % 2).rearrange("p (k c) -> p k c", c=64),
                                         bc2q_b.unsqueeze(1).to_broadcast([P, KT, 64]), ALU.add))
                dve_link(v.tensor_tensor(sq, qq[r], qq[r], ALU.mult))
                dve_link(v.tensor_reduce(ss[:, r, :], sq.rearrange("p (g q) -> p g q", q=NQ), axis=AX.X, op=ALU.add))
                v.tensor_scalar(ss[:, r, :], ss[:, r, :], 1e-37, None, ALU.max).then_inc(s["ss_ready"], 1)
            ssf, y = ss[:, :, :].rearrange("p r g -> p (r g)"), inv[:, :, :].rearrange("p r g -> p (r g)")
            dve.wait_ge(s["inv_ready"], 1)
            dve_link(v.reciprocal(y, y))
            dve_link(v.tensor_tensor(sq[:, 0:256], ssf, y, ALU.mult))
            dve_link(v.tensor_tensor(sq[:, 0:256], sq[:, 0:256], y, ALU.mult))
            dve_link(v.tensor_scalar(sq[:, 0:256], sq[:, 0:256], -0.5, 1.5, ALU.mult, ALU.add))
            dve_link(v.tensor_tensor(y, y, sq[:, 0:256], ALU.mult))
            for r in range(4):
                v.tensor_tensor(qq[r].rearrange("p (g q) -> p g q", q=NQ), qq[r].rearrange("p (g q) -> p g q", q=NQ),
                                inv[:, r, :].unsqueeze(2).to_broadcast([P, 64, NQ]), ALU.mult).then_inc(s["qh_ready"], 1)
            for r in range(5):
                if r < 4:
                    dve_split(dve, 4 + r, 64, 1.0, qf[r])
                if r >= 1:
                    dve_split_end(dve, 4 + r - 1, 64)
            v.tensor_tensor(nrm.rearrange("p (r h k) -> p r k h", r=4, h=H0), ss[:, :, :].rearrange("p r (k h) -> p r k h", h=H0),
                            inv[:, :, :].rearrange("p r (k h) -> p r k h", h=H0), ALU.mult)
            dve_link(v.tensor_reduce(small[:, 1:2], ss[:, :, :].rearrange("p r g -> p (r g)"), axis=AX.X, op=ALU.min))
            v.tensor_scalar(small[:, 0:1], small[:, 1:2], EPS_COS * 1.01, None, ALU.is_lt).then_inc(s["nrm_ready"], 1)
            dve.wait_ge(s["nt_ready"], 1)
            v.tensor_copy(nT, bank(2)[0:64, :])
            v.tensor_scalar(flag_i[:], bank(3)[0:1, 0:1], 1.0, None, ALU.min).then_inc(s["flag_ready"], 1)
            for n in range(16):
                dve_max(dve, 0, n)
            dve_mt_copy(dve, 0, 0)
            dve.wait_ge(s["flag_ready"], 1)
            flag = dve.value_load(flag_i[0:1, 0:1], min_val=0, max_val=1)
            with dve.Fori(0, PAIRS0 - 1) as p:
                dve_pair(dve, p, flag, False)
            dve_pair(dve, PAIRS0 - 1, flag, True)
            dve_post0(dve)
            dve_layer1(dve)


_OUT = ((B, S, C), "float32")


def kernel(**inputs):
    import concourse.bacc as bacc
    from concourse.bass_utils import run_bass_kernel_spmd

    nc = bacc.Bacc("TRN2", target_bir_lowering=False, num_devices=1)
    arrays, args = {}, {}
    for name, value in inputs.items():
        arr = np.ascontiguousarray(value)
        arrays["in_" + name] = arr
        args[name] = nc.dram_tensor("in_" + name, arr.shape, mybir.dt.from_np(arr.dtype), kind="ExternalInput").ap()
    out = nc.dram_tensor("out_x", _OUT[0], mybir.dt.from_np(np.dtype(_OUT[1])), kind="ExternalOutput").ap()
    build(nc, args, out)
    result = run_bass_kernel_spmd(nc, [arrays], core_ids=[0])
    return result.results[0]["out_x"]
```
